# Optimizing a Trainium2 kernel written in Bass

```python
import numpy as np
import jax
import jax.numpy as jnp

def _softmax(x, axis=-1):
    return jax.nn.softmax(x, axis=axis)

def _gelu(x):
    return jax.nn.gelu(x, approximate=True)

def _silu(x):
    return jax.nn.silu(x)

def _sigmoid(x):
    return jax.nn.sigmoid(x)

def _layernorm(x, axis=-1, eps=1e-05):
    m = jnp.mean(x, axis=axis, keepdims=True)
    v = jnp.var(x, axis=axis, keepdims=True)
    return (x - m) / jnp.sqrt(v + eps)

def _scatter_add(tgt, idx, src, axis=0):
    return tgt.at[idx].add(src)

def _segment_sum(src, seg, n):
    return jax.ops.segment_sum(src, seg, n)
kernel_name = 'mk_prb_d2_jaxref_r8_feacfd'

def setup_inputs(seed: int=0):
    np.random.seed(seed)
    _w = jnp.asarray

    def _L0_attn_setup():
        import jax, jax.numpy as jnp
        import numpy as np
        H, DK, DV, CHUNK = (4, 32, 32, 32)

        def _silu(x):
            return x * jax.nn.sigmoid(x)

        def _l2norm(x, eps=1e-06):
            return x * jax.lax.rsqrt(jnp.sum(x * x, -1, keepdims=True) + eps)

        def _rmsnorm(x, w, eps=1e-05):
            return x * jax.lax.rsqrt(jnp.mean(x * x, -1, keepdims=True) + eps) * w

        def _causal_dwconv(x, w):
            C = x.shape[-1]
            K = w.shape[-1]
            xp = jnp.pad(x, ((0, 0), (K - 1, 0), (0, 0))).transpose(0, 2, 1)
            y = jax.lax.conv_general_dilated(xp, w[:, None, :], (1,), 'VALID', feature_group_count=C, dimension_numbers=('NCH', 'OIH', 'NCH'))
            return y.transpose(0, 2, 1)

        def _fir(x, filt):
            B, L, h, d = x.shape
            y = _causal_dwconv(x.reshape(B, L, h * d), filt.reshape(h * d, -1))
            return y.reshape(B, L, h, d)

        def _delta_rule_chunkwise(q, k, v, beta):
            b, h, L, dk = q.shape
            dv = v.shape[-1]
            n = L // CHUNK
            q = _l2norm(q)
            k = _l2norm(k)
            v = v * beta[..., None]
            k_beta = k * beta[..., None]
            rs = lambda t: t.reshape(b, h, n, CHUNK, -1)
            q, k, v, k_beta = (rs(q), rs(k), rs(v), rs(k_beta))
            eye = jnp.eye(CHUNK, dtype=q.dtype)
            strict_lower = jnp.tril(jnp.ones((CHUNK, CHUNK), bool), -1)
            A = jnp.where(strict_lower, jnp.einsum('bhncd,bhnsd->bhncs', k_beta, k), 0.0)
            attn_inv = jax.scipy.linalg.solve_triangular(eye + A, jnp.broadcast_to(eye, A.shape), lower=True)
            u = attn_inv @ v
            w = attn_inv @ k_beta
            incl_lower = jnp.tril(jnp.ones((CHUNK, CHUNK), bool))

            def step(S, inp):
                q_i, k_i, u_i, w_i = inp
                attn_local = jnp.where(incl_lower, q_i @ jnp.swapaxes(k_i, -1, -2), 0.0)
                u_t = u_i - w_i @ S
                o_i = q_i @ S + attn_local @ u_t
                return (S + jnp.swapaxes(k_i, -1, -2) @ u_t, o_i)
            S0 = jnp.zeros((b, h, dk, dv), q.dtype)
            xs = tuple((jnp.moveaxis(t, 2, 0) for t in (q, k, u, w)))
            S, out = jax.lax.scan(step, S0, xs)
            return (jnp.moveaxis(out, 0, 2).reshape(b, h, L, dv), S)

        def _stats(x):
            return jnp.stack([x.mean(-1), x.var(-1), jnp.abs(x).mean(-1), jnp.sqrt(jnp.sum(x * x, -1))], -1)

        def _forward(x, Wq, Wk, Wv, Wb, conv_q, conv_k, conv_v, fir_long, fir_short, W1, b1, W2, b2, log_temp, base_bias, conv_residual_logit, rms_w, Wo):
            B, L, D = x.shape
            q = _silu(_causal_dwconv(x @ Wq, conv_q)).reshape(B, L, H, DK)
            k = _silu(_causal_dwconv(x @ Wk, conv_k)).reshape(B, L, H, DK)
            v = _silu(_causal_dwconv(x @ Wv, conv_v)).reshape(B, L, H, DV)
            beta = jax.nn.sigmoid(x @ Wb)
            delta, _S = _delta_rule_chunkwise(q.transpose(0, 2, 1, 3), k.transpose(0, 2, 1, 3), v.transpose(0, 2, 1, 3), beta.transpose(0, 2, 1))
            delta = delta.transpose(0, 2, 1, 3)
            f_short = _fir(v, fir_short)
            f_long = _fir(v, fir_long)
            stats = jnp.concatenate([_stats(f_short), _stats(f_long), _stats(delta), _stats(v)], -1)
            hidden_exp = jnp.broadcast_to(x[:, :, None, :], (B, L, H, D))
            gate_in = jnp.concatenate([hidden_exp, stats], -1)
            h1 = jax.nn.gelu(gate_in @ W1 + b1, approximate=False)
            logits = h1 @ W2 + b2 + base_bias
            temp = jax.nn.softplus(log_temp) + 0.0001
            p = jax.nn.softmax(logits / temp[:, None], -1)
            eps = 0.05
            p = jnp.maximum(p, jnp.array([eps, eps, 0.0, 0.0], p.dtype))
            p = p / jnp.sum(p, -1, keepdims=True)
            o = p[..., 0:1] * f_short + p[..., 1:2] * f_long + p[..., 2:3] * delta + p[..., 3:4] * v
            o = o + 0.5 * jax.nn.sigmoid(conv_residual_logit)[None, None, :, None] * f_short
            o = _rmsnorm(o, rms_w)
            return o.reshape(B, L, H * DV) @ Wo
        key = jax.random.key(seed)
        ks = jax.random.split(key, 13)
        B, L, D = (2, 256, 128)
        f = jnp.float32
        n = lambda k, shape, s=0.02: jax.random.normal(k, shape, f) * s
        return {'x': jax.random.normal(ks[0], (B, L, D), f), 'Wq': n(ks[1], (D, D)), 'Wk': n(ks[2], (D, D)), 'Wv': n(ks[3], (D, D)), 'Wb': n(ks[4], (D, H)), 'conv_q': n(ks[5], (D, 4), 0.1), 'conv_k': n(ks[6], (D, 4), 0.1), 'conv_v': n(ks[7], (D, 4), 0.1), 'fir_long': n(ks[8], (H, DV, 64)), 'fir_short': n(ks[9], (H, DV, 5)), 'W1': n(ks[10], (D + 16, D)), 'b1': jnp.zeros((D,), f), 'W2': n(ks[11], (D, 4)), 'b2': jnp.zeros((4,), f), 'log_temp': jnp.full((H,), float(np.log(np.expm1(0.7))), f), 'base_bias': jnp.tile(jnp.array([-0.5, -0.5, 1.0, 3.0], f), (H, 1)), 'conv_residual_logit': jnp.full((H,), -2.0, f), 'rms_w': jnp.ones((DV,), f), 'Wo': n(ks[12], (D, D))}
    _L0_attn_in = _L0_attn_setup()

    def _L0_ffn_setup():
        import jax, jax.numpy as jnp
        import numpy as np
        from jax import lax
        B, N, D, H, E, K = (16, 128, 128, 512, 8, 2)
        key = jax.random.key(seed)
        ks = jax.random.split(key, 12)
        s = 0.02
        return {'x': jax.random.normal(ks[0], (B, N, D), jnp.float32), 'alpha': jnp.asarray(0.9, jnp.float32), 'w_gate': jax.random.normal(ks[1], (D, E), jnp.float32) * s, 'b_gate': jnp.zeros((E,), jnp.float32), 'W1m': jax.random.normal(ks[2], (D, H), jnp.float32) * s, 'b1m': jnp.zeros((H,), jnp.float32), 'W2m': jax.random.normal(ks[3], (H, D), jnp.float32) * s, 'b2m': jnp.zeros((D,), jnp.float32), 'W1e': jax.random.normal(ks[4], (E, D, H), jnp.float32) * s, 'b1e': jnp.zeros((E, H), jnp.float32), 'W2e': jax.random.normal(ks[5], (E, H, D), jnp.float32) * s, 'b2e': jnp.zeros((E, D), jnp.float32)}
    _L0_ffn_in = _L0_ffn_setup()

    def _L1_attn_setup():
        import jax, jax.numpy as jnp
        import numpy as np
        import math
        B, S, D, H = (4, 256, 128, 16)
        DK = D // H
        key = jax.random.key(seed)
        ks = jax.random.split(key, 5)
        scale = 1.0 / math.sqrt(D)
        return {'x': jax.random.normal(ks[0], (B, S, D), dtype=jnp.float32), 'Wv': jax.random.normal(ks[1], (D, D), dtype=jnp.float32) * scale, 'bv': jax.random.normal(ks[2], (D,), dtype=jnp.float32) * scale, 'Wo': jax.random.normal(ks[3], (D, D), dtype=jnp.float32) * scale, 'bo': jax.random.normal(ks[4], (D,), dtype=jnp.float32) * scale}
    _L1_attn_in = _L1_attn_setup()

    def _L1_ffn_setup():
        import jax, jax.numpy as jnp
        import numpy as np
        EPS = 1e-05

        @jax.custom_vjp
        def ste_quantize(w):
            scale = jnp.maximum(jnp.mean(jnp.abs(w)), EPS)
            return jnp.clip(jnp.round(w / scale), -1.0, 1.0)

        def _ste_fwd(w):
            return (ste_quantize(w), None)

        def _ste_bwd(_, g):
            return (g,)
        ste_quantize.defvjp(_ste_fwd, _ste_bwd)
        key = jax.random.key(seed)
        k1, k2 = jax.random.split(key)
        x = jax.random.normal(k1, (8, 1024, 128), dtype=jnp.float32)
        weight = jax.random.normal(k2, (128, 128), dtype=jnp.float32) * 0.02
        return {'x': x, 'weight': weight}
    _L1_ffn_in = _L1_ffn_setup()
    _d = {'L0_attn_x': _L0_attn_in['x'], 'L0_attn_Wq': _L0_attn_in['Wq'], 'L0_attn_Wk': _L0_attn_in['Wk'], 'L0_attn_Wv': _L0_attn_in['Wv'], 'L0_attn_Wb': _L0_attn_in['Wb'], 'L0_attn_conv_q': _L0_attn_in['conv_q'], 'L0_attn_conv_k': _L0_attn_in['conv_k'], 'L0_attn_conv_v': _L0_attn_in['conv_v'], 'L0_attn_fir_long': _L0_attn_in['fir_long'], 'L0_attn_fir_short': _L0_attn_in['fir_short'], 'L0_attn_W1': _L0_attn_in['W1'], 'L0_attn_b1': _L0_attn_in['b1'], 'L0_attn_W2': _L0_attn_in['W2'], 'L0_attn_b2': _L0_attn_in['b2'], 'L0_attn_log_temp': _L0_attn_in['log_temp'], 'L0_attn_base_bias': _L0_attn_in['base_bias'], 'L0_attn_conv_residual_logit': _L0_attn_in['conv_residual_logit'], 'L0_attn_rms_w': _L0_attn_in['rms_w'], 'L0_attn_Wo': _L0_attn_in['Wo'], 'L0_ffn_alpha': _L0_ffn_in['alpha'], 'L0_ffn_w_gate': _L0_ffn_in['w_gate'], 'L0_ffn_b_gate': _L0_ffn_in['b_gate'], 'L0_ffn_W1m': _L0_ffn_in['W1m'], 'L0_ffn_b1m': _L0_ffn_in['b1m'], 'L0_ffn_W2m': _L0_ffn_in['W2m'], 'L0_ffn_b2m': _L0_ffn_in['b2m'], 'L0_ffn_W1e': _L0_ffn_in['W1e'], 'L0_ffn_b1e': _L0_ffn_in['b1e'], 'L0_ffn_W2e': _L0_ffn_in['W2e'], 'L0_ffn_b2e': _L0_ffn_in['b2e'], 'L1_attn_Wv': _L1_attn_in['Wv'], 'L1_attn_bv': _L1_attn_in['bv'], 'L1_attn_Wo': _L1_attn_in['Wo'], 'L1_attn_bo': _L1_attn_in['bo'], 'L1_ffn_weight': _L1_ffn_in['weight']}
    _x0 = _d['L0_attn_x']
    _d['L0_attn_x'] = jax.random.normal(jax.random.fold_in(jax.random.key(seed), 1), (8, 256, 128), dtype=_x0.dtype)
    del _x0
    return _d

def reference(L0_attn_x, L0_attn_Wq, L0_attn_Wk, L0_attn_Wv, L0_attn_Wb, L0_attn_conv_q, L0_attn_conv_k, L0_attn_conv_v, L0_attn_fir_long, L0_attn_fir_short, L0_attn_W1, L0_attn_b1, L0_attn_W2, L0_attn_b2, L0_attn_log_temp, L0_attn_base_bias, L0_attn_conv_residual_logit, L0_attn_rms_w, L0_attn_Wo, L0_ffn_alpha, L0_ffn_w_gate, L0_ffn_b_gate, L0_ffn_W1m, L0_ffn_b1m, L0_ffn_W2m, L0_ffn_b2m, L0_ffn_W1e, L0_ffn_b1e, L0_ffn_W2e, L0_ffn_b2e, L1_attn_Wv, L1_attn_bv, L1_attn_Wo, L1_attn_bo, L1_ffn_weight):

    def _L0_attn_ref(x, Wq, Wk, Wv, Wb, conv_q, conv_k, conv_v, fir_long, fir_short, W1, b1, W2, b2, log_temp, base_bias, conv_residual_logit, rms_w, Wo):
        import jax, jax.numpy as jnp
        import numpy as np
        H, DK, DV, CHUNK = (4, 32, 32, 32)

        def _silu(x):
            return x * jax.nn.sigmoid(x)

        def _l2norm(x, eps=1e-06):
            return x * jax.lax.rsqrt(jnp.sum(x * x, -1, keepdims=True) + eps)

        def _rmsnorm(x, w, eps=1e-05):
            return x * jax.lax.rsqrt(jnp.mean(x * x, -1, keepdims=True) + eps) * w

        def _causal_dwconv(x, w):
            C = x.shape[-1]
            K = w.shape[-1]
            xp = jnp.pad(x, ((0, 0), (K - 1, 0), (0, 0))).transpose(0, 2, 1)
            y = jax.lax.conv_general_dilated(xp, w[:, None, :], (1,), 'VALID', feature_group_count=C, dimension_numbers=('NCH', 'OIH', 'NCH'))
            return y.transpose(0, 2, 1)

        def _fir(x, filt):
            B, L, h, d = x.shape
            y = _causal_dwconv(x.reshape(B, L, h * d), filt.reshape(h * d, -1))
            return y.reshape(B, L, h, d)

        def _delta_rule_chunkwise(q, k, v, beta):
            b, h, L, dk = q.shape
            dv = v.shape[-1]
            n = L // CHUNK
            q = _l2norm(q)
            k = _l2norm(k)
            v = v * beta[..., None]
            k_beta = k * beta[..., None]
            rs = lambda t: t.reshape(b, h, n, CHUNK, -1)
            q, k, v, k_beta = (rs(q), rs(k), rs(v), rs(k_beta))
            eye = jnp.eye(CHUNK, dtype=q.dtype)
            strict_lower = jnp.tril(jnp.ones((CHUNK, CHUNK), bool), -1)
            A = jnp.where(strict_lower, jnp.einsum('bhncd,bhnsd->bhncs', k_beta, k), 0.0)
            attn_inv = jax.scipy.linalg.solve_triangular(eye + A, jnp.broadcast_to(eye, A.shape), lower=True)
            u = attn_inv @ v
            w = attn_inv @ k_beta
            incl_lower = jnp.tril(jnp.ones((CHUNK, CHUNK), bool))

            def step(S, inp):
                q_i, k_i, u_i, w_i = inp
                attn_local = jnp.where(incl_lower, q_i @ jnp.swapaxes(k_i, -1, -2), 0.0)
                u_t = u_i - w_i @ S
                o_i = q_i @ S + attn_local @ u_t
                return (S + jnp.swapaxes(k_i, -1, -2) @ u_t, o_i)
            S0 = jnp.zeros((b, h, dk, dv), q.dtype)
            xs = tuple((jnp.moveaxis(t, 2, 0) for t in (q, k, u, w)))
            S, out = jax.lax.scan(step, S0, xs)
            return (jnp.moveaxis(out, 0, 2).reshape(b, h, L, dv), S)

        def _stats(x):
            return jnp.stack([x.mean(-1), x.var(-1), jnp.abs(x).mean(-1), jnp.sqrt(jnp.sum(x * x, -1))], -1)

        def _forward(x, Wq, Wk, Wv, Wb, conv_q, conv_k, conv_v, fir_long, fir_short, W1, b1, W2, b2, log_temp, base_bias, conv_residual_logit, rms_w, Wo):
            B, L, D = x.shape
            q = _silu(_causal_dwconv(x @ Wq, conv_q)).reshape(B, L, H, DK)
            k = _silu(_causal_dwconv(x @ Wk, conv_k)).reshape(B, L, H, DK)
            v = _silu(_causal_dwconv(x @ Wv, conv_v)).reshape(B, L, H, DV)
            beta = jax.nn.sigmoid(x @ Wb)
            delta, _S = _delta_rule_chunkwise(q.transpose(0, 2, 1, 3), k.transpose(0, 2, 1, 3), v.transpose(0, 2, 1, 3), beta.transpose(0, 2, 1))
            delta = delta.transpose(0, 2, 1, 3)
            f_short = _fir(v, fir_short)
            f_long = _fir(v, fir_long)
            stats = jnp.concatenate([_stats(f_short), _stats(f_long), _stats(delta), _stats(v)], -1)
            hidden_exp = jnp.broadcast_to(x[:, :, None, :], (B, L, H, D))
            gate_in = jnp.concatenate([hidden_exp, stats], -1)
            h1 = jax.nn.gelu(gate_in @ W1 + b1, approximate=False)
            logits = h1 @ W2 + b2 + base_bias
            temp = jax.nn.softplus(log_temp) + 0.0001
            p = jax.nn.softmax(logits / temp[:, None], -1)
            eps = 0.05
            p = jnp.maximum(p, jnp.array([eps, eps, 0.0, 0.0], p.dtype))
            p = p / jnp.sum(p, -1, keepdims=True)
            o = p[..., 0:1] * f_short + p[..., 1:2] * f_long + p[..., 2:3] * delta + p[..., 3:4] * v
            o = o + 0.5 * jax.nn.sigmoid(conv_residual_logit)[None, None, :, None] * f_short
            o = _rmsnorm(o, rms_w)
            return o.reshape(B, L, H * DV) @ Wo
        return _forward(x, Wq, Wk, Wv, Wb, conv_q, conv_k, conv_v, fir_long, fir_short, W1, b1, W2, b2, log_temp, base_bias, conv_residual_logit, rms_w, Wo)

    def _L0_ffn_ref(x, alpha, w_gate, b_gate, W1m, b1m, W2m, b2m, W1e, b1e, W2e, b2e):
        import jax, jax.numpy as jnp
        import numpy as np
        from jax import lax
        B, N, D, H, E, K = (16, 128, 128, 512, 8, 2)
        main = jax.nn.gelu(x @ W1m + b1m) @ W2m + b2m
        logits = jnp.mean(x, axis=1) @ w_gate + b_gate
        probs = jax.nn.softmax(logits, axis=-1)
        top_vals, top_idx = lax.top_k(probs, K)
        gate_w = top_vals / jnp.sum(top_vals, axis=-1, keepdims=True)
        W1g = W1e[top_idx]
        b1g = b1e[top_idx]
        W2g = W2e[top_idx]
        b2g = b2e[top_idx]
        h = jax.nn.gelu(jnp.einsum('bnd,bkdh->bknh', x, W1g) + b1g[:, :, None, :])
        eo = jnp.einsum('bknh,bkhd->bknd', h, W2g) + b2g[:, :, None, :]
        expert_out = jnp.einsum('bk,bknd->bnd', gate_w, eo)
        a = jnp.clip(alpha, 0.1, 1.0)
        return a * main + (1.0 - a) * expert_out

    def _L1_attn_ref(x, Wv, bv, Wo, bo):
        import jax, jax.numpy as jnp
        import numpy as np
        import math
        B, S, D, H = (4, 256, 128, 16)
        DK = D // H
        b, s, d = x.shape
        h, dk = (H, DK)
        p = jnp.einsum('bsd,ed->bse', x, Wv) + bv
        p = p.reshape(b, s, h, dk).transpose(0, 2, 1, 3)
        q = k = v = p
        scores = jnp.einsum('bhqd,bhkd->bhqk', q, k) / math.sqrt(dk)
        attn = jax.nn.softmax(scores, axis=-1)
        out = jnp.einsum('bhqk,bhkd->bhqd', attn, v)
        out = out.reshape(b, s, h * dk)
        return jnp.einsum('bsd,ed->bse', out, Wo) + bo

    def _L1_ffn_ref(x, weight):
        import jax, jax.numpy as jnp
        import numpy as np
        EPS = 1e-05

        @jax.custom_vjp
        def ste_quantize(w):
            scale = jnp.maximum(jnp.mean(jnp.abs(w)), EPS)
            return jnp.clip(jnp.round(w / scale), -1.0, 1.0)

        def _ste_fwd(w):
            return (ste_quantize(w), None)

        def _ste_bwd(_, g):
            return (g,)
        ste_quantize.defvjp(_ste_fwd, _ste_bwd)
        w_ternary = ste_quantize(weight)
        scale = jnp.maximum(jnp.mean(jnp.abs(weight)), EPS)
        return jnp.einsum('bsi,oi->bso', x, w_ternary * scale)
    x = L0_attn_x
    xn = _layernorm(x, axis=-1)
    x = x + _L0_attn_ref(xn, L0_attn_Wq, L0_attn_Wk, L0_attn_Wv, L0_attn_Wb, L0_attn_conv_q, L0_attn_conv_k, L0_attn_conv_v, L0_attn_fir_long, L0_attn_fir_short, L0_attn_W1, L0_attn_b1, L0_attn_W2, L0_attn_b2, L0_attn_log_temp, L0_attn_base_bias, L0_attn_conv_residual_logit, L0_attn_rms_w, L0_attn_Wo) + _L0_ffn_ref(xn, L0_ffn_alpha, L0_ffn_w_gate, L0_ffn_b_gate, L0_ffn_W1m, L0_ffn_b1m, L0_ffn_W2m, L0_ffn_b2m, L0_ffn_W1e, L0_ffn_b1e, L0_ffn_W2e, L0_ffn_b2e)
    xn = _layernorm(x, axis=-1)
    x = x + _L1_attn_ref(xn, L1_attn_Wv, L1_attn_bv, L1_attn_Wo, L1_attn_bo) + _L1_ffn_ref(xn, L1_ffn_weight)
    return x

_drawn_inputs = setup_inputs


def setup_inputs(seed=0):
    import zlib

    import numpy as np

    out = dict(_drawn_inputs(seed))
    spreads = {'L0_attn_b1': (0.0, 0.8),
     'L0_attn_b2': (0.0, 0.8),
     'L0_attn_log_temp': (0.013658997602760792, 0.6),
     'L0_attn_conv_residual_logit': (-2.0, 0.6),
     'L0_attn_rms_w': (1.0, 0.2),
     'L0_ffn_b_gate': (0.0, 0.617),
     'L0_ffn_b1m': (0.0, 0.285),
     'L0_ffn_b2m': (0.0, 0.1),
     'L0_ffn_b1e': (0.0, 0.8),
     'L0_ffn_b2e': (0.0, 0.765)}
    factors = {'L0_attn_Wq': 8.0,
     'L0_attn_Wk': 8.0,
     'L0_attn_Wb': 8.0,
     'L0_attn_conv_q': 8.0,
     'L0_attn_conv_k': 8.0,
     'L0_attn_fir_long': 8.0,
     'L0_attn_fir_short': 8.0,
     'L0_attn_W1': 8.0,
     'L0_attn_W2': 8.0,
     'L0_ffn_w_gate': 8.0,
     'L0_ffn_W1e': 8.0,
     'L0_ffn_W2e': 8.0}
    for name, (base, spread) in spreads.items():
        noise = np.random.default_rng([zlib.crc32(name.encode()), seed]).standard_normal(out[name].shape)
        drawn = base * np.exp(spread * noise) if base else spread * noise
        out[name] = jnp.asarray(drawn.astype(out[name].dtype))
    for name, factor in factors.items():
        out[name] = (out[name] * factor).astype(out[name].dtype)
    return out
```

```python
import concourse.bass as bass
from concourse import mybir
from contextlib import ExitStack

import numpy as np

F32 = mybir.dt.float32
BF16 = mybir.dt.bfloat16
U32 = mybir.dt.uint32
ALU = mybir.AluOpType
ACT = mybir.ActivationFunctionType
AX = mybir.AxisListType

P = 128
NB, L, D = 8, 256, 128
T = NB * L
NT = T // P
H, DH = 4, 32
C = 32
NCH = L // C
Q4 = 4
BH = NB // Q4
NG = NCH * BH
TAPS, FS_TAPS, FL_TAPS = 4, 5, 64
W64 = 64
NW = T // W64
EPS = 1e-5
HID = 512
NBLK = HID // P
NE, TOPK = 8, 2
PACK = HID + NBLK + HID
HS, DS = 16, 8
NJ = 4
SLOT = 64
NGRP = 6
ROWS = NGRP * DS
MROWS = 3
ROUND = 1.5 * 2.0 ** 23


def attention_mix_kernel(nc, inp, out):
    ctx = ExitStack()
    with ctx:
        def sb(name, shape, dt=F32):
            return ctx.enter_context(nc.sbuf_tensor(name, shape, dt))

        def sem(name):
            return ctx.enter_context(nc.semaphore(name))

        ps = ctx.enter_context(nc.psum_tensor("ps", [P, 8, 512], F32))
        PA, PB = ps[:, 0:4, :], ps[:, 4:8, :]

        def flat(ap):
            return ap.rearrange("p a b -> p (a b)")

        def bc(ap, axis, n):
            u = ap.unsqueeze(axis)
            shape = list(u.shape)
            shape[axis] = n
            return u.broadcast_to(shape)

        ARENA = 35328
        arena = sb("arena", [P, ARENA])
        used = [0]

        def carve(shape, dt=F32, start=None):
            if start is not None:
                used[0] = start
            words = int(np.prod(shape)) // (2 if dt == BF16 else 1)
            flat_view = arena[:, used[0]:used[0] + words]
            used[0] += words
            assert used[0] <= ARENA
            if dt == BF16:
                flat_view = flat_view.bitcast(BF16)
            names = "abcdef"[:len(shape)]
            return flat_view.rearrange("p (%s) -> p %s" % (" ".join(names), " ".join(names)), **dict(zip(names, shape)))

        ident = sb("ident", [P, P])
        ones = sb("ones", [P, P])
        tri = sb("tri", [P, C])
        X = sb("X", [P, NT, D])
        xn = X
        sq = carve([NT, D])
        xnT = sb("xnT", [P, NB, L])
        y0 = carve([NB, L])
        y1 = sb("y1", [P, NB, L])
        kT = carve([NCH, NB, C])
        qT = carve([NCH, NB, C])
        vT = carve([NCH, NB, C])
        vTp = carve([NB, W64 + L])
        wqkv = sb("wqkv", [P, 3, D])
        wb = sb("wb", [P, H])
        cw = sb("cw", [P, 3, TAPS])
        fsw = sb("fsw", [P, FS_TAPS])
        small = sb("small", [P, 8, NT * H])
        betaT = y1[0:H].rearrange("p b (n c) -> p (b n c)", c=C).rearrange("p (n b c) -> p n b c", n=NCH, c=C)
        beta_sl = sb("beta_sl", [P, H, NG])
        beta_p = sb("beta_p", [P, W64])
        k_sl = sb("k_sl", [P, NG, D])
        v_sl = carve([NG, D])
        kb_sl = X
        vb_sl = y0[:].rearrange("p b l -> p (b l)").rearrange("p (g d) -> p g d", d=D)
        A64 = carve([2, H, NG, C])
        Ap = carve([C, 2, C])
        G = carve([C, 2, C])
        AT = carve([H, NG, C])
        Sbd = carve([2, NB, P])
        knT = kT
        GT = A64[:, 0].rearrange("p h g c -> p (h g c)").rearrange("p (c x) -> p c x", c=C)
        WT = A64[:, 1].rearrange("p h g c -> p (h g c)").rearrange("p (n b c) -> p n b c", n=NCH, c=C)
        vwin = A64[:].rearrange("p a h g c -> p (a h g c)").rearrange("p (w x) -> p w x", w=NW)
        flw = vT[:].rearrange("p n b c -> p (n b c)").rearrange("p (d o) -> p d o", o=W64)
        U = vT[:].rearrange("p n b c -> p (n b c)").rearrange("p (g d) -> p g d", d=D)
        delta_sl = U
        Tf = carve([2, H, 8, W64])
        fl64 = Tf[0:W64].rearrange("p a h d o -> p (a h d o)").rearrange("p (w x) -> p w x", w=NW)
        fs_sl = carve([NG, D])
        fl_sl = carve([NG, D])
        fsT = y1
        fsC = sq[:].rearrange("p g d -> p (g d)").rearrange("p (n b c) -> p n b c", n=NCH, c=C)
        stats = G[:].rearrange("p c q t -> p (c q t)").rearrange("p (x k) -> p x k", k=32)
        statsT = Ap[:].rearrange("p s q c -> p (s q c)")
        h1 = Tf[:].rearrange("p a h d o -> p (a h d o)").rearrange("p (s x) -> p s x", x=1024)
        logT = kT[:].rearrange("p n b c -> p (n b c)")
        osl = y0[:].rearrange("p b l -> p (b l)").rearrange("p (g d) -> p g d", d=D)
        oT = X[:].rearrange("p g d -> p (g d)").rearrange("p (b l) -> p b l", b=NB)
        x1 = k_sl
        xres = y1[:].rearrange("p b l -> p (b l)").rearrange("p (g d) -> p g d", d=D)
        w1x = sb("w1x", [P, D])
        w1s = sb("w1s", [P, D])
        b1 = sb("b1", [P, 1])
        w2p = sb("w2p", [P, 32])
        bcst = sb("bcst", [P, 64])
        rmsw = sb("rmsw", [P, 1])
        wo = sb("wo", [P, D])
        lg = sb("lg", [P, NG * H, 4])
        gp = sb("gp", [P, 4, NG * H])
        wm = sb("wm", [P, PACK])
        we = sb("we", [P, 2, PACK])
        hT = sb("hT", [P, 3, NBLK, L])
        tmp = hT[:, 0].rearrange("p k l -> p (k l)")
        gw = sb("gw", [NB, 64])
        idx = sb("idx", [NB, 8], U32)
        gwd = sb("gwd", [NB, NB, TOPK])
        gall = sb("gall", [P, NB * TOPK])
        wg = sb("wg", [P, NE])
        bgate = sb("bgate", [NB, NE])
        iota8 = sb("iota8", [NB, NE])
        b2e = sb("b2e", [NE, D])
        b2m = sb("b2m", [1, D])
        biasb = sb("biasb", [NB, D])
        alph = sb("alph", [P, 4])

        x_in = sem("x_in")
        w_in = sem("w_in")
        consts = sem("consts")
        xsq = sem("xsq")
        xc_done = sem("xc_done")
        lnvar = sem("lnvar")
        lnstd = sem("lnstd")
        xn_done = sem("xn_done")
        xT_ps = sem("xT_ps")
        xnT_done = sem("xnT_done")
        proj_ps = sem("proj_ps")
        tap_done = sem("tap_done")
        conv_done = sem("conv_done")
        silu_done = sem("silu_done")
        sl_ps = sem("sl_ps")
        slsq = sem("slsq")
        ssq = sem("ssq")
        norm = sem("norm")
        sl_done = sem("sl_done")
        beta_fm = sem("beta_fm")
        beta_done = sem("beta_done")
        bp_ps = sem("bp_ps")
        vs_done = sem("vs_done")
        kb_done = sem("kb_done")
        knT_ps = sem("knT_ps")
        knT_done = sem("knT_done")
        A_ps = sem("A_ps")
        A_done = sem("A_done")
        Ap_ps = sem("Ap_ps")
        Ap_done = sem("Ap_done")
        kq_ps = sem("kq_ps")
        kq_done = sem("kq_done")
        AT_done = sem("AT_done")
        vkb_done = sem("vkb_done")
        G_init = sem("G_init")
        G_done = sem("G_done")
        GT_ps = sem("GT_ps")
        GT_done = sem("GT_done")
        uw_ps = sem("uw_ps")
        U_done = sem("U_done")
        WT_done = sem("WT_done")
        w_ps = sem("w_ps")
        ut_done = sem("ut_done")
        dS_ps = sem("dS_ps")
        S_done = sem("S_done")
        o_ps = sem("o_ps")
        o_done = sem("o_done")
        for_names = ("T_in0 T_in1 fs_tap fs_conv fsC_done fs_ps fs_done win_ps win_done fir_ps flw_done fl_ps fl64_done fl_in "
                     "st_sq st_done stz st_ps stT_done h1_ps h1_done lg_ps lgT_done lgs_ps lg_done ex_done mix_sq rms_v rms_s o_done2 "
                     "oT_ps oT_done g_in2 m_done gl_ps gl_done gexp g_ready gb_ps gd_done gT_ps gT_done bb_ps bb_done "
                     "gates e_in0 e_in1 e_scaled e_used up_ps up_done y_ps y_done xr_in out_done").split()
        S = {name: sem(name) for name in for_names}
        T_in = (S["T_in0"], S["T_in1"])
        e_in = (S["e_in0"], S["e_in1"])
        dve_chain = sem("dve_chain")
        pool_chain = sem("pool_chain")

        psB = ps[:, 0:2, :]
        psC = ps[:, 2:4, :]
        psOT = ps[:, 4:6, :].rearrange("p a (g q) -> p (a g) q", q=L)
        psM = ps[:, 6, 0:2 * D]
        psT = ps[:, 7, :]
        psT16 = psT.bitcast(BF16)

        used[0] = 0
        wv1 = sb("l1_wv", [P, D]); bv1 = sb("l1_bv", [P, D]); wo1 = sb("l1_wo", [P, D]); bo1 = sb("l1_bo", [P, D])
        wt = sb("l1_wt", [P, D]); wsc = sb("l1_wsc", [P, 4])
        identb = carve([P], BF16)
        sel = carve([NJ, DS + 1])
        st6 = carve([2, 6]); mv = sb("l1_mv", [P, 2, 2])
        nhalf = carve([2])
        xn1 = carve([2, 2, D])
        xn1T = carve([NB, L])
        V1 = carve([4, 2, HS, 32])
        res1 = carve([2, 2, HS, DS])
        KTM = carve([2, HS, SLOT], BF16)
        QTM = carve([2, HS, SLOT], BF16)
        KT = carve([3, HS // 2, L], BF16)
        QT = carve([3, HS // 2, L], BF16)
        mx = carve([2, 2, HS])
        mr = carve([2, 2, HS])
        mt = carve([2, 2, 2, MROWS, HS // 2], BF16)
        mT = carve([2, L], BF16)[0:2 * MROWS * HS // 2]
        E1 = carve([4, 2, L])
        OT1 = carve([4, L])
        rz = carve([2, HS // 2, NJ])[0:64]
        O1 = carve([NJ, HS, DS])[0:64]
        oT1 = carve([L])

        names1 = ("w_in var_done rstd_done w_abs w_sum w_scale w_tern seldone init xn_done x1b xT_ps xT_done P_ps V_done p1 r1 p2 r2 p3 q_done "
                 "tr_ps tr_done B_ps max_done m_split mT_ps mT_done m_in0 m_in1 m_in2 C_ps E_done PV_ps OT_done S1_ps S1_done S2_ps S2_done y_ps y_done "
                 "out_done psM_free psT_free chain pchain").split()
        Z = {n: sem("l1_" + n) for n in names1}
        m_in = (Z["m_in0"], Z["m_in1"], Z["m_in2"])

        AT_LN, AT_XT, AT_P, AT_SPLIT = -42, -40, -38, -37
        AT_TR = (-32, -30, -28, -26)
        AT_B = -24
        AT_M = -4
        AT_S1 = (19, 21)
        AT_S2 = 24
        AT_Y = 27
        LAG = 2
        FIRST, LAST = AT_LN, 16 * (NB - 1) + AT_Y + 3

        def due(s, at):
            b, r = divmod(s - at, 16)
            return b if r == 0 and 0 <= b < NB else None

        def heads_due(s, at):
            b, h = divmod(s - at, 16)
            return (b, h) if 0 <= b < NB else None

        order = {"M": [], "T": []}
        for s in range(FIRST, LAST):
            for name, at in (("xT", AT_XT), ("P", AT_P), ("S2", AT_S2), ("y", AT_Y)):
                b = due(s, at)
                if b is not None:
                    order["M"].append((name, b))
            for name, at in (("TR0", AT_TR[0]), ("TR1", AT_TR[1]), ("TR2", AT_TR[2]), ("TR3", AT_TR[3]), ("mT", AT_M), ("S10", AT_S1[0]), ("S11", AT_S1[1])):
                b = due(s, at)
                if b is not None:
                    order["T"].append((name, b))

        def before(bank, name, b):
            return order[bank].index((name, b))

        def head_rows(h, n):
            return slice(SLOT * (h % 2), SLOT * (h % 2) + n)

        def pe_program(pe):
            def free(bank, name, b):
                n = before(bank, name, b)
                if n:
                    pe.wait_ge(Z["psM_free" if bank == "M" else "psT_free"], n)

            pe.wait_ge(S["y_done"], NB)
            pe.wait_ge(S["up_done"], 6 * NB)
            pe.wait_ge(Z["w_abs"], 1)
            pe.wait_ge(Z["init"], 1)
            pe.matmul(psM[:, 0:1], ones[:], wsc[:, 0:1], start=True, stop=True).then_inc(Z["w_sum"], 1)
            pe.wait_ge(Z["w_scale"], 1)
            pe.wait_ge(Z["w_in"], 80)
            for s in range(FIRST, LAST):
                b = due(s, AT_XT)
                if b is not None:
                    pe.wait_ge(Z["xn_done"], b + 1)
                    free("M", "xT", b)
                    for t in range(2):
                        ins = pe.transpose(psM[:, P * t:P * t + P], xn1[:, b % 2, t, :], ident[:])
                    ins.then_inc(Z["xT_ps"], 1)
                b = due(s, AT_P)
                if b is not None:
                    pe.wait_ge(Z["xT_done"], b + 1)
                    free("M", "P", b)
                    for t in range(2):
                        ins = pe.matmul(psM[:, P * t:P * t + P], xn1T[:, b, P * t:P * t + P], wv1[:], start=True, stop=True)
                    ins.then_inc(Z["P_ps"], 1)
                for r in range(4):
                    b = due(s, AT_TR[r])
                    if b is not None:
                        pe.wait_ge(Z["q_done"], b + 1)
                        free("T", "TR%d" % r, b)
                        src = (KTM, QTM)[r % 2]
                        for pr in range(4):
                            pair = 4 * (r // 2) + pr
                            for t in range(2):
                                ins = pe.transpose(psT16[:, L * pr + P * t:L * pr + P * t + P],
                                                   src[:, t, 2 * pair:2 * pair + 2, :].rearrange("p h s -> p (h s)"), identb[:])
                        ins.then_inc(Z["tr_ps"], 1)
                bh = heads_due(s, AT_B)
                if bh:
                    b, h = bh
                    u = HS * b + h
                    pe.wait_ge(Z["tr_done"], 4 * b + 2 + 2 * (h // 8))
                    if u >= 2:
                        pe.wait_ge(Z["max_done"], u - 1)
                    rows = head_rows(h, ROWS)
                    for t in range(2):
                        ins = pe.matmul(psB[:, u % 2, L * t:L * t + L], QT[rows, b % 3, h // 2, P * t:P * t + P],
                                        KT[rows, b % 3, h // 2, :], start=True, stop=True)
                    ins.then_inc(Z["B_ps"], 1)
                b = due(s, AT_M)
                if b is not None:
                    pe.wait_ge(Z["m_split"], b + 1)
                    free("T", "mT", b)
                    for t in range(2):
                        ins = pe.transpose(psT16[0:48, P * t:P * t + P],
                                           mt[:, b % 2, t].rearrange("p a k h -> p (a k h)"), identb[:])
                    ins.then_inc(Z["mT_ps"], 1)
                bh = heads_due(s, 0)
                if bh:
                    b, h = bh
                    u = HS * b + h
                    if h == 0:
                        pe.wait_ge(m_in[b % 3], 32 * (b // 3 + 1))
                    if u >= 2:
                        pe.wait_ge(Z["E_done"], u - 1)
                    rows = head_rows(h, ROWS + MROWS)
                    for t in range(2):
                        ins = pe.matmul(psC[:, u % 2, L * t:L * t + L], KT[rows, b % 3, h // 2, P * t:P * t + P],
                                        QT[rows, b % 3, h // 2, :], start=True, stop=True)
                    ins.then_inc(Z["C_ps"], 1)
                bh = heads_due(s, LAG)
                if bh:
                    b, h = bh
                    u = HS * b + h
                    pe.wait_ge(Z["E_done"], u + 1)
                    if b and h % 8 == 0:
                        pe.wait_ge(Z["OT_done"], 2 * (b - 1) + 1 + h // 8)
                    jj = h % 4
                    for t in range(2):
                        ins = pe.matmul(psOT[32 * jj:32 * jj + 32, h // 4, :], V1[:, b % 4, t, h, :], E1[:, u % 4, t, :],
                                        start=(t == 0), stop=(t == 1))
                    ins.then_inc(Z["PV_ps"], 1)
                for k in range(2):
                    b = due(s, AT_S1[k])
                    if b is not None:
                        pe.wait_ge(Z["OT_done"], 2 * b + 2)
                        free("T", "S1%d" % k, b)
                        ot = OT1[:].rearrange("p g q -> p (g q)")
                        for r in range(8):
                            ins = pe.matmul(psT[0:64, 36 * r:36 * r + 36], ot[:, 8 * k + r::16], sel[:].rearrange("p j d -> p (j d)"), start=True, stop=True)
                        ins.then_inc(Z["S1_ps"], 1)
                b = due(s, AT_S2)
                if b is not None:
                    pe.wait_ge(Z["S1_done"], 2 * b + 2)
                    free("M", "S2", b)
                    for j in range(NJ):
                        ins = pe.transpose(psM[:, 64 * j:64 * j + 64], O1[:, j].rearrange("p r d -> p (r d)"), ident[0:64, 0:64])
                    ins.then_inc(Z["S2_ps"], 1)
                b = due(s, AT_Y)
                if b is not None:
                    pe.wait_ge(Z["S2_done"], b + 1)
                    free("M", "y", b)
                    if b == 0:
                        pe.wait_ge(Z["w_tern"], 1)
                    for t in range(2):
                        pe.matmul(psM[:, P * t:P * t + P], oT1[:, P * t:P * t + P], wo1[:], start=True, stop=False)
                        ins = pe.matmul(psM[:, P * t:P * t + P], xn1T[:, b, P * t:P * t + P], wt[:], start=False, stop=True)
                    ins.then_inc(Z["y_ps"], 1)

        def act_program(act):
            for s in range(FIRST, LAST):
                b = due(s, AT_XT)
                if b is not None:
                    act.wait_ge(Z["xT_ps"], b + 1)
                    act.copy(xn1T[:, b, :], psM).then_inc(Z["xT_done"], 1)
                    act.wait_ge(Z["xT_done"], b + 1)
                    act.nop().then_inc(Z["psM_free"], 1)
                b = due(s, AT_SPLIT)
                if b is not None:
                    v = V1[:, b % 4, :, :, 0:DS].rearrange("p t h d -> p (t h) d")
                    k = KTM[:, :, :, 0:ROWS].rearrange("p t h (g d) -> p (t h) g d", d=DS)
                    act.wait_ge(Z["V_done"], b + 1)
                    if b:
                        act.wait_ge(Z["tr_ps"], 4 * b)
                    act.copy(k[:, :, 0:3, :], v.unsqueeze(2).broadcast_to([P, 2 * HS, 3, DS])).then_inc(Z["p1"], 1)
                    act.wait_ge(Z["r1"], b + 1)
                    rr = res1[:, 0].rearrange("p t h d -> p (t h) d")
                    act.copy(k[:, :, 3:5, :], rr.unsqueeze(2).broadcast_to([P, 2 * HS, 2, DS])).then_inc(Z["p2"], 1)
                    act.wait_ge(Z["r2"], b + 1)
                    act.copy(k[:, :, 5, :], res1[:, 1].rearrange("p t h d -> p (t h) d")).then_inc(Z["p3"], 1)
                for r in (1, 3):
                    b = due(s, AT_TR[r])
                    if b is not None:
                        act.wait_ge(Z["tr_ps"], 4 * b + r + 1)
                        if b >= 3:
                            act.wait_ge(Z["C_ps"], HS * (b - 2))
                        act.copy(QT[:, b % 3, 4 * (r // 2):4 * (r // 2) + 4, :].rearrange("p a q -> p (a q)"), psT16).then_inc(Z["tr_done"], 1)
                        act.wait_ge(Z["tr_done"], 4 * b + r + 1)
                        act.nop().then_inc(Z["psT_free"], 1)
                bh = heads_due(s, 0)
                if bh:
                    b, h = bh
                    u = HS * b + h
                    act.wait_ge(Z["C_ps"], u + 1)
                    if u >= 4:
                        act.wait_ge(Z["PV_ps"], u - 3)
                    act.activation(E1[:, u % 4].rearrange("p t q -> p (t q)"), psC[:, u % 2, :], ACT.Exp, scale=DS ** -0.5).then_inc(Z["E_done"], 1)
                b = due(s, 17)
                if b is not None:
                    act.wait_ge(Z["PV_ps"], HS * b + 16)
                    act.wait_ge(Z["OT_done"], 2 * b + 1)
                    act.copy(OT1[:, 2:4, :], psOT[:, 2:4, :]).then_inc(Z["OT_done"], 1)
                b = due(s, AT_S2)
                if b is not None:
                    act.wait_ge(Z["S2_ps"], b + 1)
                    if b:
                        act.wait_ge(Z["y_ps"], b)
                    act.copy(oT1[:].rearrange("p (g j i) -> p j g i", g=4, j=NJ), psM.rearrange("p (j g i) -> p j g i", g=4, j=NJ)).then_inc(Z["S2_done"], 1)
                    act.wait_ge(Z["S2_done"], b + 1)
                    act.nop().then_inc(Z["psM_free"], 1)

        def dve_program(dve):
            chain1 = [0]

            def link1(ins):
                chain1[0] += 1
                ins.then_inc(Z["chain"], 1)
                dve.wait_ge(Z["chain"], chain1[0])

            dve.wait_ge(Z["w_in"], 80)
            dve.tensor_reduce(wsc[:, 0:1], wt[:], axis=AX.X, op=ALU.add, apply_absolute_value=True).then_inc(Z["w_abs"], 1)
            dve.wait_ge(Z["w_sum"], 1)
            link1(dve.tensor_scalar(wsc[:, 1:2], psM[:, 0:1], 1.0 / (D * D), 1e-5, ALU.mult, ALU.max))
            dve.reciprocal(wsc[:, 2:3], wsc[:, 1:2]).then_inc(Z["w_scale"], 1)
            for s in range(FIRST, LAST):
                b = due(s, AT_LN)
                if b is not None:
                    dve.wait_ge(S["y_done"], b + 1)
                    xb = x1[:, 2 * b:2 * b + 2, :]
                    for t in range(2):
                        link1(dve.bn_stats(st6[:, t, :], xb[:, t, :]))
                    for t in range(2):
                        link1(dve.bn_aggr(mv[:, t, :], st6[:, t, :]))
                    dve.tensor_scalar(mv[:, :, 1], mv[:, :, 1], EPS, None, ALU.add).then_inc(Z["var_done"], 1)
                    dve.wait_ge(Z["rstd_done"], b + 1)
                    if b >= 2:
                        dve.wait_ge(Z["xT_ps"], b - 1)
                    for t in range(2):
                        ins = dve.tensor_scalar(xn1[:, b % 2, t, :], xb[:, t, :], mv[:, t, 0:1], mv[:, t, 1:2], ALU.subtract, ALU.mult)
                    ins.then_inc(Z["xn_done"], 1)
                b = due(s, AT_P)
                if b is not None:
                    dve.wait_ge(Z["P_ps"], b + 1)
                    if b >= 4:
                        dve.wait_ge(Z["PV_ps"], HS * (b - 3))
                    v = V1[:, b % 4, :, :, 0:DS]
                    for t in range(2):
                        ins = dve.tensor_tensor(v[:, t], psM[:, P * t:P * t + P].rearrange("p (h d) -> p h d", d=DS),
                                            bv1[:].rearrange("p (h d) -> p h d", d=DS), ALU.add)
                    ins.then_inc(Z["V_done"], 1)
                    dve.wait_ge(Z["V_done"], b + 1)
                    dve.nop().then_inc(Z["psM_free"], 1)
                for r in (0, 2):
                    b = due(s, AT_TR[r])
                    if b is not None:
                        dve.wait_ge(Z["tr_ps"], 4 * b + r + 1)
                        if b >= 3:
                            dve.wait_ge(Z["C_ps"], HS * (b - 2))
                        dve.tensor_copy(KT[:, b % 3, 4 * (r // 2):4 * (r // 2) + 4, :].rearrange("p a q -> p (a q)"), psT16).then_inc(Z["tr_done"], 1)
                        dve.wait_ge(Z["tr_done"], 4 * b + r + 1)
                        dve.nop().then_inc(Z["psT_free"], 1)
                bh = heads_due(s, AT_B)
                if bh:
                    b, h = bh
                    u = HS * b + h
                    dve.wait_ge(Z["B_ps"], u + 1)
                    if b >= 2 and h == 0:
                        dve.wait_ge(Z["m_split"], b - 1)
                    dve.reduce_max(mx[:, b % 2, :, h], psB[:, u % 2, :].rearrange("p (t k) -> p t k", t=2), axis=AX.X).then_inc(Z["max_done"], 1)
                b = due(s, AT_B + 15)
                if b is not None:
                    dve.wait_ge(Z["max_done"], HS * b + 16)
                    if b >= 2:
                        dve.wait_ge(Z["mT_ps"], b - 1)
                    m = mx[:, b % 2].rearrange("p t (a r) -> p t r a", r=2)
                    r_ = mr[:, b % 2].rearrange("p t (a r) -> p t r a", r=2)
                    o = mt[:, b % 2]
                    for t in range(2):
                        link1(dve.tensor_scalar(o[:, t, :, 0], m[:, t], -1.0, None, ALU.mult))
                        link1(dve.scalar_tensor_tensor(out=r_[:, t], in0=m[:, t], scalar=-1.0, in1=o[:, t, :, 0], op0=ALU.mult, op1=ALU.subtract))
                        link1(dve.tensor_copy(o[:, t, :, 1], r_[:, t]))
                        link1(dve.tensor_tensor(r_[:, t], r_[:, t], o[:, t, :, 1], ALU.subtract))
                        ins = dve.tensor_copy(o[:, t, :, 2], r_[:, t])
                    ins.then_inc(Z["m_split"], 1)
                b = due(s, AT_M)
                if b is not None:
                    dve.wait_ge(Z["mT_ps"], b + 1)
                    if b >= 2:
                        dve.wait_ge(m_in[(b - 2) % 3], 32 * ((b - 2) // 3 + 1))
                    dve.tensor_copy(mT[:, b % 2, :], psT16[0:48, 0:L]).then_inc(Z["mT_done"], 1)
                    dve.wait_ge(Z["mT_done"], b + 1)
                    dve.nop().then_inc(Z["psT_free"], 1)
                b = due(s, 9)
                if b is not None:
                    dve.wait_ge(Z["PV_ps"], HS * b + 8)
                    if b:
                        dve.wait_ge(Z["S1_ps"], 2 * b)
                    dve.tensor_copy(OT1[:, 0:2, :], psOT[:, 0:2, :]).then_inc(Z["OT_done"], 1)
                for k in range(2):
                    b = due(s, AT_S1[k])
                    if b is not None:
                        dve.wait_ge(Z["S1_ps"], 2 * b + k + 1)
                        if b:
                            dve.wait_ge(Z["S2_ps"], b)
                        p = psT[0:64, 0:36 * 8].rearrange("p (r j d) -> p r j d", r=8, j=NJ)
                        link1(dve.reciprocal(rz[:, k], p[:, :, :, DS]))
                        dve.tensor_tensor(O1[:, :, 8 * k:8 * k + 8, :].rearrange("p j r d -> p r j d"), p[:, :, :, 0:DS],
                                          rz[:, k].unsqueeze(3).broadcast_to([64, 8, NJ, DS]), ALU.mult).then_inc(Z["S1_done"], 1)
                        dve.wait_ge(Z["S1_done"], 2 * b + k + 1)
                        dve.nop().then_inc(Z["psT_free"], 1)
                b = due(s, AT_Y)
                if b is not None:
                    dve.wait_ge(Z["y_ps"], b + 1)
                    dve.wait_ge(Z["x1b"], b + 1)
                    xb = x1[:, 2 * b:2 * b + 2, :].rearrange("p t d -> p (t d)")
                    dve.tensor_tensor(xb, psM, xb, ALU.add).then_inc(Z["y_done"], 1)
                    dve.wait_ge(Z["y_done"], b + 1)
                    dve.nop().then_inc(Z["psM_free"], 1)

        def pool_program(pool):
            chain1 = [0]

            def link1(ins):
                chain1[0] += 1
                ins.then_inc(Z["pchain"], 1)
                pool.wait_ge(Z["pchain"], chain1[0])
            pool.wait_ge(S["oT_done"], 1)
            link1(pool.memset(nhalf[:], -0.5))
            link1(pool.memset(KTM[:], 0.0))
            link1(pool.memset(KTM[:, :, :, ROWS:ROWS + MROWS], 1.0))
            link1(pool.memset(QTM[:], 0.0))
            link1(pool.memset(V1[:], 0.0))
            link1(pool.memset(V1[:, :, :, :, DS:DS + 1], 1.0))
            link1(pool.tensor_copy(identb[:], ident[:]))
            link1(pool.tensor_copy(sel[:], ident[:].rearrange("p (j d) -> p j d", j=NJ)[:, :, 0:DS + 1]))
            pool.nop().then_inc(Z["init"], 1)
            pool.wait_ge(Z["w_scale"], 1)
            link1(pool.tensor_scalar(wt[:], wt[:], wsc[:, 2:3], None, ALU.mult))
            link1(pool.tensor_scalar(wt[:], wt[:], 1.0, -1.0, ALU.min, ALU.max))
            link1(pool.tensor_scalar(wt[:], wt[:], ROUND, None, ALU.add))
            link1(pool.tensor_scalar(wt[:], wt[:], ROUND, None, ALU.subtract))
            pool.tensor_scalar(wt[:], wt[:], wsc[:, 1:2], None, ALU.mult).then_inc(Z["w_tern"], 1)
            for s in range(FIRST, LAST):
                b = due(s, AT_LN)
                if b is not None:
                    pool.wait_ge(Z["var_done"], b + 1)
                    pool.tensor_tensor(mv[:, :, 1], mv[:, :, 1], nhalf[:], ALU.pow).then_inc(Z["rstd_done"], 1)
                b = due(s, AT_SPLIT)
                if b is not None:
                    v = V1[:, b % 4, :, :, 0:DS].rearrange("p t h d -> p (t h) d")
                    k = KTM[:, :, :, 0:ROWS].rearrange("p t h (g d) -> p (t h) g d", d=DS)
                    q = QTM[:, :, :, 0:ROWS].rearrange("p t h (g d) -> p (t h) g d", d=DS)
                    r = [res1[:, i].rearrange("p t h d -> p (t h) d") for i in range(2)]
                    pool.wait_ge(Z["p1"], b + 1)
                    pool.tensor_tensor(r[0], v, k[:, :, 0, :], ALU.subtract).then_inc(Z["r1"], 1)
                    pool.wait_ge(Z["p2"], b + 1)
                    pool.tensor_tensor(r[1], r[0], k[:, :, 3, :], ALU.subtract).then_inc(Z["r2"], 1)
                    pool.tensor_copy(q[:, :, 0:6:3, :], k[:, :, 0:2, :])
                    pool.tensor_copy(q[:, :, 5, :], k[:, :, 0, :])
                    pool.tensor_copy(q[:, :, 1:5:3, :], k[:, :, 3:5, :])
                    pool.wait_ge(Z["p3"], b + 1)
                    pool.tensor_copy(q[:, :, 2, :], k[:, :, 5, :]).then_inc(Z["q_done"], 1)
                    pool.wait_ge(Z["xn_done"], b + 1)
                    xb = x1[:, 2 * b:2 * b + 2, :]
                    pool.tensor_tensor(xb, xb, bo1[:].unsqueeze(1).broadcast_to([P, 2, D]), ALU.add).then_inc(Z["x1b"], 1)

        def sp_program(sp):
            for dst, n in ((wv1, "wvT"), (bv1, "bv"), (wo1, "woT"), (bo1, "bo"), (wt, "wtT")):
                sp.dma_start(dst[:], inp["l1_" + n]).then_inc(Z["w_in"], 16)
            for s in range(FIRST, LAST):
                b = due(s, AT_M)
                if b is not None:
                    sp.wait_ge(Z["mT_done"], b + 1)
                    sp.wait_ge(Z["tr_done"], 4 * b + 4)
                    for par in range(2):
                        r0 = SLOT * par + ROWS
                        sp.dma_start(QT[r0:r0 + MROWS, b % 3], mT[24 * par:24 * par + 24, b % 2, :]).then_inc(m_in[b % 3], 16)
                b = due(s, AT_Y)
                if b is not None:
                    sp.wait_ge(Z["y_done"], b + 1)
                    sp.dma_start(out[b].rearrange("(t p) d -> p t d", p=P), x1[:, 2 * b:2 * b + 2, :]).then_inc(Z["out_done"], 16)
            sp.wait_ge(Z["out_done"], 16 * NB)


        block = ctx.enter_context(nc.Block())

        KV = {"k": 0, "v": 1, "q": 2}

        def chunk_tile(ap, n, bh):
            return ap[:, n, Q4 * bh:Q4 * bh + Q4, :].rearrange("p q c -> p (q c)")

        psW = ps[:, 4, 0:BH * D].rearrange("p (b x) -> p b x", b=BH)
        psO = ps[:, 5, 0:BH * D].rearrange("p (b x) -> p b x", b=BH)
        psS = ps[:, 0:4, 0:BH * DH].rearrange("p q (b x) -> p q b x", b=BH)

        def chunked(ap):
            return ap.rearrange("p b (n c) -> p b n c", c=C)

        def by_batch(ap):
            return ap.rearrange("p n b c -> p b n c")

        def gt_view(a, r):
            return GT[W64 * a:W64 * a + W64, 16 * r:16 * r + 16, :]

        def gt_ps(bank, a):
            return flat(bank)[0:W64].rearrange("p (c a x) -> p c a x", a=2, x=H * NG)[:, :, a, :]

        def wt_view(q):
            return WT.rearrange("p n (bh q) c -> p n bh q c", q=Q4)[:, :, :, q, :]

        def wt_ps(q):
            return PB[:, q, :].rearrange("p (n b c) -> p n b c", b=BH, c=C)

        def fl64_view(r):
            return fl64.rearrange("p w (h d) -> p w h d", h=H)[:, :, :, 16 * r:16 * r + 16]

        def fl_psv(bank):
            return flat(bank)[0:W64].rearrange("p (d h w) -> p w h d", h=H, w=NW)

        SRC = (fs_sl[:], fl_sl[:], delta_sl, v_sl[:])

        def heads(ap):
            return ap.rearrange("p g (h d) -> p (g h) d", d=DH)

        LB = bcst[:, 0:16].rearrange("p (h k) -> p h k", h=H)

        def act_tail(act):
            act.wait_ge(S["fs_conv"], 1)
            act.copy(fsC.rearrange("p n b c -> p b n c"), chunked(fsT[:])).then_inc(S["fsC_done"], 1)
            act.wait_ge(S["fs_ps"], 1)
            act.copy(fs_sl[:].rearrange("p g d -> p (g d)"), flat(PA)).then_inc(S["fs_done"], 1)
            act.wait_ge(S["fs_done"], 1)
            act.wait_ge(S["fl_in"], 16 * 16)
            act.wait_ge(o_done, NCH)
            for i, src in enumerate(SRC):
                if i:
                    act.wait_ge(S["st_done"], i)
                act.activation(sq[:], src, ACT.Square).then_inc(S["st_sq"], 1)
            act.wait_ge(S["st_done"], 5)
            l2 = stats[:, :, 3:16:4]
            act.activation(l2, l2, ACT.Sqrt).then_inc(S["st_sq"], 1)
            act.wait_ge(S["st_ps"], 1)
            act.copy(statsT, flat(PA)).then_inc(S["stT_done"], 1)
            for u in range(2 * H):
                act.wait_ge(S["h1_ps"], u + 1)
                if u >= 2:
                    act.wait_ge(S["lg_ps"], u - 1)
                act.activation(h1[:, u % 2, :], flat(PA[:, 2 * (u % 2):2 * (u % 2) + 2, :]), ACT.Gelu,
                               bias=b1[:]).then_inc(S["h1_done"], 1)
            act.wait_ge(S["lg_ps"], 2 * H)
            act.copy(logT, flat(PB)).then_inc(S["lgT_done"], 1)
            act.wait_ge(S["lg_done"], 1)
            act.activation(bcst[:, 44:48], bcst[:, 40:44], ACT.Exp, scale=-1.0).then_inc(S["ex_done"], 1)
            act.wait_ge(S["ex_done"], 1)
            act.activation(bcst[:, 44:48], bcst[:, 44:48], ACT.Ln, bias=1.0).then_inc(S["ex_done"], 1)
            act.activation(bcst[:, 48:52], bcst[:, 24:28], ACT.Sigmoid).then_inc(S["ex_done"], 1)
            act.wait_ge(S["lg_done"], 2)
            act.activation(lg[:], lg[:], ACT.Exp).then_inc(S["ex_done"], 1)
            act.wait_ge(S["mix_sq"], 1)
            act.activation(sq[:], osl, ACT.Square).then_inc(S["mix_sq"], 1)
            act.wait_ge(S["rms_v"], 1)
            act.activation(gp[:, 0, :], gp[:, 0, :], ACT.Sqrt, scale=1.0 / DH, bias=small[:, 7, 0:1]).then_inc(S["rms_s"], 1)
            act.wait_ge(S["oT_ps"], 1)
            act.activation(oT.rearrange("p b (n c) -> p n b c", c=C), flat(PA).rearrange("p (n b c) -> p n b c", b=NB, c=C),
                           ACT.Copy, scale=rmsw[:]).then_inc(S["oT_done"], 1)
            act.wait_ge(S["gl_done"], 1)
            act.activation(gw[:, 0:8], gw[:, 0:8], ACT.Exp).then_inc(S["gexp"], 1)
            for b in range(NB):
                for e in range(3):
                    bias = wm if e == 0 else we[:, e - 1, :]
                    for m in range(2):
                        u = 6 * b + 2 * e + m
                        act.wait_ge(S["up_ps"], u + 1)
                        if b and m == 0 and e == 0:
                            act.wait_ge(S["y_ps"], b)
                        for k in (2 * m, 2 * m + 1):
                            ins = act.activation(hT[:, e, k, :], PA[:, u % 2, L * (k % 2):L * (k % 2) + L],
                                                 ACT.Gelu_apprx_tanh, bias=bias[:, HID + k:HID + k + 1])
                        ins.then_inc(S["up_done"], 1)
            act_program(act)

        @block.sync
        def _(sp):
            sp.dma_start(X[:], inp["x"]).then_inc(x_in, 16)
            for dst, name in ((w1x[:], "w1x"), (w1s[:], "w1s"), (b1[:], "b1"), (bcst[:, 0:40], "bcst"), (rmsw[:], "rmsw"),
                              (wo[:], "wo"), (wm[:], "wm"), (wg[:], "wg"), (bgate[:], "bgate"), (b2e[:], "b2e"),
                              (b2m[:], "b2m"), (alph[:, 0:1], "alpha")):
                sp.dma_start(dst, inp[name]).then_inc(S["g_in2"], 16)
            sp.wait_ge(S["stz"], 1)
            sp.dma_start(w2p[:, 0:4], inp["w2"]).then_inc(S["g_in2"], 16)
            for j in range(4):
                if j >= 2:
                    sp.wait_ge(S["fir_ps"], j - 1)
                for h in range(H):
                    src = bass.AP(inp["frev"].tensor, (DH * h + 8 * j) * 192, [[1, P], [192, 8], [1, W64]])
                    sp.dma_start(Tf[:, j % 2, h, :, :], src).then_inc(T_in[j % 2], 16)
            sp.wait_ge(S["fl64_done"], 2)
            for q in range(Q4):
                for par in range(2):
                    for bh in range(BH):
                        src = fl64[C * par:C * par + C, 4 * (Q4 * bh + q):4 * (Q4 * bh + q) + 4, :]
                        dst = fl_sl[C * q:C * q + C].rearrange("p (nh par bh) x -> p nh par bh x", par=2, bh=BH)[:, :, par, bh, :]
                        sp.dma_start(dst, src).then_inc(S["fl_in"], 16)
            sp.wait_ge(S["fsC_done"], 1)
            sp.dma_start(xres, inp["x"]).then_inc(S["xr_in"], 16)
            sp.wait_ge(S["g_ready"], 1)
            for i in range(NB * TOPK):
                if i >= 2:
                    sp.wait_ge(S["y_ps"], i // 2)
                e = sp.value_load(idx[i // TOPK:i // TOPK + 1, i % TOPK:i % TOPK + 1], min_val=0, max_val=NE - 1)
                sp.dma_start(we[:, i % 2, :], inp["experts"][bass.ds(e, 1), :, :].rearrange("e p x -> p (e x)")).then_inc(e_in[i % 2], 16)
            sp_program(sp)

        @block.gpsimd
        def _(pool):
            chain = [0]

            def link(ins):
                chain[0] += 1
                ins.then_inc(pool_chain, 1)
                pool.wait_ge(pool_chain, chain[0])

            link(pool.memset(ident[:], 0.0))
            pool.affine_select(out=ident[:], in_=ident[:], compare_op=ALU.not_equal, fill=1.0, base=0,
                               pattern=[[-1, P]], channel_multiplier=1).then_inc(consts, 1)
            link(pool.memset(tri[:], 1.0))
            for q in range(Q4):
                link(pool.affine_select(out=tri[C * q:C * q + C, :], in_=tri[C * q:C * q + C, :],
                                        compare_op=ALU.is_ge, fill=0.0, base=0,
                                        pattern=[[1, C]], channel_multiplier=-1))
            pool.memset(ones[:], 1.0).then_inc(consts, 1)
            link(pool.memset(w2p[:], 0.0))
            pool.iota(iota8[:], [[1, NE]], base=0, channel_multiplier=0, allow_small_or_imprecise_dtypes=True).then_inc(S["stz"], 1)
            link(pool.memset(G[:], 0.0))
            pool.affine_select(out=G[:], in_=G[:], compare_op=ALU.not_equal, fill=1.0, base=0,
                               pattern=[[1, C], [0, 2], [-1, C]], channel_multiplier=0).then_inc(G_init, 1)
            pool.wait_ge(beta_done, 1)
            pool.wait_ge(silu_done, 3)
            for src, dst, ready in ((v_sl, vb_sl, vs_done), (k_sl, kb_sl, sl_done)):
                pool.wait_ge(ready, 1)
                pool.tensor_tensor(dst[:].rearrange("p g (h d) -> p g h d", h=H),
                                   src[:].rearrange("p g (h d) -> p g h d", h=H),
                                   bc(beta_sl[:].rearrange("p h g -> p g h"), 3, DH), ALU.mult).then_inc(vkb_done, 1)
            pool.wait_ge(kq_done, 1)
            at3 = AT[:].rearrange("p h g c -> p (h g) c")
            pool.tensor_tensor(at3, at3, bc(tri[:], 1, H * NG), ALU.mult).then_inc(AT_done, 1)
            pool.wait_ge(GT_ps, 2)
            pool.memset(stats, 0.0).then_inc(S["stz"], 1)
            pool.wait_ge(S["gates"], 1)
            for i in range(NB * TOPK):
                pool.wait_ge(e_in[i % 2], 16 * (i // 2 + 1))
                w2 = we[:, i % 2, HID + NBLK:]
                pool.tensor_scalar(w2, w2, gall[:, i:i + 1], None, ALU.mult).then_inc(S["e_scaled"], 1)
            pool_program(pool)

        @block.scalar
        def _(act):
            act.dma_start(wqkv[:], inp["wqkv"]).then_inc(w_in, 16)
            act.dma_start(wb[:], inp["wb"]).then_inc(w_in, 16)
            act.dma_start(cw[:], inp["cw"]).then_inc(w_in, 16)
            act.dma_start(fsw[:], inp["fsw"]).then_inc(w_in, 16)
            act.wait_ge(xc_done, 1)
            act.activation(sq[:], xn[:], ACT.Square).then_inc(xsq, 1)
            act.wait_ge(lnvar, 1)
            act.activation(small[:, 1, 0:NT], small[:, 1, 0:NT], ACT.Sqrt, scale=1.0 / D,
                           bias=small[:, 7, 0:1]).then_inc(lnstd, 1)
            for i in (2, 3):
                act.wait_ge(xT_ps, i + 1)
                act.copy(xnT[:, 2 * i:2 * i + 2, :], PA[:, i, :]).then_inc(xnT_done, 1)
            act.wait_ge(w_in, 64)

            def newest_tap(i, y, bank):
                act.wait_ge(proj_ps, i + 1)
                act.activation(y[:].rearrange("p b l -> p (b l)"), flat(bank), ACT.Copy,
                               scale=cw[:, i, TAPS - 1:TAPS]).then_inc(tap_done, 1)

            newest_tap(0, y0, PB)
            newest_tap(1, y1, PA)
            act.wait_ge(conv_done, 1)
            act.activation(by_batch(kT[:]), chunked(y0[:]), ACT.Silu).then_inc(silu_done, 1)
            act.wait_ge(silu_done, 1)
            newest_tap(2, y0, PB)
            act.wait_ge(conv_done, 2)
            act.activation(by_batch(vT[:]), chunked(y1[:]), ACT.Silu)
            act.activation(vTp[:, :, W64:], y1[:], ACT.Silu).then_inc(silu_done, 1)
            act.wait_ge(conv_done, 3)
            act.activation(by_batch(qT[:]), chunked(y0[:]), ACT.Silu).then_inc(silu_done, 1)
            act.wait_ge(sl_ps, 1)
            act.activation(sq[:].rearrange("p a b -> p (a b)"), flat(PA), ACT.Square).then_inc(slsq, 1)
            act.wait_ge(ssq, 1)
            act.activation(small[:, 2, :], small[:, 2, :], ACT.Sqrt, bias=small[:, 7, 1:2]).then_inc(norm, 1)
            act.wait_ge(proj_ps, 4)
            act.activation(by_batch(betaT), flat(PB)[0:H].rearrange("p (b n c) -> p b n c", n=NCH, c=C),
                           ACT.Sigmoid).then_inc(beta_fm, 1)
            act.wait_ge(sl_ps, 3)
            act.copy(v_sl[:].rearrange("p a b -> p (a b)"), flat(PA)).then_inc(vs_done, 1)
            act.wait_ge(sl_ps, 4)
            act.activation(sq[:].rearrange("p a b -> p (a b)"), flat(PA), ACT.Square).then_inc(slsq, 1)
            act.wait_ge(ssq, 2)
            act.activation(small[:, 3, :], small[:, 3, :], ACT.Sqrt, bias=small[:, 7, 1:2]).then_inc(norm, 1)
            act.wait_ge(knT_ps, 2)
            act.copy(knT[:, NCH // 2:].rearrange("p n b c -> p (n b c)"), flat(PB[:, 2:4, :])).then_inc(knT_done, 1)
            act.wait_ge(A_ps, 2)
            act.copy(A64[0:W64, 1].rearrange("p h g c -> p (h g c)"), flat(PB)[0:W64]).then_inc(A_done, 1)
            act.wait_ge(sl_ps, 2)
            act.activation(fsT[:], vTp[:, :, W64:], ACT.Copy, scale=fsw[:, FS_TAPS - 1:FS_TAPS]).then_inc(S["fs_tap"], 1)
            act.wait_ge(kq_ps, 1)
            act.copy(AT[:].rearrange("p h g c -> p (h g c)"), flat(PB)).then_inc(kq_done, 1)
            act.wait_ge(S["win_ps"], 2)
            act.copy(vwin[:, NW // 2:, :].rearrange("p w x -> p (w x)"), flat(PB)).then_inc(S["win_done"], 1)
            for j in range(4):
                act.wait_ge(S["fir_ps"], j + 1)
                act.copy(flw[:, 8 * j:8 * j + 8, :],
                         PA[:, j, :].rearrange("p (d o) -> p d o", o=W64)[:, :, ::-1]).then_inc(S["flw_done"], 1)
            act.wait_ge(S["fl_ps"], 2)
            act.copy(fl64_view(1), fl_psv(PB)).then_inc(S["fl64_done"], 1)
            act.wait_ge(GT_ps, 2)
            for a in range(2):
                ins = act.copy(gt_view(a, 1), gt_ps(PB, a))
            ins.then_inc(GT_done, 1)
            act.wait_ge(uw_ps, 1)
            act.copy(U.rearrange("p g d -> p (g d)"), flat(PA)).then_inc(U_done, 1)
            act.wait_ge(uw_ps, 2)
            for q in (2, 3):
                ins = act.copy(wt_view(q), wt_ps(q))
            ins.then_inc(WT_done, 1)
            act_tail(act)

        @block.vector
        def _(dve):
            chain = [0]

            def link(ins):
                chain[0] += 1
                ins.then_inc(dve_chain, 1)
                dve.wait_ge(dve_chain, chain[0])

            dve.memset(small[:, 7, 0:1], EPS)
            dve.memset(small[:, 7, 1:2], 1e-6)
            dve.memset(vTp[:, :, 0:W64], 0.0)
            link(dve.memset(Sbd[:], 0.0))
            dve.wait_ge(x_in, 16)
            link(dve.reduce_sum(small[:, 0, 0:NT], X[:], axis=AX.X))
            link(dve.tensor_scalar(small[:, 0, 0:NT], small[:, 0, 0:NT], 1.0 / D, None, ALU.mult))
            dve.tensor_tensor(xn[:], X[:], bc(small[:, 0, 0:NT], 2, D), ALU.subtract).then_inc(xc_done, 1)
            dve.wait_ge(xsq, 1)
            dve.reduce_sum(small[:, 1, 0:NT], sq[:], axis=AX.X).then_inc(lnvar, 1)
            dve.wait_ge(lnstd, 1)
            link(dve.reciprocal(small[:, 1, 0:NT], small[:, 1, 0:NT]))
            dve.tensor_tensor(xn[:], xn[:], bc(small[:, 1, 0:NT], 2, D), ALU.mult).then_inc(xn_done, 1)
            for i in (0, 1):
                dve.wait_ge(xT_ps, i + 1)
                dve.tensor_copy(xnT[:, 2 * i:2 * i + 2, :], PA[:, i, :]).then_inc(xnT_done, 1)
            for i, (y, bank) in enumerate(((y0, PB), (y1, PA), (y0, PB))):
                dve.wait_ge(tap_done, i + 1)
                p3 = flat(bank).rearrange("p (b l) -> p b l", b=NB)
                for s in range(1, TAPS):
                    ins = dve.scalar_tensor_tensor(out=y[:, :, s:], in0=p3[:, :, 0:L - s],
                                                   scalar=cw[:, i, TAPS - 1 - s:TAPS - s], in1=y[:, :, s:],
                                                   op0=ALU.mult, op1=ALU.add)
                    if s < TAPS - 1:
                        link(ins)
                ins.then_inc(conv_done, 1)
            dve.wait_ge(slsq, 1)
            dve.reduce_sum(small[:, 2, :], sq[:].rearrange("p g (h d) -> p (g h) d", d=DH), axis=AX.X).then_inc(ssq, 1)
            dve.wait_ge(norm, 1)
            link(dve.reciprocal(small[:, 2, :], small[:, 2, :]))
            dve.tensor_tensor(k_sl[:].rearrange("p g (h d) -> p (g h) d", d=DH),
                              flat(PA).rearrange("p (g d) -> p g d", d=DH),
                              bc(small[:, 2, :], 2, DH), ALU.mult).then_inc(sl_done, 1)
            dve.wait_ge(sl_ps, 2)
            dve.tensor_copy(beta_sl[:].rearrange("p h g -> p g h"),
                            PB[:, 0, 0:NG * H].rearrange("p (g h) -> p g h", h=H)).then_inc(beta_done, 1)
            dve.wait_ge(bp_ps, 1)
            for qhi in range(2):
                ins = dve.tensor_copy(beta_p[W64 * qhi:W64 * qhi + W64, :], PB[0:W64, 1 + qhi, 0:W64])
            ins.then_inc(sl_done, 1)
            dve.wait_ge(slsq, 2)
            dve.reduce_sum(small[:, 3, :], sq[:].rearrange("p g (h d) -> p (g h) d", d=DH), axis=AX.X).then_inc(ssq, 1)
            dve.wait_ge(norm, 2)
            link(dve.reciprocal(small[:, 3, :], small[:, 3, :]))
            dve.wait_ge(knT_ps, 1)
            dve.tensor_copy(knT[:, 0:NCH // 2].rearrange("p n b c -> p (n b c)"), flat(PB[:, 0:2, :])).then_inc(knT_done, 1)
            dve.wait_ge(A_ps, 1)
            dve.tensor_copy(A64[0:W64, 0].rearrange("p h g c -> p (h g c)"), flat(PA)[0:W64]).then_inc(A_done, 1)
            dve.wait_ge(Ap_ps, 1)
            dve.tensor_tensor(Ap[:].rearrange("p s q c -> p s (q c)"), flat(PA).rearrange("p (s x) -> p s x", s=C),
                              bc(beta_p[:], 1, C), ALU.mult).then_inc(Ap_done, 1)
            dve.wait_ge(Ap_done, 1)
            dve.wait_ge(G_init, 1)
            for s in range(C - 1):
                m, w = C - 1 - s, s + 1
                t = tmp[:, 0:m * 2 * w].rearrange("p (c q t) -> p c q t", q=2, t=w)
                link(dve.tensor_tensor(t, bc(Ap[:, s, :, w:].rearrange("p q c -> p c q"), 3, w),
                                       bc(G[:, s, :, 0:w], 1, m), ALU.mult))
                ins = dve.tensor_tensor(G[:, w:, :, 0:w], G[:, w:, :, 0:w], t, ALU.subtract)
                if s < C - 2:
                    link(ins)
            ins.then_inc(G_done, 1)
            dve.wait_ge(S["win_ps"], 1)
            dve.tensor_copy(vwin[:, 0:NW // 2, :].rearrange("p w x -> p (w x)"), flat(PA)).then_inc(S["win_done"], 1)
            dve.wait_ge(S["fl_ps"], 1)
            dve.tensor_copy(fl64_view(0), fl_psv(PA)).then_inc(S["fl64_done"], 1)
            dve.wait_ge(GT_ps, 1)
            for a in range(2):
                ins = dve.tensor_copy(gt_view(a, 0), gt_ps(PA, a))
            ins.then_inc(GT_done, 1)
            dve.wait_ge(S["fs_tap"], 1)
            for t in range(1, FS_TAPS):
                ins = dve.scalar_tensor_tensor(out=fsT[:], in0=vTp[:, :, W64 - t:W64 - t + L],
                                               scalar=fsw[:, FS_TAPS - 1 - t:FS_TAPS - t], in1=fsT[:],
                                               op0=ALU.mult, op1=ALU.add)
                if t < FS_TAPS - 1:
                    link(ins)
            ins.then_inc(S["fs_conv"], 1)
            dve.wait_ge(uw_ps, 2)
            for q in (0, 1):
                ins = dve.tensor_copy(wt_view(q), wt_ps(q))
            ins.then_inc(WT_done, 1)
            for n in range(NCH):
                gs = slice(BH * n, BH * n + BH)
                if n:
                    dve.wait_ge(w_ps, n)
                    dve.tensor_tensor(U[:, gs, :], U[:, gs, :], psW, ALU.subtract).then_inc(ut_done, 1)
                if n < NCH - 1:
                    dve.wait_ge(dS_ps, n + 1)
                    for h in range(H):
                        hs = slice(DH * h, DH * h + DH)
                        old, new = (Sbd[hs, i % 2].rearrange("p (bh q) x -> p q bh x", q=Q4)[:, :, :, hs]
                                    for i in (n, n + 1))
                        if n:
                            ins = dve.tensor_tensor(new, old, psS[hs], ALU.add)
                        else:
                            ins = dve.tensor_copy(new, psS[hs])
                    ins.then_inc(S_done, 1)
                dve.wait_ge(o_ps, n + 1)
                dve.tensor_tensor(delta_sl[:, gs, :].rearrange("p g (h d) -> p (g h) d", d=DH),
                                  psO.rearrange("p g (h d) -> p (g h) d", d=DH),
                                  bc(small[:, 3, BH * H * n:BH * H * (n + 1)], 2, DH), ALU.mult).then_inc(o_done, 1)

            dve.wait_ge(S["stz"], 2)
            dve.wait_ge(S["fl_in"], 16 * 16)
            dve.wait_ge(S["fs_done"], 1)
            for i, src in enumerate(SRC):
                dve.reduce_sum(stats[:, :, 4 * i], heads(src), axis=AX.X)
                dve.tensor_reduce(stats[:, :, 4 * i + 2], heads(src), axis=AX.X, op=ALU.add, apply_absolute_value=True)
                dve.wait_ge(S["st_sq"], i + 1)
                dve.reduce_sum(stats[:, :, 4 * i + 3], heads(sq[:]), axis=AX.X).then_inc(S["st_done"], 1)
            dve.wait_ge(S["st_done"], 4)
            link(dve.tensor_scalar(stats[:, :, 0:16:2], stats[:, :, 0:16:2], 1.0 / DH, None, ALU.mult))
            mean, var, l2 = (stats[:, :, k:16:4] for k in (0, 1, 3))
            link(dve.tensor_tensor(var, mean, mean, ALU.mult))
            dve.scalar_tensor_tensor(out=var, in0=l2, scalar=1.0 / DH, in1=var, op0=ALU.mult,
                                     op1=ALU.subtract).then_inc(S["st_done"], 1)
            dve.wait_ge(S["g_in2"], 16 * 13)
            link(dve.tensor_tensor(LB, LB, bc(bcst[:, 16:20], 1, H), ALU.add))
            link(dve.scalar_tensor_tensor(out=bcst[:, 40:44], in0=bcst[:, 20:24], scalar=-1.0, in1=bcst[:, 20:24],
                                          op0=ALU.mult, op1=ALU.max))
            dve.wait_ge(S["lgs_ps"], 1)
            lps = flat(PA).rearrange("p (g h k) -> p g h k", h=H, k=32)[:, :, :, 0:4]
            lg4 = lg[:].rearrange("p (g h) k -> p g h k", h=H)
            dve.tensor_tensor(lg4, lps, bc(LB, 1, NG), ALU.add).then_inc(S["lg_done"], 1)
            dve.wait_ge(S["ex_done"], 3)
            link(dve.scalar_tensor_tensor(out=bcst[:, 44:48], in0=bcst[:, 20:24], scalar=0.0, in1=bcst[:, 44:48],
                                          op0=ALU.max, op1=ALU.add))
            link(dve.tensor_scalar(bcst[:, 44:48], bcst[:, 44:48], 1e-4, None, ALU.add))
            link(dve.reciprocal(bcst[:, 44:48], bcst[:, 44:48]))
            link(dve.tensor_tensor(lg4, lg4, bc(bc(bcst[:, 44:48], 1, NG), 3, 4), ALU.mult))
            link(dve.reduce_max(gp[:, 0, :], lg[:], axis=AX.X))
            dve.tensor_tensor(lg[:], lg[:], bc(gp[:, 0, :], 2, 4), ALU.subtract).then_inc(S["lg_done"], 1)
            dve.wait_ge(S["ex_done"], 4)
            for last in range(2):
                link(dve.reduce_sum(gp[:, 1, :], lg[:], axis=AX.X))
                link(dve.reciprocal(gp[:, 1, :], gp[:, 1, :]))
                link(dve.tensor_tensor(lg[:], lg[:], bc(gp[:, 1, :], 2, 4), ALU.mult))
                if not last:
                    link(dve.tensor_scalar(lg[:, :, 0:2], lg[:, :, 0:2], 0.05, None, ALU.max))
            p0 = lg4[:, :, :, 0]
            link(dve.scalar_tensor_tensor(out=p0, in0=bc(bcst[:, 48:52], 1, NG), scalar=0.5, in1=p0, op0=ALU.mult, op1=ALU.add))
            link(dve.tensor_tensor(heads(osl), heads(SRC[0]), bc(lg[:, :, 0], 2, DH), ALU.mult))
            for i in range(1, 4):
                link(dve.tensor_tensor(heads(sq[:]), heads(SRC[i]), bc(lg[:, :, i], 2, DH), ALU.mult))
                ins = dve.tensor_tensor(osl, osl, sq[:], ALU.add)
                if i < 3:
                    link(ins)
            ins.then_inc(S["mix_sq"], 1)
            dve.wait_ge(S["mix_sq"], 2)
            dve.reduce_sum(gp[:, 0, :], heads(sq[:]), axis=AX.X).then_inc(S["rms_v"], 1)
            dve.wait_ge(S["rms_s"], 1)
            link(dve.reciprocal(gp[:, 0, :], gp[:, 0, :]))
            dve.tensor_tensor(heads(osl), heads(osl), bc(gp[:, 0, :], 2, DH), ALU.mult).then_inc(S["o_done2"], 1)
            dve.wait_ge(xnT_done, 4)
            dve.reduce_sum(small[:, 4, 0:NB], xnT[:], axis=AX.X).then_inc(S["m_done"], 1)
            dve.wait_ge(S["gl_ps"], 1)
            link(dve.scalar_tensor_tensor(out=gw[:, 0:8], in0=PB[0:NB, 0, 0:NE], scalar=1.0 / L, in1=bgate[:],
                                          op0=ALU.mult, op1=ALU.add))
            link(dve.reduce_max(gw[:, 8:9], gw[:, 0:8], axis=AX.X))
            dve.tensor_scalar(gw[:, 0:8], gw[:, 0:8], gw[:, 8:9], None, ALU.subtract).then_inc(S["gl_done"], 1)
            dve.wait_ge(S["gexp"], 1)
            link(dve.reduce_sum(gw[:, 8:9], gw[:, 0:8], axis=AX.X))
            link(dve.reciprocal(gw[:, 8:9], gw[:, 8:9]))
            link(dve.tensor_scalar(gw[:, 0:8], gw[:, 0:8], gw[:, 8:9], None, ALU.mult))
            link(dve.max(gw[:, 16:24], gw[:, 0:8]))
            dve.max_index(idx[:], gw[:, 16:24], gw[:, 0:8]).then_inc(S["g_ready"], 1)
            dve.wait_ge(S["g_ready"], 1)
            link(dve.reduce_sum(gw[:, 8:9], gw[:, 16:18], axis=AX.X))
            link(dve.reciprocal(gw[:, 8:9], gw[:, 8:9]))
            link(dve.tensor_scalar(alph[:, 1:2], alph[:, 0:1], 0.1, 1.0, ALU.max, ALU.min))
            link(dve.tensor_scalar(alph[:, 2:3], alph[:, 1:2], -1.0, 1.0, ALU.mult, ALU.add))
            link(dve.tensor_scalar(gw[:, 24:26], gw[:, 16:18], gw[:, 8:9], alph[0:NB, 2:3], ALU.mult, ALU.mult))
            link(dve.tensor_copy(gw[:, 26:28], idx[:, 0:2]))
            link(dve.tensor_scalar(gw[:, 32:40], iota8[:], gw[:, 26:27], gw[:, 24:25], ALU.is_equal, ALU.mult))
            link(dve.tensor_scalar(gw[:, 40:48], iota8[:], gw[:, 27:28], gw[:, 25:26], ALU.is_equal, ALU.mult))
            link(dve.tensor_tensor(gw[:, 32:40], gw[:, 32:40], gw[:, 40:48], ALU.add))
            link(dve.tensor_copy(gw[0:1, 48:56], alph[0:1, 1:2].broadcast_to([1, NB])))
            w2 = wm[:, HID + NBLK:]
            link(dve.tensor_scalar(w2, w2, alph[:, 1:2], None, ALU.mult))
            dve.tensor_tensor(gwd[:], bc(ident[0:NB, 0:NB], 2, TOPK), bc(gw[:, 24:26], 1, NB), ALU.mult).then_inc(S["gd_done"], 1)
            dve.wait_ge(S["gT_ps"], 1)
            dve.tensor_copy(gall[:], PB[:, 0, 0:NB * TOPK]).then_inc(S["gates"], 1)
            dve.tensor_copy(gw[:, 56:64], PB[0:NE, 1, 0:NB]).then_inc(S["gT_done"], 1)
            dve.wait_ge(S["bb_ps"], 1)
            dve.tensor_copy(biasb[:], PB[0:NB, 2, 0:D]).then_inc(S["bb_done"], 1)
            for b in range(NB):
                dve.wait_ge(S["y_ps"], b + 1)
                if b == 0:
                    dve.wait_ge(S["xr_in"], 16)
                dve.tensor_tensor(x1[:, 2 * b:2 * b + 2, :], PB[:, 2 + b % 2, 0:2 * D].rearrange("p (t d) -> p t d", d=D),
                                  xres[:, 2 * b:2 * b + 2, :], ALU.add).then_inc(S["y_done"], 1)
            dve_program(dve)

        @block.tensor
        def _(pe):
            pe.wait_ge(consts, 2)
            pe.wait_ge(xn_done, 1)
            for i in range(NT):
                ins = pe.transpose(PA[:, i // 4, P * (i % 4):P * (i % 4) + P], xn[:, i, :], ident[:])
                if i % 4 == 3:
                    ins.then_inc(xT_ps, 1)
            pe.wait_ge(w_in, 64)
            pe.wait_ge(xnT_done, 4)

            def project(w, bank, m=P):
                for j in range(4):
                    ins = pe.matmul(bank[0:m, j, :], w, xnT[:, 2 * j:2 * j + 2, :], start=True, stop=True)
                ins.then_inc(proj_ps, 1)

            def to_chunks(src, bank):
                for n in range(NCH):
                    for bh in range(BH):
                        g = BH * n + bh
                        ins = pe.transpose(bank[:, g // 4, P * (g % 4):P * (g % 4) + P], chunk_tile(src, n, bh), ident[:])
                return ins

            project(wqkv[:, 0, :], PB)
            project(wqkv[:, 1, :], PA)
            pe.wait_ge(conv_done, 1)
            project(wqkv[:, 2, :], PB)
            pe.wait_ge(conv_done, 2)
            pe.wait_ge(silu_done, 1)
            to_chunks(kT, PA).then_inc(sl_ps, 1)
            pe.wait_ge(conv_done, 3)
            project(wb[:], PB, H)
            pe.wait_ge(beta_fm, 1)
            for n in range(NCH):
                for bh in range(BH):
                    g = BH * n + bh
                    ins = pe.transpose(PB[:, 0, H * g:H * g + H], chunk_tile(betaT, n, bh), ident[0:H, 0:H])
            ins.then_inc(sl_ps, 1)
            pe.wait_ge(beta_done, 1)
            for qhi in range(2):
                part = slice(W64 * qhi, W64 * qhi + W64)
                ins = pe.transpose(PB[0:W64, 1 + qhi, 0:W64], beta_sl[part].rearrange("p h g -> p (h g)"), ident[part, part])
            ins.then_inc(bp_ps, 1)
            pe.wait_ge(sl_done, 1)
            pe.wait_ge(silu_done, 2)
            to_chunks(vT, PA).then_inc(sl_ps, 1)
            pe.wait_ge(vs_done, 1)
            pe.wait_ge(silu_done, 3)
            to_chunks(qT, PA).then_inc(sl_ps, 1)
            pe.wait_ge(sl_done, 2)
            for g in range(NG):
                ins = pe.transpose(PB[:, g // 4, P * (g % 4):P * (g % 4) + P], k_sl[:, g, :], ident[:])
                if g % (NG // 2) == NG // 2 - 1:
                    ins.then_inc(knT_ps, 1)
            pe.wait_ge(knT_done, 2)
            pe.wait_ge(slsq, 2)
            for a, bank in enumerate((PA, PB)):
                for g in range(NG):
                    for q in range(2):
                        for h in range(H):
                            hs = slice(DH * h, DH * h + DH)
                            kc = knT[hs, g // BH, Q4 * (g % BH) + 2 * a + q, :]
                            ins = pe.matmul(bank[C * q:C * q + C, h, C * g:C * g + C], kc, kc, start=True, stop=True)
                ins.then_inc(A_ps, 1)
            pe.wait_ge(A_done, 2)
            a3 = A64[0:W64].rearrange("p a h g s -> p (a h g) s")
            for s in range(C):
                ins = pe.transpose(PA[:, s // 8, W64 * (s % 8):W64 * (s % 8) + W64], a3[:, :, s], ident[0:W64, 0:W64])
            ins.then_inc(Ap_ps, 1)
            for g in range(NG):
                for q in range(Q4):
                    for h in range(H):
                        hs = slice(DH * h, DH * h + DH)
                        b = Q4 * (g % BH) + q
                        ins = pe.matmul(PB[C * q:C * q + C, h, C * g:C * g + C], knT[hs, g // BH, b, :],
                                        qT[hs, g // BH, b, :], start=True, stop=True)
            ins.then_inc(kq_ps, 1)
            pe.wait_ge(Ap_done, 1)
            pe.wait_ge(kq_done, 1)
            for w in range(NW):
                bank = (PA, PB)[w // 16]
                ins = pe.transpose(bank[:, w % 16 // 4, P * (w % 4):P * (w % 4) + P],
                                   vTp[:, w // 4, W64 * (w % 4):W64 * (w % 4) + P], ident[:])
                if w % 16 == 15:
                    ins.then_inc(S["win_ps"], 1)
            pe.wait_ge(S["win_done"], 2)
            for j in range(4):
                pe.wait_ge(T_in[j % 2], 16 * H * (j // 2 + 1))
                for d in range(8):
                    for h in range(H):
                        ins = pe.matmul(PA[C * h:C * h + C, j, W64 * d:W64 * d + W64], vwin[:, :, DH * h + 8 * j + d],
                                        Tf[:, j % 2, h, d, :], start=True, stop=True)
                ins.then_inc(S["fir_ps"], 1)
            pe.wait_ge(S["flw_done"], 4)
            for d in range(DH):
                bank = (PA, PB)[d // 16]
                ins = pe.transpose(bank[0:W64, d % 16 // 4, P * (d % 4):P * (d % 4) + P], flw[:, d, :], ident[:])
                if d % 16 == 15:
                    ins.then_inc(S["fl_ps"], 1)
            pe.wait_ge(G_done, 1)
            pe.wait_ge(S["fl64_done"], 2)
            for c in range(C):
                bank = (PA, PB)[c // 16]
                ins = pe.transpose(bank[0:W64, c % 16 // 4, P * (c % 4):P * (c % 4) + P],
                                   G[:, c].rearrange("p q t -> p (q t)"), ident[:])
                if c % 16 == 15:
                    ins.then_inc(GT_ps, 1)
            pe.wait_ge(GT_done, 2)
            pe.wait_ge(vkb_done, 2)
            for g in range(NG):
                for h in range(H):
                    for q in range(Q4):
                        qs = slice(C * q, C * q + C)
                        ins = pe.matmul(PA[qs, g // 4, P * (g % 4) + DH * h:P * (g % 4) + DH * h + DH],
                                        GT[qs, :, NG * h + g], vb_sl[qs, g, DH * h:DH * h + DH], start=True, stop=True)
            ins.then_inc(uw_ps, 1)
            for g in range(NG):
                for h in range(H):
                    for q in range(Q4):
                        qs = slice(C * q, C * q + C)
                        ins = pe.matmul(PB[DH * h:DH * h + DH, q, C * g:C * g + C], kb_sl[qs, g, DH * h:DH * h + DH],
                                        GT[qs, :, NG * h + g], start=True, stop=True)
            ins.then_inc(uw_ps, 1)
            pe.wait_ge(U_done, 1)
            pe.wait_ge(WT_done, 2)
            pe.wait_ge(AT_done, 1)
            for n in range(NCH):
                if n:
                    pe.wait_ge(S_done, n)
                    for b in range(NB):
                        q, bh = b % Q4, b // Q4
                        ins = pe.matmul(psW[C * q:C * q + C, bh, :], WT[:, n, b, :], Sbd[:, n % 2, b, :], start=True, stop=True)
                    ins.then_inc(w_ps, 1)
                    pe.wait_ge(ut_done, n)
                if n < NCH - 1:
                    for bh in range(BH):
                        for h in range(H):
                            for q in range(Q4):
                                qs = slice(C * q, C * q + C)
                                ins = pe.matmul(psS[DH * h:DH * h + DH, q, bh, :], k_sl[qs, BH * n + bh, DH * h:DH * h + DH],
                                                U[qs, BH * n + bh, DH * h:DH * h + DH], start=True, stop=True)
                    ins.then_inc(dS_ps, 1)
                if n:
                    pe.wait_ge(o_done, n)
                for b in range(NB):
                    q, bh = b % Q4, b // Q4
                    qs = slice(C * q, C * q + C)
                    if n:
                        pe.matmul(psO[qs, bh, :], qT[:, n, b, :], Sbd[:, n % 2, b, :], start=True, stop=False)
                    for h in range(H):
                        hs = slice(DH * h, DH * h + DH)
                        ins = pe.matmul(psO[qs, bh, hs], AT[qs, h, BH * n + bh, :], U[qs, BH * n + bh, hs],
                                        start=(n == 0), stop=(n == 0 or h == H - 1))
                ins.then_inc(o_ps, 1)
            pe.wait_ge(S["fsC_done"], 1)
            pe.wait_ge(S_done, NCH - 1)
            to_chunks(fsC, PA).then_inc(S["fs_ps"], 1)
            pe.wait_ge(S["st_sq"], 5)
            for g in range(NG):
                ins = pe.transpose(PA[:, g // 4, P * (g % 4):P * (g % 4) + P],
                                   stats[:, H * g:H * g + H, :].rearrange("p h k -> p (h k)"), ident[:])
            ins.then_inc(S["st_ps"], 1)
            pe.wait_ge(S["stT_done"], 1)
            pe.wait_ge(o_done, NCH)
            xc = xnT[:].rearrange("p b (n c) -> p n b c", c=C)

            def gate_logits(u):
                h, half = u // 2, u % 2
                pe.wait_ge(S["h1_done"], u + 1)
                for k in range(2):
                    ins = pe.matmul(PB[DH * h:DH * h + DH, 2 * half + k, :], w2p[:], h1[:, u % 2, 512 * k:512 * k + 512],
                                    start=True, stop=True)
                ins.then_inc(S["lg_ps"], 1)

            pe.wait_ge(S["g_in2"], 16 * 13)
            for u in range(2 * H):
                h, half = u // 2, u % 2
                if u >= 2:
                    gate_logits(u - 2)
                for k in range(2):
                    j = 2 * half + k
                    bank = PA[:, 2 * (u % 2) + k, :]
                    pe.matmul(bank, w1x[:], xc[:, 2 * j:2 * j + 2], start=True, stop=False)
                    ins = pe.matmul(bank, w1s[DH * h:DH * h + 16, :], statsT[DH * h:DH * h + 16, 512 * j:512 * j + 512],
                                    start=False, stop=True)
                ins.then_inc(S["h1_ps"], 1)
            gate_logits(2 * H - 2)
            gate_logits(2 * H - 1)
            pe.wait_ge(S["lgT_done"], 1)
            for g in range(NG):
                ins = pe.transpose(PA[:, g // 4, P * (g % 4):P * (g % 4) + P], logT[:, P * g:P * g + P], ident[:])
            ins.then_inc(S["lgs_ps"], 1)
            pe.wait_ge(S["o_done2"], 1)
            for g in range(NG):
                ins = pe.transpose(PA[:, g // 4, P * (g % 4):P * (g % 4) + P], osl[:, g, :], ident[:])
            ins.then_inc(S["oT_ps"], 1)
            pe.wait_ge(S["m_done"], 1)
            pe.matmul(PB[0:NB, 0, 0:NE], small[:, 4, 0:NB], wg[:], start=True, stop=True).then_inc(S["gl_ps"], 1)
            pe.wait_ge(S["gd_done"], 1)
            pe.matmul(PB[:, 0, 0:NB * TOPK], ones[0:NB, :], gwd[:], start=True, stop=True)
            pe.transpose(PB[0:NE, 1, 0:NB], gw[:, 32:40], ident[0:NB, 0:NB]).then_inc(S["gT_ps"], 1)
            pe.wait_ge(S["gT_done"], 1)
            pe.matmul(PB[0:NB, 2, 0:D], gw[:, 56:64], b2e[:], start=True, stop=False)
            pe.matmul(PB[0:NB, 2, 0:D], gw[0:1, 48:56], b2m[:], start=False, stop=True).then_inc(S["bb_ps"], 1)
            pe.wait_ge(S["bb_done"], 1)
            pe.wait_ge(S["oT_done"], 1)

            def expert(b, e):
                return (wm[:] if e == 0 else we[:, e - 1, :])

            for b in range(NB):
                for e in range(3):
                    if e:
                        pe.wait_ge(S["e_scaled"], 2 * b + e)
                    for m in range(2):
                        u = 6 * b + 2 * e + m
                        if u >= 2:
                            pe.wait_ge(S["up_done"], u - 1)
                        for k in (2 * m, 2 * m + 1):
                            ins = pe.matmul(PA[:, u % 2, L * (k % 2):L * (k % 2) + L], expert(b, e)[:, P * k:P * k + P],
                                            xnT[:, b, :], start=True, stop=True)
                        ins.then_inc(S["up_ps"], 1)
                pe.wait_ge(S["up_done"], 6 * b + 6)
                if b >= 2:
                    pe.wait_ge(S["y_done"], b - 1)
                for t in range(2):
                    y = PB[:, 2 + b % 2, D * t:D * t + D]
                    pe.matmul(y, ident[0:NB, b:b + 1].broadcast_to([NB, P]), biasb[:], start=True, stop=False)
                    pe.matmul(y, oT[:, b, P * t:P * t + P], wo[:], start=False, stop=False)
                    for e in range(3):
                        for k in range(NBLK):
                            ins = pe.matmul(y, hT[:, e, k, P * t:P * t + P],
                                            expert(b, e)[:, HID + NBLK + P * k:HID + NBLK + P * k + P],
                                            start=False, stop=(e == 2 and k == NBLK - 1))
                ins.then_inc(S["y_ps"], 1)
            pe_program(pe)


def lay_out(i):
    import numpy as np
    f = lambda n: np.asarray(i["L0_attn_" + n])
    g = lambda n: np.asarray(i["L0_ffn_" + n])
    l = lambda n: np.asarray(i["L1_" + n])
    con = np.ascontiguousarray

    def packed(w1, b, w2):
        return np.concatenate([w1, b.reshape(NBLK, P).T, w2.reshape(NBLK, P, D).transpose(1, 0, 2).reshape(P, HID)], 1)

    return {
        "x": con(f("x").reshape(NT, P, D).transpose(1, 0, 2)),
        "wqkv": con(np.stack([f("Wk"), f("Wv"), f("Wq")], 1)),
        "wb": f("Wb"),
        "cw": con(np.stack([f("conv_k"), f("conv_v"), f("conv_q")], 1)),
        "fsw": con(f("fir_short").reshape(P, FS_TAPS)),
        "frev": con(np.pad(f("fir_long").reshape(P, FL_TAPS), ((0, 0), (FL_TAPS, FL_TAPS)))),
        "w1x": con(f("W1")[0:D]),
        "w1s": con(np.tile(np.pad(f("W1")[D:], ((0, 16), (0, 0))), (H, 1))),
        "b1": con(f("b1")[:, None]),
        "w2": f("W2"),
        "bcst": con(np.tile(np.concatenate([f("base_bias").ravel(), f("b2"), f("log_temp"), f("conv_residual_logit"),
                                            np.zeros(12, np.float32)])[None], (P, 1))),
        "rmsw": con(np.tile(f("rms_w"), H)[:, None]),
        "wo": f("Wo"),
        "wm": con(packed(g("W1m"), g("b1m"), g("W2m"))),
        "experts": con(np.stack([packed(*w) for w in zip(g("W1e"), g("b1e"), g("W2e"))])),
        "wg": g("w_gate"),
        "bgate": con(np.tile(g("b_gate")[None], (NB, 1))),
        "b2e": g("b2e"),
        "b2m": con(g("b2m")[None]),
        "alpha": con(np.tile(g("alpha").reshape(1, 1), (P, 1))),
        "l1_wvT": con(l("attn_Wv").T),
        "l1_woT": con(l("attn_Wo").T),
        "l1_wtT": con(l("ffn_weight").T),
        "l1_bv": con(np.tile(l("attn_bv")[None], (P, 1))),
        "l1_bo": con(np.tile(l("attn_bo")[None], (P, 1))),
    }


def kernel(**inputs):
    import concourse.bacc as _bacc
    from concourse.bass_utils import run_bass_kernel_spmd as _run
    arrays = lay_out(inputs)
    nc = _bacc.Bacc("TRN2", target_bir_lowering=False, num_devices=1)
    inp = {name: nc.dram_tensor("in_" + name, a.shape, mybir.dt.from_np(a.dtype), kind="ExternalInput").ap()
           for name, a in arrays.items()}
    out = nc.dram_tensor("out_0_dram", (NB, L, D), F32, kind="ExternalOutput").ap()
    attention_mix_kernel(nc, inp, out)
    r = _run(nc, [{"in_" + name: a for name, a in arrays.items()}], core_ids=[0])
    return r.results[0]["out_0_dram"]
```

```python
import concourse.bass as bass
from concourse import mybir
from contextlib import ExitStack

import numpy as np

F32 = mybir.dt.float32
BF16 = mybir.dt.bfloat16
U32 = mybir.dt.uint32
ALU = mybir.AluOpType
ACT = mybir.ActivationFunctionType
AX = mybir.AxisListType

P = 128
NB, L, D = 8, 256, 128
T = NB * L
NT = T // P
H, DH = 4, 32
C = 32
NCH = L // C
Q4 = 4
BH = NB // Q4
NG = NCH * BH
TAPS, FS_TAPS, FL_TAPS = 4, 5, 64
W64 = 64
NW = T // W64
EPS = 1e-5
HID = 512
NBLK = HID // P
NE, TOPK = 8, 2
PACK = HID + NBLK + HID
HS, DS = 16, 8
NJ = 4
SLOT = 64
NGRP = 6
ROWS = NGRP * DS
MROWS = 3
ROUND = 1.5 * 2.0 ** 23


def attention_mix_kernel(nc, inp, out):
    ctx = ExitStack()
    with ctx:
        def sb(name, shape, dt=F32):
            return ctx.enter_context(nc.sbuf_tensor(name, shape, dt))

        def sem(name):
            return ctx.enter_context(nc.semaphore(name))

        ps = ctx.enter_context(nc.psum_tensor("ps", [P, 8, 512], F32))
        PA, PB = ps[:, 0:4, :], ps[:, 4:8, :]

        def flat(ap):
            return ap.rearrange("p a b -> p (a b)")

        def bc(ap, axis, n):
            u = ap.unsqueeze(axis)
            shape = list(u.shape)
            shape[axis] = n
            return u.broadcast_to(shape)

        ARENA = 35328
        arena = sb("arena", [P, ARENA])
        used = [0]

        def carve(shape, dt=F32, start=None, layer=1):
            if start is not None:
                used[0] = start
            words = int(np.prod(shape)) // (2 if dt == BF16 else 1)
            if used[0] < 25096 and used[0] + words > 23040 and layer == 2:
                used[0] = 25096
            flat_view = arena[:, used[0]:used[0] + words]
            used[0] += words
            assert used[0] <= ARENA
            if dt == BF16:
                flat_view = flat_view.bitcast(BF16)
            names = "abcdef"[:len(shape)]
            return flat_view.rearrange("p (%s) -> p %s" % (" ".join(names), " ".join(names)), **dict(zip(names, shape)))

        ident = sb("ident", [P, P])
        ones = sb("ones", [P, P])
        tri = sb("tri", [P, C])
        X = sb("X", [P, NT, D])
        xn = X
        sq = carve([NT, D])
        xnT = sb("xnT", [P, NB, L])
        y0 = carve([NB, L])
        y1 = sb("y1", [P, NB, L])
        kT = carve([NCH, NB, C])
        qT = carve([NCH, NB, C])
        vT = carve([NCH, NB, C])
        vTp = carve([NB, W64 + L])
        wqkv = sb("wqkv", [P, 3, D])
        wb = sb("wb", [P, H])
        cw = sb("cw", [P, 3, TAPS])
        fsw = sb("fsw", [P, FS_TAPS])
        small = sb("small", [P, 8, NT * H])
        betaT = y1[0:H].rearrange("p b (n c) -> p (b n c)", c=C).rearrange("p (n b c) -> p n b c", n=NCH, c=C)
        beta_sl = sb("beta_sl", [P, H, NG])
        beta_p = sb("beta_p", [P, W64])
        k_sl = sb("k_sl", [P, NG, D])
        v_sl = carve([NG, D])
        kb_sl = X
        vb_sl = y0[:].rearrange("p b l -> p (b l)").rearrange("p (g d) -> p g d", d=D)
        A64 = carve([2, H, NG, C])
        Ap = carve([C, 2, C])
        G = carve([C, 2, C])
        AT = carve([H, NG, C])
        Sbd = carve([2, NB, P])
        knT = kT
        GT = A64[:, 0].rearrange("p h g c -> p (h g c)").rearrange("p (c x) -> p c x", c=C)
        WT = A64[:, 1].rearrange("p h g c -> p (h g c)").rearrange("p (n b c) -> p n b c", n=NCH, c=C)
        vwin = A64[:].rearrange("p a h g c -> p (a h g c)").rearrange("p (w x) -> p w x", w=NW)
        flw = vT[:].rearrange("p n b c -> p (n b c)").rearrange("p (d o) -> p d o", o=W64)
        U = vT[:].rearrange("p n b c -> p (n b c)").rearrange("p (g d) -> p g d", d=D)
        delta_sl = U
        Tf = carve([2, H, 8, W64])
        fl64 = Tf[0:W64].rearrange("p a h d o -> p (a h d o)").rearrange("p (w x) -> p w x", w=NW)
        fs_sl = carve([NG, D])
        fl_sl = carve([NG, D])
        fsT = y1
        fsC = sq[:].rearrange("p g d -> p (g d)").rearrange("p (n b c) -> p n b c", n=NCH, c=C)
        stats = G[:].rearrange("p c q t -> p (c q t)").rearrange("p (x k) -> p x k", k=32)
        statsT = Ap[:].rearrange("p s q c -> p (s q c)")
        h1 = Tf[:].rearrange("p a h d o -> p (a h d o)").rearrange("p (s x) -> p s x", x=1024)
        logT = kT[:].rearrange("p n b c -> p (n b c)")
        osl = y0[:].rearrange("p b l -> p (b l)").rearrange("p (g d) -> p g d", d=D)
        oT = X[:].rearrange("p g d -> p (g d)").rearrange("p (b l) -> p b l", b=NB)
        x1 = k_sl
        xres = y1[:].rearrange("p b l -> p (b l)").rearrange("p (g d) -> p g d", d=D)
        w1x = sb("w1x", [P, D])
        w1s = sb("w1s", [P, D])
        b1 = sb("b1", [P, 1])
        w2p = sb("w2p", [P, 32])
        bcst = sb("bcst", [P, 64])
        rmsw = sb("rmsw", [P, 1])
        wo = sb("wo", [P, D])
        lg = sb("lg", [P, NG * H, 4])
        gp = sb("gp", [P, 4, NG * H])
        wm = sb("wm", [P, PACK])
        we = sb("we", [P, 2, PACK])
        NWE = 2 * TOPK
        we_more = carve([TOPK, PACK], start=23040)
        hT = sb("hT", [P, 3, NBLK, L])
        tmp = hT[:, 0].rearrange("p k l -> p (k l)")
        gw = sb("gw", [NB, 64])
        idx = sb("idx", [NB, 8], U32)
        gwd = sb("gwd", [NB, NB, TOPK])
        gall = sb("gall", [P, NB * TOPK])
        wg = sb("wg", [P, NE])
        bgate = sb("bgate", [NB, NE])
        iota8 = sb("iota8", [NB, NE])
        b2e = sb("b2e", [NE, D])
        b2m = sb("b2m", [1, D])
        biasb = sb("biasb", [NB, D])
        alph = sb("alph", [P, 4])

        x_in = sem("x_in")
        w_in = sem("w_in")
        consts = sem("consts")
        xsq = sem("xsq")
        xc_done = sem("xc_done")
        lnvar = sem("lnvar")
        lnstd = sem("lnstd")
        xn_done = sem("xn_done")
        xT_ps = sem("xT_ps")
        xnT_done = sem("xnT_done")
        proj_ps = sem("proj_ps")
        tap_done = sem("tap_done")
        conv_done = sem("conv_done")
        silu_done = sem("silu_done")
        sl_ps = sem("sl_ps")
        slsq = sem("slsq")
        ssq = sem("ssq")
        norm = sem("norm")
        sl_done = sem("sl_done")
        beta_fm = sem("beta_fm")
        beta_done = sem("beta_done")
        bp_ps = sem("bp_ps")
        vs_done = sem("vs_done")
        kb_done = sem("kb_done")
        knT_ps = sem("knT_ps")
        knT_done = sem("knT_done")
        A_ps = sem("A_ps")
        A_done = sem("A_done")
        Ap_ps = sem("Ap_ps")
        Ap_done = sem("Ap_done")
        kq_ps = sem("kq_ps")
        kq_done = sem("kq_done")
        AT_done = sem("AT_done")
        vkb_done = sem("vkb_done")
        G_init = sem("G_init")
        G_done = sem("G_done")
        GT_ps = sem("GT_ps")
        GT_done = sem("GT_done")
        uw_ps = sem("uw_ps")
        U_done = sem("U_done")
        WT_done = sem("WT_done")
        w_ps = sem("w_ps")
        ut_done = sem("ut_done")
        dS_ps = sem("dS_ps")
        S_done = sem("S_done")
        o_ps = sem("o_ps")
        o_done = sem("o_done")
        for_names = ("T_in0 T_in1 fs_tap fs_conv fsC_done fs_ps fs_done win_ps win_done fir_ps flw_done fl_ps fl64_done fl_in "
                     "st_sq st_done stz st_ps stT_done h1_ps h1_done lg_ps lgT_done lgs_ps lg_done ex_done mix_sq rms_v rms_s o_done2 "
                     "oT_ps oT_done g_in2 m_done gl_ps gl_done gexp g_ready gb_ps gd_done gT_ps gT_done bb_ps bb_done "
                     "gates e_in0 e_in1 e_in2 e_in3 e_scaled e_used up_ps up_done y_ps y_done xr_in out_done").split()
        S = {name: sem(name) for name in for_names}
        T_in = (S["T_in0"], S["T_in1"])
        e_in = tuple(S["e_in%d" % i] for i in range(NWE))
        dve_chain = sem("dve_chain")
        pool_chain = sem("pool_chain")

        psB = ps[:, 0:2, :]
        psC = ps[:, 2:5, :]
        psOT = ps[:, 5, 0:L]
        psM = ps[:, 6, 0:2 * D]
        psT = ps[:, 7, :]
        psT16 = psT.bitcast(BF16)

        used[0] = 0
        wv1 = sb("l1_wv", [P, D]); bv1 = sb("l1_bv", [P, D]); wo1 = sb("l1_wo", [P, D]); bo1 = sb("l1_bo", [P, D])
        wt = sb("l1_wt", [P, D]); wsc = sb("l1_wsc", [P, 4])
        identb = carve([P], BF16, layer=2)
        sel = carve([NJ, DS + 1], layer=2)
        st6 = carve([2, 6], layer=2); mv = sb("l1_mv", [P, 2, 2])
        nhalf = carve([2], layer=2)
        xn1 = carve([2, 2, D], layer=2)
        xn1T = carve([NB, L], layer=2)
        V1 = carve([5, 2, HS, 32], layer=2)
        res1 = carve([2, 2, HS, DS], layer=2)
        KTM = carve([2, 2, HS, SLOT], BF16, layer=2)
        QTM = carve([2, 2, HS, SLOT], BF16, layer=2)
        KT = carve([3, HS // 2, L], BF16, layer=2)
        QT = carve([3, HS // 2, L], BF16, layer=2)
        mx = carve([2, 2, 2, HS // 2], layer=2)
        mr = carve([2, 2, 2, HS // 2], layer=2)
        mt = carve([2, 2, 2, MROWS, HS // 2], BF16, layer=2)
        mT = carve([2, L], BF16, layer=2)[0:2 * MROWS * HS // 2]
        E1 = carve([8, 2, L], layer=2)
        OT1 = carve([4, L], layer=2)
        rz = carve([2, HS // 2, NJ], layer=2)[0:64]
        O1 = carve([NJ, HS, DS], layer=2)[0:64]
        oT1 = carve([L], layer=2)

        names1 = ("w_in var_done rstd_done w_abs w_sum w_scale w_tern seldone init xn_done x1b xT_ps xT_done P_ps V_done p1 r1 p2 r2 p3 q_done "
                 "tr_ps tr_done B_ps max_done m_split mT_ps mT_done m_in0 m_in1 m_in2 C_ps E_done PV_ps OT_done S1_ps S1_done S2_ps S2_done y_ps y_done "
                 "out_done chain pchain").split()
        Z = {n: sem("l1_" + n) for n in names1}
        m_in = (Z["m_in0"], Z["m_in1"], Z["m_in2"])

        AT_LN, AT_XT, AT_P, AT_SPLIT = -57, -52, -50, (-45, -43, -41)
        AT_TR = (-35, -33, -31, -25)
        AT_B = -24
        AT_M = -5
        AT_S1 = (19, 21)
        AT_S2 = 24
        AT_Y = 26
        LAG = 2
        FIRST, LAST = AT_LN, 16 * (NB - 1) + AT_Y + 4

        def due(s, at):
            b, r = divmod(s - at, 16)
            return b if r == 0 and 0 <= b < NB else None

        def heads_due(s, at):
            b, h = divmod(s - at, 16)
            return (b, h) if 0 <= b < NB else None

        order = {"M": [], "T": []}
        for s in range(FIRST, LAST):
            for name, at in (("xT", AT_XT), ("P", AT_P), ("S2", AT_S2), ("y", AT_Y)):
                b = due(s, at)
                if b is not None:
                    order["M"].append((name, b))
            for name, at in (("TR0", AT_TR[0]), ("TR1", AT_TR[1]), ("TR2", AT_TR[2]), ("TR3", AT_TR[3]), ("mT", AT_M), ("S10", AT_S1[0]), ("S11", AT_S1[1])):
                b = due(s, at)
                if b is not None:
                    order["T"].append((name, b))

        DONE = {"xT": ("xT_done", 1, 1), "P": ("V_done", 1, 1), "S2": ("S2_done", 1, 1), "y": ("y_done", 1, 1),
                "TR0": ("tr_done", 4, 1), "TR1": ("tr_done", 4, 2), "TR2": ("tr_done", 4, 3), "TR3": ("tr_done", 4, 4),
                "mT": ("mT_done", 1, 1), "S10": ("S1_done", 2, 1), "S11": ("S1_done", 2, 2)}

        def before(bank, name, b):
            return order[bank].index((name, b))

        def head_rows(h, n):
            return slice(SLOT * (h % 2), SLOT * (h % 2) + n)

        def parts(tm, b):
            return tm[:, b % 2, :, :, 0:ROWS].rearrange("p t h (g d) -> p (t h) g d", d=DS)

        def P_rows(b):
            return V1[:, b % 5, :, :, 0:DS].rearrange("p t h d -> p (t h) d")

        def rest(i):
            return res1[:, i].rearrange("p t h d -> p (t h) d")

        PIECES = 7
        HEAD_START = 2 * PIECES

        def weave(ffn_piece, prelude, step):
            s = FIRST
            for i in range(PIECES * NB):
                ffn_piece(*divmod(i, PIECES))
                if i == HEAD_START - 1:
                    prelude()
                while i >= HEAD_START and s < FIRST + (i + 1 - HEAD_START) * (-FIRST) // (PIECES * NB - HEAD_START):
                    step(s)
                    s += 1
            for s in range(s, LAST):
                step(s)

        def pe_program(pe, ffn_piece):
            def free(bank, name, b):
                n = before(bank, name, b)
                if n:
                    name, b = order[bank][n - 1]
                    done, per, first = DONE[name]
                    pe.wait_ge(Z[done], per * b + first)

            def prelude():
                pe.wait_ge(Z["w_abs"], 1)
                pe.wait_ge(Z["init"], 2)
                pe.wait_ge(Z["w_in"], 80)
                pe.matmul(psM[:, 0:1], ones[:], wsc[:, 0:1], start=True, stop=True).then_inc(Z["w_sum"], 1)
                pe.wait_ge(Z["w_scale"], 1)

            def step(s):
                b = due(s, AT_XT)
                if b is not None:
                    pe.wait_ge(Z["xn_done"], b + 1)
                    free("M", "xT", b)
                    for t in range(2):
                        ins = pe.transpose(psM[:, P * t:P * t + P], xn1[:, b % 2, t, :], ident[:])
                    ins.then_inc(Z["xT_ps"], 1)
                b = due(s, AT_P)
                if b is not None:
                    pe.wait_ge(Z["xT_done"], b + 1)
                    free("M", "P", b)
                    for t in range(2):
                        ins = pe.matmul(psM[:, P * t:P * t + P], xn1T[:, b, P * t:P * t + P], wv1[:], start=True, stop=True)
                    ins.then_inc(Z["P_ps"], 1)
                for r in range(4):
                    b = due(s, AT_TR[r])
                    if b is not None:
                        pe.wait_ge(Z["q_done"], b + 1)
                        free("T", "TR%d" % r, b)
                        src = (KTM, QTM)[r % 2]
                        for pr in range(4):
                            pair = 4 * (r // 2) + pr
                            for t in range(2):
                                ins = pe.transpose(psT16[:, L * pr + P * t:L * pr + P * t + P],
                                                   src[:, b % 2, t, 2 * pair:2 * pair + 2, :].rearrange("p h s -> p (h s)"), identb[:])
                        ins.then_inc(Z["tr_ps"], 1)
                b = due(s, AT_M)
                if b is not None:
                    pe.wait_ge(Z["m_split"], b + 1)
                    free("T", "mT", b)
                    for t in range(2):
                        ins = pe.transpose(psT16[0:48, P * t:P * t + P],
                                           mt[:, b % 2, t].rearrange("p a k h -> p (a k h)"), identb[:])
                    ins.then_inc(Z["mT_ps"], 1)
                for k in range(2):
                    b = due(s, AT_S1[k])
                    if b is not None:
                        pe.wait_ge(Z["OT_done"], NJ * b + NJ)
                        free("T", "S1%d" % k, b)
                        ot = OT1[:].rearrange("p g q -> p (g q)")
                        for r in range(8):
                            ins = pe.matmul(psT[0:64, 36 * r:36 * r + 36], ot[:, 8 * k + r::16], sel[:].rearrange("p j d -> p (j d)"), start=True, stop=True)
                        ins.then_inc(Z["S1_ps"], 1)
                b = due(s, AT_S2)
                if b is not None:
                    pe.wait_ge(Z["S1_done"], 2 * b + 2)
                    free("M", "S2", b)
                    for j in range(NJ):
                        ins = pe.transpose(psM[:, 64 * j:64 * j + 64], O1[:, j].rearrange("p r d -> p (r d)"), ident[0:64, 0:64])
                    ins.then_inc(Z["S2_ps"], 1)
                b = due(s, AT_Y)
                if b is not None:
                    pe.wait_ge(Z["S2_done"], b + 1)
                    free("M", "y", b)
                    if b == 0:
                        pe.wait_ge(Z["w_tern"], 1)
                    for t in range(2):
                        pe.matmul(psM[:, P * t:P * t + P], oT1[:, P * t:P * t + P], wo1[:], start=True, stop=False)
                        ins = pe.matmul(psM[:, P * t:P * t + P], xn1T[:, b, P * t:P * t + P], wt[:], start=False, stop=True)
                    ins.then_inc(Z["y_ps"], 1)
                bh = heads_due(s, AT_B)
                if bh:
                    b, h = bh
                    u = HS * b + h
                    pe.wait_ge(Z["tr_done"], 4 * b + 2 + 2 * (h // 8))
                    if u >= 2:
                        pe.wait_ge(Z["max_done"], u - 1)
                    rows = head_rows(h, SLOT)
                    for t in range(2):
                        ins = pe.matmul(psB[:, u % 2, L * t:L * t + L], QT[rows, b % 3, h // 2, P * t:P * t + P],
                                        KT[rows, b % 3, h // 2, :], start=True, stop=True)
                    ins.then_inc(Z["B_ps"], 1)
                bh = heads_due(s, 0)
                if bh:
                    b, h = bh
                    u = HS * b + h
                    if h == 0:
                        pe.wait_ge(m_in[b % 3], 32 * (b // 3 + 1))
                    if u == 0:
                        pe.wait_ge(S["y_done"], NB)
                    if u >= 3:
                        pe.wait_ge(Z["E_done"], u - 2)
                    rows = head_rows(h, SLOT)
                    for t in range(2):
                        ins = pe.matmul(psC[:, u % 3, L * t:L * t + L], KT[rows, b % 3, h // 2, P * t:P * t + P],
                                        QT[rows, b % 3, h // 2, :], start=True, stop=True)
                    ins.then_inc(Z["C_ps"], 1)
                for g in range(NJ):
                    b = due(s, 4 * g + 3 + LAG)
                    if b is not None:
                        group = NJ * b + g
                        pe.wait_ge(Z["E_done"], NJ * (group + 1))
                        if group:
                            pe.wait_ge(Z["OT_done"], group)
                        for t in range(2):
                            for jj in range(NJ):
                                ins = pe.matmul(psOT[32 * jj:32 * jj + 32, :], V1[:, b % 5, t, 4 * g + jj, :],
                                                E1[:, (4 * g + jj) % 8, t, :], start=(t == 0), stop=(t == 1))
                        ins.then_inc(Z["PV_ps"], 1)
            weave(ffn_piece, prelude, step)

        def act_program(act, ffn_piece):
            def prelude():
                pass

            def step(s):
                b = due(s, AT_XT)
                if b is not None:
                    act.wait_ge(Z["xT_ps"], b + 1)
                    act.copy(xn1T[:, b, :], psM).then_inc(Z["xT_done"], 1)
                b = due(s, AT_SPLIT[0])
                if b is not None:
                    act.wait_ge(Z["V_done"], b + 1)
                    if b >= 2:
                        act.wait_ge(Z["tr_ps"], 4 * (b - 1))
                    act.copy(parts(KTM, b)[:, :, 0:3, :], P_rows(b).unsqueeze(2).broadcast_to([P, 2 * HS, 3, DS])).then_inc(Z["p1"], 1)
                b = due(s, AT_SPLIT[1])
                if b is not None:
                    act.wait_ge(Z["r1"], b + 1)
                    act.copy(parts(KTM, b)[:, :, 3:5, :], rest(0).unsqueeze(2).broadcast_to([P, 2 * HS, 2, DS])).then_inc(Z["p2"], 1)
                b = due(s, AT_SPLIT[2])
                if b is not None:
                    act.wait_ge(Z["r2"], b + 1)
                    act.copy(parts(KTM, b)[:, :, 5, :], rest(1)).then_inc(Z["p3"], 1)
                for r in (1, 3):
                    b = due(s, AT_TR[r])
                    if b is not None:
                        act.wait_ge(Z["tr_ps"], 4 * b + r + 1)
                        if b >= 3:
                            act.wait_ge(Z["C_ps"], HS * (b - 3) + 8 * (r // 2 + 1))
                        act.copy(QT[:, b % 3, 4 * (r // 2):4 * (r // 2) + 4, :].rearrange("p a q -> p (a q)"), psT16).then_inc(Z["tr_done"], 1)
                for g in range(NJ):
                    b = due(s, 4 * g + 3 + LAG + 1)
                    if b is not None:
                        act.wait_ge(Z["PV_ps"], NJ * b + g + 1)
                        if b:
                            act.wait_ge(Z["S1_ps"], 2 * b)
                        act.copy(OT1[:, g, :], psOT).then_inc(Z["OT_done"], 1)
                b = due(s, AT_S2)
                if b is not None:
                    act.wait_ge(Z["S2_ps"], b + 1)
                    if b:
                        act.wait_ge(Z["y_ps"], b)
                    act.copy(oT1[:].rearrange("p (g j i) -> p j g i", g=4, j=NJ), psM.rearrange("p (j g i) -> p j g i", g=4, j=NJ)).then_inc(Z["S2_done"], 1)
                bh = heads_due(s, 0)
                if bh:
                    b, h = bh
                    u = HS * b + h
                    act.wait_ge(Z["C_ps"], u + 1)
                    if u >= 8:
                        act.wait_ge(Z["PV_ps"], u // 4 - 1)
                    act.activation(E1[:, u % 8].rearrange("p t q -> p (t q)"), psC[:, u % 3, :], ACT.Exp, scale=DS ** -0.5).then_inc(Z["E_done"], 1)
            weave(ffn_piece, prelude, step)

        def dve_program(dve, ffn_piece):
            chain1 = [0]

            def link1(ins):
                chain1[0] += 1
                ins.then_inc(Z["chain"], 1)
                dve.wait_ge(Z["chain"], chain1[0])

            def prelude():
                dve.wait_ge(S["oT_done"], 1)
                link1(dve.memset(KTM, 0.0))
                link1(dve.memset(KTM[:, :, :, :, ROWS:ROWS + MROWS], 1.0))
                link1(dve.memset(QTM, 0.0))
                link1(dve.memset(V1, 0.0))
                dve.memset(V1[:, :, :, :, DS:DS + 1], 1.0).then_inc(Z["init"], 1)
                dve.wait_ge(Z["w_in"], 80)
                dve.tensor_reduce(wsc[:, 0:1], wt[:], axis=AX.X, op=ALU.add, apply_absolute_value=True).then_inc(Z["w_abs"], 1)
                dve.wait_ge(Z["w_sum"], 1)
                link1(dve.tensor_scalar(wsc[:, 1:2], psM[:, 0:1], 1.0 / (D * D), 1e-5, ALU.mult, ALU.max))
                dve.reciprocal(wsc[:, 2:3], wsc[:, 1:2]).then_inc(Z["w_scale"], 1)

            def step(s):
                b = due(s, AT_LN)
                if b is not None:
                    dve.wait_ge(S["y_done"], b + 1)
                    xb = x1[:, 2 * b:2 * b + 2, :]
                    for t in range(2):
                        link1(dve.bn_stats(st6[:, t, :], xb[:, t, :]))
                    for t in range(2):
                        link1(dve.bn_aggr(mv[:, t, :], st6[:, t, :]))
                    dve.tensor_scalar(mv[:, :, 1], mv[:, :, 1], EPS, None, ALU.add).then_inc(Z["var_done"], 1)
                b = due(s, AT_LN + 2)
                if b is not None:
                    xb = x1[:, 2 * b:2 * b + 2, :]
                    dve.wait_ge(Z["rstd_done"], b + 1)
                    if b >= 2:
                        dve.wait_ge(Z["xT_ps"], b - 1)
                    for t in range(2):
                        ins = dve.tensor_scalar(xn1[:, b % 2, t, :], xb[:, t, :], mv[:, t, 0:1], mv[:, t, 1:2], ALU.subtract, ALU.mult)
                    ins.then_inc(Z["xn_done"], 1)
                b = due(s, AT_P)
                if b is not None:
                    dve.wait_ge(Z["P_ps"], b + 1)
                    if b >= 5:
                        dve.wait_ge(Z["PV_ps"], NJ * (b - 4))
                    v = V1[:, b % 5, :, :, 0:DS]
                    for t in range(2):
                        ins = dve.tensor_tensor(v[:, t], psM[:, P * t:P * t + P].rearrange("p (h d) -> p h d", d=DS),
                                            bv1[:].rearrange("p (h d) -> p h d", d=DS), ALU.add)
                    ins.then_inc(Z["V_done"], 1)
                for r in (0, 2):
                    b = due(s, AT_TR[r])
                    if b is not None:
                        dve.wait_ge(Z["tr_ps"], 4 * b + r + 1)
                        if b >= 3:
                            dve.wait_ge(Z["C_ps"], HS * (b - 3) + 8 * (r // 2 + 1))
                        dve.tensor_copy(KT[:, b % 3, 4 * (r // 2):4 * (r // 2) + 4, :].rearrange("p a q -> p (a q)"), psT16).then_inc(Z["tr_done"], 1)
                b = due(s, AT_M)
                if b is not None:
                    dve.wait_ge(Z["mT_ps"], b + 1)
                    if b >= 2:
                        dve.wait_ge(m_in[(b - 2) % 3], 32 * ((b - 2) // 3 + 1))
                    dve.tensor_copy(mT[:, b % 2, :], psT16[0:48, 0:L]).then_inc(Z["mT_done"], 1)
                for k in range(2):
                    b = due(s, AT_S1[k])
                    if b is not None:
                        dve.wait_ge(Z["S1_ps"], 2 * b + k + 1)
                        if b:
                            dve.wait_ge(Z["S2_ps"], b)
                        p = psT[0:64, 0:36 * 8].rearrange("p (r j d) -> p r j d", r=8, j=NJ)
                        link1(dve.reciprocal(rz[:, k], p[:, :, :, DS]))
                        dve.tensor_tensor(O1[:, :, 8 * k:8 * k + 8, :].rearrange("p j r d -> p r j d"), p[:, :, :, 0:DS],
                                          rz[:, k].unsqueeze(3).broadcast_to([64, 8, NJ, DS]), ALU.mult).then_inc(Z["S1_done"], 1)
                b = due(s, AT_Y)
                if b is not None:
                    dve.wait_ge(Z["y_ps"], b + 1)
                    dve.wait_ge(Z["x1b"], b + 1)
                    xb = x1[:, 2 * b:2 * b + 2, :].rearrange("p t d -> p (t d)")
                    dve.tensor_tensor(xb, psM, xb, ALU.add).then_inc(Z["y_done"], 1)
                bh = heads_due(s, AT_B)
                if bh:
                    b, h = bh
                    u = HS * b + h
                    dve.wait_ge(Z["B_ps"], u + 1)
                    if b >= 2 and h == 0:
                        dve.wait_ge(Z["m_split"], b - 1)
                    dve.reduce_max(mx[:, b % 2, :, h % 2, h // 2], psB[:, u % 2, :].rearrange("p (t k) -> p t k", t=2), axis=AX.X).then_inc(Z["max_done"], 1)
                b = due(s, AT_B + 16)
                if b is not None:
                    dve.wait_ge(Z["max_done"], HS * b + 16)
                    if b >= 2:
                        dve.wait_ge(Z["mT_ps"], b - 1)
                    m = mx[:, b % 2].rearrange("p t r a -> p (t r) a")
                    left = mr[:, b % 2].rearrange("p t r a -> p (t r) a")
                    o = mt[:, b % 2].rearrange("p t r k a -> p (t r) k a")
                    link1(dve.tensor_scalar(o[:, :, 0], m, -1.0, None, ALU.mult))
                    link1(dve.scalar_tensor_tensor(out=left, in0=m, scalar=-1.0, in1=o[:, :, 0], op0=ALU.mult, op1=ALU.subtract))
                    link1(dve.tensor_copy(o[:, :, 1], left))
                    link1(dve.tensor_tensor(left, left, o[:, :, 1], ALU.subtract))
                    ins = dve.tensor_copy(o[:, :, 2], left)
                    ins.then_inc(Z["m_split"], 1)
            weave(ffn_piece, prelude, step)

        def pool_program(pool, ffn_piece):
            chain1 = [0]

            def link1(ins):
                chain1[0] += 1
                ins.then_inc(Z["pchain"], 1)
                pool.wait_ge(Z["pchain"], chain1[0])
            def prelude():
                pool.wait_ge(S["oT_done"], 1)
                link1(pool.memset(nhalf[:], -0.5))
                link1(pool.tensor_copy(identb[:], ident[:]))
                link1(pool.tensor_copy(sel[:], ident[:].rearrange("p (j d) -> p j d", j=NJ)[:, :, 0:DS + 1]))
                pool.nop().then_inc(Z["init"], 1)
                pool.wait_ge(Z["w_scale"], 1)
                link1(pool.tensor_scalar(wt[:], wt[:], wsc[:, 2:3], None, ALU.mult))
                link1(pool.tensor_scalar(wt[:], wt[:], 1.0, -1.0, ALU.min, ALU.max))
                link1(pool.tensor_scalar(wt[:], wt[:], ROUND, None, ALU.add))
                link1(pool.tensor_scalar(wt[:], wt[:], ROUND, None, ALU.subtract))
                pool.tensor_scalar(wt[:], wt[:], wsc[:, 1:2], None, ALU.mult).then_inc(Z["w_tern"], 1)

            def step(s):
                b = due(s, AT_LN)
                if b is not None:
                    pool.wait_ge(Z["var_done"], b + 1)
                    pool.tensor_tensor(mv[:, :, 1], mv[:, :, 1], nhalf[:], ALU.pow).then_inc(Z["rstd_done"], 1)
                b = due(s, AT_SPLIT[0])
                if b is not None:
                    k, q = parts(KTM, b), parts(QTM, b)
                    pool.wait_ge(Z["p1"], b + 1)
                    pool.tensor_tensor(rest(0), P_rows(b), k[:, :, 0, :], ALU.subtract).then_inc(Z["r1"], 1)
                    pool.tensor_copy(q[:, :, 0:6:3, :], k[:, :, 0:2, :])
                    pool.wait_ge(Z["p2"], b + 1)
                    pool.tensor_tensor(rest(1), rest(0), k[:, :, 3, :], ALU.subtract).then_inc(Z["r2"], 1)
                    pool.tensor_copy(q[:, :, 5, :], k[:, :, 0, :])
                    pool.tensor_copy(q[:, :, 1:5:3, :], k[:, :, 3:5, :])
                    pool.wait_ge(Z["p3"], b + 1)
                    pool.tensor_copy(q[:, :, 2, :], k[:, :, 5, :]).then_inc(Z["q_done"], 1)
                    pool.wait_ge(Z["xn_done"], b + 1)
                    xb = x1[:, 2 * b:2 * b + 2, :]
                    pool.tensor_tensor(xb, xb, bo1[:].unsqueeze(1).broadcast_to([P, 2, D]), ALU.add).then_inc(Z["x1b"], 1)
            weave(ffn_piece, prelude, step)

        def sp_program(sp):
            for s in range(FIRST, LAST):
                b = due(s, AT_M)
                if b is not None:
                    sp.wait_ge(Z["mT_done"], b + 1)
                    sp.wait_ge(Z["tr_done"], 4 * b + 4)
                    for par in range(2):
                        r0 = SLOT * par + ROWS
                        sp.dma_start(QT[r0:r0 + MROWS, b % 3], mT[24 * par:24 * par + 24, b % 2, :]).then_inc(m_in[b % 3], 16)
                b = due(s, AT_Y)
                if b is not None:
                    sp.wait_ge(Z["y_done"], b + 1)
                    sp.dma_start(out[b].rearrange("(t p) d -> p t d", p=P), x1[:, 2 * b:2 * b + 2, :]).then_inc(Z["out_done"], 16)
            sp.wait_ge(Z["out_done"], 16 * NB)


        block = ctx.enter_context(nc.Block())

        ffn_h, ffn_y = ps[:, 2:4, :], ps[:, 4:6, :]

        def expert(b, e):
            if e == 0:
                return wm[:]
            return (we, we_more)[b % 2][:, e - 1, :]

        KV = {"k": 0, "v": 1, "q": 2}

        def chunk_tile(ap, n, bh):
            return ap[:, n, Q4 * bh:Q4 * bh + Q4, :].rearrange("p q c -> p (q c)")

        psW = ps[:, 4, 0:BH * D].rearrange("p (b x) -> p b x", b=BH)
        psO = ps[:, 5, 0:BH * D].rearrange("p (b x) -> p b x", b=BH)
        psS = ps[:, 0:4, 0:BH * DH].rearrange("p q (b x) -> p q b x", b=BH)

        def chunked(ap):
            return ap.rearrange("p b (n c) -> p b n c", c=C)

        def by_batch(ap):
            return ap.rearrange("p n b c -> p b n c")

        def gt_view(a, r):
            return GT[W64 * a:W64 * a + W64, 16 * r:16 * r + 16, :]

        def gt_ps(bank, a):
            return flat(bank)[0:W64].rearrange("p (c a x) -> p c a x", a=2, x=H * NG)[:, :, a, :]

        def wt_view(q):
            return WT.rearrange("p n (bh q) c -> p n bh q c", q=Q4)[:, :, :, q, :]

        def wt_ps(q):
            return PB[:, q, :].rearrange("p (n b c) -> p n b c", b=BH, c=C)

        def fl64_view(r):
            return fl64.rearrange("p w (h d) -> p w h d", h=H)[:, :, :, 16 * r:16 * r + 16]

        def fl_psv(bank):
            return flat(bank)[0:W64].rearrange("p (d h w) -> p w h d", h=H, w=NW)

        SRC = (fs_sl[:], fl_sl[:], delta_sl, v_sl[:])

        def heads(ap):
            return ap.rearrange("p g (h d) -> p (g h) d", d=DH)

        LB = bcst[:, 0:16].rearrange("p (h k) -> p h k", h=H)

        def act_tail(act):
            act.wait_ge(S["fs_conv"], 1)
            act.copy(fsC.rearrange("p n b c -> p b n c"), chunked(fsT[:])).then_inc(S["fsC_done"], 1)
            act.wait_ge(S["fs_ps"], 1)
            act.copy(fs_sl[:].rearrange("p g d -> p (g d)"), flat(PA)).then_inc(S["fs_done"], 1)
            act.wait_ge(S["fs_done"], 1)
            act.wait_ge(S["fl_in"], 16 * 16)
            act.wait_ge(o_done, NCH)
            for i, src in enumerate(SRC):
                if i:
                    act.wait_ge(S["st_done"], i)
                act.activation(sq[:], src, ACT.Square).then_inc(S["st_sq"], 1)
            act.wait_ge(S["st_done"], 5)
            l2 = stats[:, :, 3:16:4]
            act.activation(l2, l2, ACT.Sqrt).then_inc(S["st_sq"], 1)
            act.wait_ge(S["st_ps"], 1)
            act.copy(statsT, flat(PA)).then_inc(S["stT_done"], 1)
            for u in range(2 * H):
                act.wait_ge(S["h1_ps"], u + 1)
                if u >= 2:
                    act.wait_ge(S["lg_ps"], u - 1)
                act.activation(h1[:, u % 2, :], flat(PA[:, 2 * (u % 2):2 * (u % 2) + 2, :]), ACT.Gelu,
                               bias=b1[:]).then_inc(S["h1_done"], 1)
            act.wait_ge(S["lg_ps"], 2 * H)
            act.copy(logT, flat(PB)).then_inc(S["lgT_done"], 1)
            act.wait_ge(S["lg_done"], 1)
            act.activation(bcst[:, 44:48], bcst[:, 40:44], ACT.Exp, scale=-1.0).then_inc(S["ex_done"], 1)
            act.wait_ge(S["ex_done"], 1)
            act.activation(bcst[:, 44:48], bcst[:, 44:48], ACT.Ln, bias=1.0).then_inc(S["ex_done"], 1)
            act.activation(bcst[:, 48:52], bcst[:, 24:28], ACT.Sigmoid).then_inc(S["ex_done"], 1)
            act.wait_ge(S["lg_done"], 2)
            act.activation(lg[:], lg[:], ACT.Exp).then_inc(S["ex_done"], 1)
            act.wait_ge(S["mix_sq"], 1)
            act.activation(sq[:], osl, ACT.Square).then_inc(S["mix_sq"], 1)
            act.wait_ge(S["rms_v"], 1)
            act.activation(gp[:, 0, :], gp[:, 0, :], ACT.Sqrt, scale=1.0 / DH, bias=small[:, 7, 0:1]).then_inc(S["rms_s"], 1)
            act.wait_ge(S["oT_ps"], 1)
            act.activation(oT.rearrange("p b (n c) -> p n b c", c=C), flat(PA).rearrange("p (n b c) -> p n b c", b=NB, c=C),
                           ACT.Copy, scale=rmsw[:]).then_inc(S["oT_done"], 1)
            act.wait_ge(S["gl_done"], 1)
            act.activation(gw[:, 0:8], gw[:, 0:8], ACT.Exp).then_inc(S["gexp"], 1)
            def hidden(b, piece):
                if piece < 6:
                    e, m = divmod(piece, 2)
                    u = 6 * b + piece
                    act.wait_ge(S["up_ps"], u + 1)
                    if b and piece == 0:
                        act.wait_ge(S["y_ps"], b)
                    for k in (2 * m, 2 * m + 1):
                        ins = act.activation(hT[:, e, k, :], ffn_h[:, u % 2, L * (k % 2):L * (k % 2) + L],
                                             ACT.Gelu_apprx_tanh, bias=expert(b, e)[:, HID + k:HID + k + 1])
                    ins.then_inc(S["up_done"], 1)

            act_program(act, hidden)

        @block.sync
        def _(sp):
            sp.dma_start(X[:], inp["x"]).then_inc(x_in, 16)
            for dst, name in ((w1x[:], "w1x"), (w1s[:], "w1s"), (b1[:], "b1"), (bcst[:, 0:40], "bcst"), (rmsw[:], "rmsw"),
                              (wo[:], "wo"), (wm[:], "wm"), (wg[:], "wg"), (bgate[:], "bgate"), (b2e[:], "b2e"),
                              (b2m[:], "b2m"), (alph[:, 0:1], "alpha")):
                sp.dma_start(dst, inp[name]).then_inc(S["g_in2"], 16)
            for dst, n in ((wv1, "wvT"), (bv1, "bv"), (wo1, "woT"), (bo1, "bo"), (wt, "wtT")):
                sp.dma_start(dst[:], inp["l1_" + n]).then_inc(Z["w_in"], 16)
            sp.wait_ge(S["stz"], 1)
            sp.dma_start(w2p[:, 0:4], inp["w2"]).then_inc(S["g_in2"], 16)
            for j in range(4):
                if j >= 2:
                    sp.wait_ge(S["fir_ps"], j - 1)
                for h in range(H):
                    src = bass.AP(inp["frev"].tensor, (DH * h + 8 * j) * 192, [[1, P], [192, 8], [1, W64]])
                    sp.dma_start(Tf[:, j % 2, h, :, :], src).then_inc(T_in[j % 2], 16)
            sp.wait_ge(S["fl64_done"], 2)
            for q in range(Q4):
                for par in range(2):
                    for bh in range(BH):
                        src = fl64[C * par:C * par + C, 4 * (Q4 * bh + q):4 * (Q4 * bh + q) + 4, :]
                        dst = fl_sl[C * q:C * q + C].rearrange("p (nh par bh) x -> p nh par bh x", par=2, bh=BH)[:, :, par, bh, :]
                        sp.dma_start(dst, src).then_inc(S["fl_in"], 16)
            sp.wait_ge(S["fsC_done"], 1)
            sp.dma_start(xres, inp["x"]).then_inc(S["xr_in"], 16)
            sp.wait_ge(S["g_ready"], 1)
            for i in range(NB * TOPK):
                if i == 2:
                    sp.wait_ge(o_done, NCH)
                if i >= NWE:
                    sp.wait_ge(S["y_ps"], i // TOPK - 1)
                e = sp.value_load(idx[i // TOPK:i // TOPK + 1, i % TOPK:i % TOPK + 1], min_val=0, max_val=NE - 1)
                sp.dma_start(expert(i // TOPK, 1 + i % TOPK), inp["experts"][bass.ds(e, 1), :, :].rearrange("e p x -> p (e x)")).then_inc(e_in[i % NWE], 16)
            sp_program(sp)

        @block.gpsimd
        def _(pool):
            chain = [0]

            def link(ins):
                chain[0] += 1
                ins.then_inc(pool_chain, 1)
                pool.wait_ge(pool_chain, chain[0])

            link(pool.memset(ident[:], 0.0))
            pool.affine_select(out=ident[:], in_=ident[:], compare_op=ALU.not_equal, fill=1.0, base=0,
                               pattern=[[-1, P]], channel_multiplier=1).then_inc(consts, 1)
            link(pool.memset(tri[:], 1.0))
            for q in range(Q4):
                link(pool.affine_select(out=tri[C * q:C * q + C, :], in_=tri[C * q:C * q + C, :],
                                        compare_op=ALU.is_ge, fill=0.0, base=0,
                                        pattern=[[1, C]], channel_multiplier=-1))
            pool.memset(ones[:], 1.0).then_inc(consts, 1)
            link(pool.memset(w2p[:], 0.0))
            pool.iota(iota8[:], [[1, NE]], base=0, channel_multiplier=0, allow_small_or_imprecise_dtypes=True).then_inc(S["stz"], 1)
            link(pool.memset(G[:], 0.0))
            pool.affine_select(out=G[:], in_=G[:], compare_op=ALU.not_equal, fill=1.0, base=0,
                               pattern=[[1, C], [0, 2], [-1, C]], channel_multiplier=0).then_inc(G_init, 1)
            pool.wait_ge(beta_done, 1)
            pool.wait_ge(silu_done, 3)
            for src, dst, ready in ((v_sl, vb_sl, vs_done), (k_sl, kb_sl, sl_done)):
                pool.wait_ge(ready, 1)
                pool.tensor_tensor(dst[:].rearrange("p g (h d) -> p g h d", h=H),
                                   src[:].rearrange("p g (h d) -> p g h d", h=H),
                                   bc(beta_sl[:].rearrange("p h g -> p g h"), 3, DH), ALU.mult).then_inc(vkb_done, 1)
            pool.wait_ge(kq_done, 1)
            at3 = AT[:].rearrange("p h g c -> p (h g) c")
            pool.tensor_tensor(at3, at3, bc(tri[:], 1, H * NG), ALU.mult).then_inc(AT_done, 1)
            pool.wait_ge(GT_ps, 2)
            pool.memset(stats, 0.0).then_inc(S["stz"], 1)
            pool.wait_ge(S["gates"], 1)
            def scale_expert(i):
                if i < NB * TOPK:
                    pool.wait_ge(e_in[i % NWE], 16 * (i // NWE + 1))
                    w2 = expert(i // TOPK, 1 + i % TOPK)[:, HID + NBLK:]
                    pool.tensor_scalar(w2, w2, gall[:, i:i + 1], None, ALU.mult).then_inc(S["e_scaled"], 1)

            def scale_next(b, piece):
                if piece in (2, 4):
                    scale_expert(TOPK * (b + 1) + piece // 2 - 1)

            scale_expert(0)
            scale_expert(1)
            pool_program(pool, scale_next)

        @block.scalar
        def _(act):
            act.dma_start(wqkv[:], inp["wqkv"]).then_inc(w_in, 16)
            act.dma_start(wb[:], inp["wb"]).then_inc(w_in, 16)
            act.dma_start(cw[:], inp["cw"]).then_inc(w_in, 16)
            act.dma_start(fsw[:], inp["fsw"]).then_inc(w_in, 16)
            act.wait_ge(xc_done, 1)
            act.activation(sq[:], xn[:], ACT.Square).then_inc(xsq, 1)
            act.wait_ge(lnvar, 1)
            act.activation(small[:, 1, 0:NT], small[:, 1, 0:NT], ACT.Sqrt, scale=1.0 / D,
                           bias=small[:, 7, 0:1]).then_inc(lnstd, 1)
            for i in (2, 3):
                act.wait_ge(xT_ps, i + 1)
                act.copy(xnT[:, 2 * i:2 * i + 2, :], PA[:, i, :]).then_inc(xnT_done, 1)
            act.wait_ge(w_in, 64)

            def newest_tap(i, y, bank):
                act.wait_ge(proj_ps, i + 1)
                act.activation(y[:].rearrange("p b l -> p (b l)"), flat(bank), ACT.Copy,
                               scale=cw[:, i, TAPS - 1:TAPS]).then_inc(tap_done, 1)

            newest_tap(0, y0, PB)
            newest_tap(1, y1, PA)
            act.wait_ge(conv_done, 1)
            act.activation(by_batch(kT[:]), chunked(y0[:]), ACT.Silu).then_inc(silu_done, 1)
            act.wait_ge(silu_done, 1)
            newest_tap(2, y0, PB)
            act.wait_ge(conv_done, 2)
            act.activation(by_batch(vT[:]), chunked(y1[:]), ACT.Silu)
            act.activation(vTp[:, :, W64:], y1[:], ACT.Silu).then_inc(silu_done, 1)
            act.wait_ge(conv_done, 3)
            act.activation(by_batch(qT[:]), chunked(y0[:]), ACT.Silu).then_inc(silu_done, 1)
            act.wait_ge(sl_ps, 1)
            act.activation(sq[:].rearrange("p a b -> p (a b)"), flat(PA), ACT.Square).then_inc(slsq, 1)
            act.wait_ge(ssq, 1)
            act.activation(small[:, 2, :], small[:, 2, :], ACT.Sqrt, bias=small[:, 7, 1:2]).then_inc(norm, 1)
            act.wait_ge(proj_ps, 4)
            act.activation(by_batch(betaT), flat(PB)[0:H].rearrange("p (b n c) -> p b n c", n=NCH, c=C),
                           ACT.Sigmoid).then_inc(beta_fm, 1)
            act.wait_ge(sl_ps, 3)
            act.copy(v_sl[:].rearrange("p a b -> p (a b)"), flat(PA)).then_inc(vs_done, 1)
            act.wait_ge(sl_ps, 4)
            act.activation(sq[:].rearrange("p a b -> p (a b)"), flat(PA), ACT.Square).then_inc(slsq, 1)
            act.wait_ge(ssq, 2)
            act.activation(small[:, 3, :], small[:, 3, :], ACT.Sqrt, bias=small[:, 7, 1:2]).then_inc(norm, 1)
            act.wait_ge(knT_ps, 2)
            act.copy(knT[:, NCH // 2:].rearrange("p n b c -> p (n b c)"), flat(PB[:, 2:4, :])).then_inc(knT_done, 1)
            act.wait_ge(A_ps, 2)
            act.copy(A64[0:W64, 1].rearrange("p h g c -> p (h g c)"), flat(PB)[0:W64]).then_inc(A_done, 1)
            act.wait_ge(sl_ps, 2)
            act.activation(fsT[:], vTp[:, :, W64:], ACT.Copy, scale=fsw[:, FS_TAPS - 1:FS_TAPS]).then_inc(S["fs_tap"], 1)
            act.wait_ge(kq_ps, 1)
            act.copy(AT[:].rearrange("p h g c -> p (h g c)"), flat(PB)).then_inc(kq_done, 1)
            act.wait_ge(S["win_ps"], 2)
            act.copy(vwin[:, NW // 2:, :].rearrange("p w x -> p (w x)"), flat(PB)).then_inc(S["win_done"], 1)
            for j in range(4):
                act.wait_ge(S["fir_ps"], j + 1)
                act.copy(flw[:, 8 * j:8 * j + 8, :],
                         PA[:, j, :].rearrange("p (d o) -> p d o", o=W64)[:, :, ::-1]).then_inc(S["flw_done"], 1)
            act.wait_ge(S["fl_ps"], 2)
            act.copy(fl64_view(1), fl_psv(PB)).then_inc(S["fl64_done"], 1)
            act.wait_ge(GT_ps, 2)
            for a in range(2):
                ins = act.copy(gt_view(a, 1), gt_ps(PB, a))
            ins.then_inc(GT_done, 1)
            act.wait_ge(uw_ps, 1)
            act.copy(U.rearrange("p g d -> p (g d)"), flat(PA)).then_inc(U_done, 1)
            act.wait_ge(uw_ps, 2)
            for q in (2, 3):
                ins = act.copy(wt_view(q), wt_ps(q))
            ins.then_inc(WT_done, 1)
            act_tail(act)

        @block.vector
        def _(dve):
            chain = [0]

            def link(ins):
                chain[0] += 1
                ins.then_inc(dve_chain, 1)
                dve.wait_ge(dve_chain, chain[0])

            dve.memset(small[:, 7, 0:1], EPS)
            dve.memset(small[:, 7, 1:2], 1e-6)
            dve.memset(vTp[:, :, 0:W64], 0.0)
            link(dve.memset(Sbd[:], 0.0))
            dve.wait_ge(x_in, 16)
            link(dve.reduce_sum(small[:, 0, 0:NT], X[:], axis=AX.X))
            link(dve.tensor_scalar(small[:, 0, 0:NT], small[:, 0, 0:NT], 1.0 / D, None, ALU.mult))
            dve.tensor_tensor(xn[:], X[:], bc(small[:, 0, 0:NT], 2, D), ALU.subtract).then_inc(xc_done, 1)
            dve.wait_ge(xsq, 1)
            dve.reduce_sum(small[:, 1, 0:NT], sq[:], axis=AX.X).then_inc(lnvar, 1)
            dve.wait_ge(lnstd, 1)
            link(dve.reciprocal(small[:, 1, 0:NT], small[:, 1, 0:NT]))
            dve.tensor_tensor(xn[:], xn[:], bc(small[:, 1, 0:NT], 2, D), ALU.mult).then_inc(xn_done, 1)
            for i in (0, 1):
                dve.wait_ge(xT_ps, i + 1)
                dve.tensor_copy(xnT[:, 2 * i:2 * i + 2, :], PA[:, i, :]).then_inc(xnT_done, 1)
            for i, (y, bank) in enumerate(((y0, PB), (y1, PA), (y0, PB))):
                dve.wait_ge(tap_done, i + 1)
                p3 = flat(bank).rearrange("p (b l) -> p b l", b=NB)
                for s in range(1, TAPS):
                    ins = dve.scalar_tensor_tensor(out=y[:, :, s:], in0=p3[:, :, 0:L - s],
                                                   scalar=cw[:, i, TAPS - 1 - s:TAPS - s], in1=y[:, :, s:],
                                                   op0=ALU.mult, op1=ALU.add)
                    if s < TAPS - 1:
                        link(ins)
                ins.then_inc(conv_done, 1)
            dve.wait_ge(slsq, 1)
            dve.reduce_sum(small[:, 2, :], sq[:].rearrange("p g (h d) -> p (g h) d", d=DH), axis=AX.X).then_inc(ssq, 1)
            dve.wait_ge(norm, 1)
            link(dve.reciprocal(small[:, 2, :], small[:, 2, :]))
            dve.tensor_tensor(k_sl[:].rearrange("p g (h d) -> p (g h) d", d=DH),
                              flat(PA).rearrange("p (g d) -> p g d", d=DH),
                              bc(small[:, 2, :], 2, DH), ALU.mult).then_inc(sl_done, 1)
            dve.wait_ge(sl_ps, 2)
            dve.tensor_copy(beta_sl[:].rearrange("p h g -> p g h"),
                            PB[:, 0, 0:NG * H].rearrange("p (g h) -> p g h", h=H)).then_inc(beta_done, 1)
            dve.wait_ge(bp_ps, 1)
            for qhi in range(2):
                ins = dve.tensor_copy(beta_p[W64 * qhi:W64 * qhi + W64, :], PB[0:W64, 1 + qhi, 0:W64])
            ins.then_inc(sl_done, 1)
            dve.wait_ge(slsq, 2)
            dve.reduce_sum(small[:, 3, :], sq[:].rearrange("p g (h d) -> p (g h) d", d=DH), axis=AX.X).then_inc(ssq, 1)
            dve.wait_ge(norm, 2)
            link(dve.reciprocal(small[:, 3, :], small[:, 3, :]))
            dve.wait_ge(knT_ps, 1)
            dve.tensor_copy(knT[:, 0:NCH // 2].rearrange("p n b c -> p (n b c)"), flat(PB[:, 0:2, :])).then_inc(knT_done, 1)
            dve.wait_ge(A_ps, 1)
            dve.tensor_copy(A64[0:W64, 0].rearrange("p h g c -> p (h g c)"), flat(PA)[0:W64]).then_inc(A_done, 1)
            dve.wait_ge(Ap_ps, 1)
            dve.tensor_tensor(Ap[:].rearrange("p s q c -> p s (q c)"), flat(PA).rearrange("p (s x) -> p s x", s=C),
                              bc(beta_p[:], 1, C), ALU.mult).then_inc(Ap_done, 1)
            dve.wait_ge(Ap_done, 1)
            dve.wait_ge(G_init, 1)
            for s in range(C - 1):
                m, w = C - 1 - s, s + 1
                t = tmp[:, 0:m * 2 * w].rearrange("p (c q t) -> p c q t", q=2, t=w)
                link(dve.tensor_tensor(t, bc(Ap[:, s, :, w:].rearrange("p q c -> p c q"), 3, w),
                                       bc(G[:, s, :, 0:w], 1, m), ALU.mult))
                ins = dve.tensor_tensor(G[:, w:, :, 0:w], G[:, w:, :, 0:w], t, ALU.subtract)
                if s < C - 2:
                    link(ins)
            ins.then_inc(G_done, 1)
            dve.wait_ge(S["win_ps"], 1)
            dve.tensor_copy(vwin[:, 0:NW // 2, :].rearrange("p w x -> p (w x)"), flat(PA)).then_inc(S["win_done"], 1)
            dve.wait_ge(S["fl_ps"], 1)
            dve.tensor_copy(fl64_view(0), fl_psv(PA)).then_inc(S["fl64_done"], 1)
            dve.wait_ge(GT_ps, 1)
            for a in range(2):
                ins = dve.tensor_copy(gt_view(a, 0), gt_ps(PA, a))
            ins.then_inc(GT_done, 1)
            dve.wait_ge(S["fs_tap"], 1)
            for t in range(1, FS_TAPS):
                ins = dve.scalar_tensor_tensor(out=fsT[:], in0=vTp[:, :, W64 - t:W64 - t + L],
                                               scalar=fsw[:, FS_TAPS - 1 - t:FS_TAPS - t], in1=fsT[:],
                                               op0=ALU.mult, op1=ALU.add)
                if t < FS_TAPS - 1:
                    link(ins)
            ins.then_inc(S["fs_conv"], 1)
            dve.wait_ge(uw_ps, 2)
            for q in (0, 1):
                ins = dve.tensor_copy(wt_view(q), wt_ps(q))
            ins.then_inc(WT_done, 1)
            for n in range(NCH):
                gs = slice(BH * n, BH * n + BH)
                if n:
                    dve.wait_ge(w_ps, n)
                    dve.tensor_tensor(U[:, gs, :], U[:, gs, :], psW, ALU.subtract).then_inc(ut_done, 1)
                if n < NCH - 1:
                    dve.wait_ge(dS_ps, n + 1)
                    for h in range(H):
                        hs = slice(DH * h, DH * h + DH)
                        old, new = (Sbd[hs, i % 2].rearrange("p (bh q) x -> p q bh x", q=Q4)[:, :, :, hs]
                                    for i in (n, n + 1))
                        if n:
                            ins = dve.tensor_tensor(new, old, psS[hs], ALU.add)
                        else:
                            ins = dve.tensor_copy(new, psS[hs])
                    ins.then_inc(S_done, 1)
                dve.wait_ge(o_ps, n + 1)
                dve.tensor_tensor(delta_sl[:, gs, :].rearrange("p g (h d) -> p (g h) d", d=DH),
                                  psO.rearrange("p g (h d) -> p (g h) d", d=DH),
                                  bc(small[:, 3, BH * H * n:BH * H * (n + 1)], 2, DH), ALU.mult).then_inc(o_done, 1)

            dve.wait_ge(S["stz"], 2)
            dve.wait_ge(S["fl_in"], 16 * 16)
            dve.wait_ge(S["fs_done"], 1)
            for i, src in enumerate(SRC):
                dve.reduce_sum(stats[:, :, 4 * i], heads(src), axis=AX.X)
                dve.tensor_reduce(stats[:, :, 4 * i + 2], heads(src), axis=AX.X, op=ALU.add, apply_absolute_value=True)
                dve.wait_ge(S["st_sq"], i + 1)
                dve.reduce_sum(stats[:, :, 4 * i + 3], heads(sq[:]), axis=AX.X).then_inc(S["st_done"], 1)
            dve.wait_ge(S["st_done"], 4)
            link(dve.tensor_scalar(stats[:, :, 0:16:2], stats[:, :, 0:16:2], 1.0 / DH, None, ALU.mult))
            mean, var, l2 = (stats[:, :, k:16:4] for k in (0, 1, 3))
            link(dve.tensor_tensor(var, mean, mean, ALU.mult))
            dve.scalar_tensor_tensor(out=var, in0=l2, scalar=1.0 / DH, in1=var, op0=ALU.mult,
                                     op1=ALU.subtract).then_inc(S["st_done"], 1)
            dve.wait_ge(S["g_in2"], 16 * 13)
            link(dve.tensor_tensor(LB, LB, bc(bcst[:, 16:20], 1, H), ALU.add))
            link(dve.scalar_tensor_tensor(out=bcst[:, 40:44], in0=bcst[:, 20:24], scalar=-1.0, in1=bcst[:, 20:24],
                                          op0=ALU.mult, op1=ALU.max))
            dve.wait_ge(S["lgs_ps"], 1)
            lps = flat(PA).rearrange("p (g h k) -> p g h k", h=H, k=32)[:, :, :, 0:4]
            lg4 = lg[:].rearrange("p (g h) k -> p g h k", h=H)
            dve.tensor_tensor(lg4, lps, bc(LB, 1, NG), ALU.add).then_inc(S["lg_done"], 1)
            dve.wait_ge(S["ex_done"], 3)
            link(dve.scalar_tensor_tensor(out=bcst[:, 44:48], in0=bcst[:, 20:24], scalar=0.0, in1=bcst[:, 44:48],
                                          op0=ALU.max, op1=ALU.add))
            link(dve.tensor_scalar(bcst[:, 44:48], bcst[:, 44:48], 1e-4, None, ALU.add))
            link(dve.reciprocal(bcst[:, 44:48], bcst[:, 44:48]))
            link(dve.tensor_tensor(lg4, lg4, bc(bc(bcst[:, 44:48], 1, NG), 3, 4), ALU.mult))
            link(dve.reduce_max(gp[:, 0, :], lg[:], axis=AX.X))
            dve.tensor_tensor(lg[:], lg[:], bc(gp[:, 0, :], 2, 4), ALU.subtract).then_inc(S["lg_done"], 1)
            dve.wait_ge(S["ex_done"], 4)
            for last in range(2):
                link(dve.reduce_sum(gp[:, 1, :], lg[:], axis=AX.X))
                link(dve.reciprocal(gp[:, 1, :], gp[:, 1, :]))
                link(dve.tensor_tensor(lg[:], lg[:], bc(gp[:, 1, :], 2, 4), ALU.mult))
                if not last:
                    link(dve.tensor_scalar(lg[:, :, 0:2], lg[:, :, 0:2], 0.05, None, ALU.max))
            p0 = lg4[:, :, :, 0]
            link(dve.scalar_tensor_tensor(out=p0, in0=bc(bcst[:, 48:52], 1, NG), scalar=0.5, in1=p0, op0=ALU.mult, op1=ALU.add))
            link(dve.tensor_tensor(heads(osl), heads(SRC[0]), bc(lg[:, :, 0], 2, DH), ALU.mult))
            for i in range(1, 4):
                link(dve.tensor_tensor(heads(sq[:]), heads(SRC[i]), bc(lg[:, :, i], 2, DH), ALU.mult))
                ins = dve.tensor_tensor(osl, osl, sq[:], ALU.add)
                if i < 3:
                    link(ins)
            ins.then_inc(S["mix_sq"], 1)
            dve.wait_ge(S["mix_sq"], 2)
            dve.reduce_sum(gp[:, 0, :], heads(sq[:]), axis=AX.X).then_inc(S["rms_v"], 1)
            dve.wait_ge(S["rms_s"], 1)
            link(dve.reciprocal(gp[:, 0, :], gp[:, 0, :]))
            dve.tensor_tensor(heads(osl), heads(osl), bc(gp[:, 0, :], 2, DH), ALU.mult).then_inc(S["o_done2"], 1)
            dve.wait_ge(xnT_done, 4)
            dve.reduce_sum(small[:, 4, 0:NB], xnT[:], axis=AX.X).then_inc(S["m_done"], 1)
            dve.wait_ge(S["gl_ps"], 1)
            link(dve.scalar_tensor_tensor(out=gw[:, 0:8], in0=PB[0:NB, 0, 0:NE], scalar=1.0 / L, in1=bgate[:],
                                          op0=ALU.mult, op1=ALU.add))
            link(dve.reduce_max(gw[:, 8:9], gw[:, 0:8], axis=AX.X))
            dve.tensor_scalar(gw[:, 0:8], gw[:, 0:8], gw[:, 8:9], None, ALU.subtract).then_inc(S["gl_done"], 1)
            dve.wait_ge(S["gexp"], 1)
            link(dve.reduce_sum(gw[:, 8:9], gw[:, 0:8], axis=AX.X))
            link(dve.reciprocal(gw[:, 8:9], gw[:, 8:9]))
            link(dve.tensor_scalar(gw[:, 0:8], gw[:, 0:8], gw[:, 8:9], None, ALU.mult))
            link(dve.max(gw[:, 16:24], gw[:, 0:8]))
            dve.max_index(idx[:], gw[:, 16:24], gw[:, 0:8]).then_inc(S["g_ready"], 1)
            dve.wait_ge(S["g_ready"], 1)
            link(dve.reduce_sum(gw[:, 8:9], gw[:, 16:18], axis=AX.X))
            link(dve.reciprocal(gw[:, 8:9], gw[:, 8:9]))
            link(dve.tensor_scalar(alph[:, 1:2], alph[:, 0:1], 0.1, 1.0, ALU.max, ALU.min))
            link(dve.tensor_scalar(alph[:, 2:3], alph[:, 1:2], -1.0, 1.0, ALU.mult, ALU.add))
            link(dve.tensor_scalar(gw[:, 24:26], gw[:, 16:18], gw[:, 8:9], alph[0:NB, 2:3], ALU.mult, ALU.mult))
            link(dve.tensor_copy(gw[:, 26:28], idx[:, 0:2]))
            link(dve.tensor_scalar(gw[:, 32:40], iota8[:], gw[:, 26:27], gw[:, 24:25], ALU.is_equal, ALU.mult))
            link(dve.tensor_scalar(gw[:, 40:48], iota8[:], gw[:, 27:28], gw[:, 25:26], ALU.is_equal, ALU.mult))
            link(dve.tensor_tensor(gw[:, 32:40], gw[:, 32:40], gw[:, 40:48], ALU.add))
            link(dve.tensor_copy(gw[0:1, 48:56], alph[0:1, 1:2].broadcast_to([1, NB])))
            w2 = wm[:, HID + NBLK:]
            link(dve.tensor_scalar(w2, w2, alph[:, 1:2], None, ALU.mult))
            dve.tensor_tensor(gwd[:], bc(ident[0:NB, 0:NB], 2, TOPK), bc(gw[:, 24:26], 1, NB), ALU.mult).then_inc(S["gd_done"], 1)
            dve.wait_ge(S["gT_ps"], 1)
            dve.tensor_copy(gall[:], PB[:, 0, 0:NB * TOPK]).then_inc(S["gates"], 1)
            dve.tensor_copy(gw[:, 56:64], PB[0:NE, 1, 0:NB]).then_inc(S["gT_done"], 1)
            dve.wait_ge(S["bb_ps"], 1)
            dve.tensor_copy(biasb[:], PB[0:NB, 2, 0:D]).then_inc(S["bb_done"], 1)
            def residual(b, piece):
                if piece == 6:
                    dve.wait_ge(S["y_ps"], b + 1)
                    if b == 0:
                        dve.wait_ge(S["xr_in"], 16)
                    dve.tensor_tensor(x1[:, 2 * b:2 * b + 2, :], ffn_y[:, b % 2, 0:2 * D].rearrange("p (t d) -> p t d", d=D),
                                      xres[:, 2 * b:2 * b + 2, :], ALU.add).then_inc(S["y_done"], 1)

            dve_program(dve, residual)

        @block.tensor
        def _(pe):
            pe.wait_ge(consts, 2)
            pe.wait_ge(xn_done, 1)
            for i in range(NT):
                ins = pe.transpose(PA[:, i // 4, P * (i % 4):P * (i % 4) + P], xn[:, i, :], ident[:])
                if i % 4 == 3:
                    ins.then_inc(xT_ps, 1)
            pe.wait_ge(w_in, 64)
            pe.wait_ge(xnT_done, 4)

            def project(w, bank, m=P):
                for j in range(4):
                    ins = pe.matmul(bank[0:m, j, :], w, xnT[:, 2 * j:2 * j + 2, :], start=True, stop=True)
                ins.then_inc(proj_ps, 1)

            def to_chunks(src, bank):
                for n in range(NCH):
                    for bh in range(BH):
                        g = BH * n + bh
                        ins = pe.transpose(bank[:, g // 4, P * (g % 4):P * (g % 4) + P], chunk_tile(src, n, bh), ident[:])
                return ins

            project(wqkv[:, 0, :], PB)
            project(wqkv[:, 1, :], PA)
            pe.wait_ge(conv_done, 1)
            project(wqkv[:, 2, :], PB)
            pe.wait_ge(conv_done, 2)
            pe.wait_ge(silu_done, 1)
            to_chunks(kT, PA).then_inc(sl_ps, 1)
            pe.wait_ge(conv_done, 3)
            project(wb[:], PB, H)
            pe.wait_ge(beta_fm, 1)
            for n in range(NCH):
                for bh in range(BH):
                    g = BH * n + bh
                    ins = pe.transpose(PB[:, 0, H * g:H * g + H], chunk_tile(betaT, n, bh), ident[0:H, 0:H])
            ins.then_inc(sl_ps, 1)
            pe.wait_ge(beta_done, 1)
            for qhi in range(2):
                part = slice(W64 * qhi, W64 * qhi + W64)
                ins = pe.transpose(PB[0:W64, 1 + qhi, 0:W64], beta_sl[part].rearrange("p h g -> p (h g)"), ident[part, part])
            ins.then_inc(bp_ps, 1)
            pe.wait_ge(sl_done, 1)
            pe.wait_ge(silu_done, 2)
            to_chunks(vT, PA).then_inc(sl_ps, 1)
            pe.wait_ge(vs_done, 1)
            pe.wait_ge(silu_done, 3)
            to_chunks(qT, PA).then_inc(sl_ps, 1)
            pe.wait_ge(sl_done, 2)
            for g in range(NG):
                ins = pe.transpose(PB[:, g // 4, P * (g % 4):P * (g % 4) + P], k_sl[:, g, :], ident[:])
                if g % (NG // 2) == NG // 2 - 1:
                    ins.then_inc(knT_ps, 1)
            pe.wait_ge(knT_done, 2)
            pe.wait_ge(slsq, 2)
            for a, bank in enumerate((PA, PB)):
                for g in range(NG):
                    for q in range(2):
                        for h in range(H):
                            hs = slice(DH * h, DH * h + DH)
                            kc = knT[hs, g // BH, Q4 * (g % BH) + 2 * a + q, :]
                            ins = pe.matmul(bank[C * q:C * q + C, h, C * g:C * g + C], kc, kc, start=True, stop=True)
                ins.then_inc(A_ps, 1)
            pe.wait_ge(A_done, 2)
            a3 = A64[0:W64].rearrange("p a h g s -> p (a h g) s")
            for s in range(C):
                ins = pe.transpose(PA[:, s // 8, W64 * (s % 8):W64 * (s % 8) + W64], a3[:, :, s], ident[0:W64, 0:W64])
            ins.then_inc(Ap_ps, 1)
            for g in range(NG):
                for q in range(Q4):
                    for h in range(H):
                        hs = slice(DH * h, DH * h + DH)
                        b = Q4 * (g % BH) + q
                        ins = pe.matmul(PB[C * q:C * q + C, h, C * g:C * g + C], knT[hs, g // BH, b, :],
                                        qT[hs, g // BH, b, :], start=True, stop=True)
            ins.then_inc(kq_ps, 1)
            pe.wait_ge(Ap_done, 1)
            pe.wait_ge(kq_done, 1)
            for w in range(NW):
                bank = (PA, PB)[w // 16]
                ins = pe.transpose(bank[:, w % 16 // 4, P * (w % 4):P * (w % 4) + P],
                                   vTp[:, w // 4, W64 * (w % 4):W64 * (w % 4) + P], ident[:])
                if w % 16 == 15:
                    ins.then_inc(S["win_ps"], 1)
            pe.wait_ge(S["win_done"], 2)
            for j in range(4):
                pe.wait_ge(T_in[j % 2], 16 * H * (j // 2 + 1))
                for d in range(8):
                    for h in range(H):
                        ins = pe.matmul(PA[C * h:C * h + C, j, W64 * d:W64 * d + W64], vwin[:, :, DH * h + 8 * j + d],
                                        Tf[:, j % 2, h, d, :], start=True, stop=True)
                ins.then_inc(S["fir_ps"], 1)
            pe.wait_ge(S["flw_done"], 4)
            for d in range(DH):
                bank = (PA, PB)[d // 16]
                ins = pe.transpose(bank[0:W64, d % 16 // 4, P * (d % 4):P * (d % 4) + P], flw[:, d, :], ident[:])
                if d % 16 == 15:
                    ins.then_inc(S["fl_ps"], 1)
            pe.wait_ge(G_done, 1)
            pe.wait_ge(S["fl64_done"], 2)
            for c in range(C):
                bank = (PA, PB)[c // 16]
                ins = pe.transpose(bank[0:W64, c % 16 // 4, P * (c % 4):P * (c % 4) + P],
                                   G[:, c].rearrange("p q t -> p (q t)"), ident[:])
                if c % 16 == 15:
                    ins.then_inc(GT_ps, 1)
            pe.wait_ge(GT_done, 2)
            pe.wait_ge(vkb_done, 2)
            for g in range(NG):
                for h in range(H):
                    for q in range(Q4):
                        qs = slice(C * q, C * q + C)
                        ins = pe.matmul(PA[qs, g // 4, P * (g % 4) + DH * h:P * (g % 4) + DH * h + DH],
                                        GT[qs, :, NG * h + g], vb_sl[qs, g, DH * h:DH * h + DH], start=True, stop=True)
            ins.then_inc(uw_ps, 1)
            for g in range(NG):
                for h in range(H):
                    for q in range(Q4):
                        qs = slice(C * q, C * q + C)
                        ins = pe.matmul(PB[DH * h:DH * h + DH, q, C * g:C * g + C], kb_sl[qs, g, DH * h:DH * h + DH],
                                        GT[qs, :, NG * h + g], start=True, stop=True)
            ins.then_inc(uw_ps, 1)
            pe.wait_ge(U_done, 1)
            pe.wait_ge(WT_done, 2)
            pe.wait_ge(AT_done, 1)
            for n in range(NCH):
                if n:
                    pe.wait_ge(S_done, n)
                    for b in range(NB):
                        q, bh = b % Q4, b // Q4
                        ins = pe.matmul(psW[C * q:C * q + C, bh, :], WT[:, n, b, :], Sbd[:, n % 2, b, :], start=True, stop=True)
                    ins.then_inc(w_ps, 1)
                    pe.wait_ge(ut_done, n)
                if n < NCH - 1:
                    for bh in range(BH):
                        for h in range(H):
                            for q in range(Q4):
                                qs = slice(C * q, C * q + C)
                                ins = pe.matmul(psS[DH * h:DH * h + DH, q, bh, :], k_sl[qs, BH * n + bh, DH * h:DH * h + DH],
                                                U[qs, BH * n + bh, DH * h:DH * h + DH], start=True, stop=True)
                    ins.then_inc(dS_ps, 1)
                if n:
                    pe.wait_ge(o_done, n)
                for b in range(NB):
                    q, bh = b % Q4, b // Q4
                    qs = slice(C * q, C * q + C)
                    if n:
                        pe.matmul(psO[qs, bh, :], qT[:, n, b, :], Sbd[:, n % 2, b, :], start=True, stop=False)
                    for h in range(H):
                        hs = slice(DH * h, DH * h + DH)
                        ins = pe.matmul(psO[qs, bh, hs], AT[qs, h, BH * n + bh, :], U[qs, BH * n + bh, hs],
                                        start=(n == 0), stop=(n == 0 or h == H - 1))
                ins.then_inc(o_ps, 1)
            pe.wait_ge(S["fsC_done"], 1)
            pe.wait_ge(S_done, NCH - 1)
            to_chunks(fsC, PA).then_inc(S["fs_ps"], 1)
            pe.wait_ge(S["st_sq"], 5)
            for g in range(NG):
                ins = pe.transpose(PA[:, g // 4, P * (g % 4):P * (g % 4) + P],
                                   stats[:, H * g:H * g + H, :].rearrange("p h k -> p (h k)"), ident[:])
            ins.then_inc(S["st_ps"], 1)
            pe.wait_ge(S["stT_done"], 1)
            pe.wait_ge(o_done, NCH)
            xc = xnT[:].rearrange("p b (n c) -> p n b c", c=C)

            def gate_logits(u):
                h, half = u // 2, u % 2
                pe.wait_ge(S["h1_done"], u + 1)
                for k in range(2):
                    ins = pe.matmul(PB[DH * h:DH * h + DH, 2 * half + k, :], w2p[:], h1[:, u % 2, 512 * k:512 * k + 512],
                                    start=True, stop=True)
                ins.then_inc(S["lg_ps"], 1)

            pe.wait_ge(S["g_in2"], 16 * 13)
            for u in range(2 * H):
                h, half = u // 2, u % 2
                if u >= 2:
                    gate_logits(u - 2)
                for k in range(2):
                    j = 2 * half + k
                    bank = PA[:, 2 * (u % 2) + k, :]
                    pe.matmul(bank, w1x[:], xc[:, 2 * j:2 * j + 2], start=True, stop=False)
                    ins = pe.matmul(bank, w1s[DH * h:DH * h + 16, :], statsT[DH * h:DH * h + 16, 512 * j:512 * j + 512],
                                    start=False, stop=True)
                ins.then_inc(S["h1_ps"], 1)
            gate_logits(2 * H - 2)
            gate_logits(2 * H - 1)
            pe.wait_ge(S["lgT_done"], 1)
            for g in range(NG):
                ins = pe.transpose(PA[:, g // 4, P * (g % 4):P * (g % 4) + P], logT[:, P * g:P * g + P], ident[:])
            ins.then_inc(S["lgs_ps"], 1)
            pe.wait_ge(S["o_done2"], 1)
            for g in range(NG):
                ins = pe.transpose(PA[:, g // 4, P * (g % 4):P * (g % 4) + P], osl[:, g, :], ident[:])
            ins.then_inc(S["oT_ps"], 1)
            pe.wait_ge(S["m_done"], 1)
            pe.matmul(PB[0:NB, 0, 0:NE], small[:, 4, 0:NB], wg[:], start=True, stop=True).then_inc(S["gl_ps"], 1)
            pe.wait_ge(S["gd_done"], 1)
            pe.matmul(PB[:, 0, 0:NB * TOPK], ones[0:NB, :], gwd[:], start=True, stop=True)
            pe.transpose(PB[0:NE, 1, 0:NB], gw[:, 32:40], ident[0:NB, 0:NB]).then_inc(S["gT_ps"], 1)
            pe.wait_ge(S["gT_done"], 1)
            pe.matmul(PB[0:NB, 2, 0:D], gw[:, 56:64], b2e[:], start=True, stop=False)
            pe.matmul(PB[0:NB, 2, 0:D], gw[0:1, 48:56], b2m[:], start=False, stop=True).then_inc(S["bb_ps"], 1)
            pe.wait_ge(S["bb_done"], 1)
            pe.wait_ge(S["oT_done"], 1)

            def experts(b, piece):
                if piece < 6:
                    e, m = divmod(piece, 2)
                    u = 6 * b + piece
                    if e and m == 0:
                        pe.wait_ge(S["e_scaled"], 2 * b + e)
                    if u >= 2:
                        pe.wait_ge(S["up_done"], u - 1)
                    for k in (2 * m, 2 * m + 1):
                        ins = pe.matmul(ffn_h[:, u % 2, L * (k % 2):L * (k % 2) + L], expert(b, e)[:, P * k:P * k + P],
                                        xnT[:, b, :], start=True, stop=True)
                    ins.then_inc(S["up_ps"], 1)
                    return
                if b >= 2:
                    pe.wait_ge(S["y_done"], b - 1)
                y = ffn_y[:, b % 2]
                for t in range(2):
                    yt = y[:, D * t:D * t + D]
                    pe.matmul(yt, ident[0:NB, b:b + 1].broadcast_to([NB, P]), biasb[:], start=True, stop=False)
                    pe.matmul(yt, oT[:, b, P * t:P * t + P], wo[:], start=False, stop=False)
                    for e in range(3):
                        if t == 0:
                            pe.wait_ge(S["up_done"], 6 * b + 2 * e + 2)
                        for k in range(NBLK):
                            ins = pe.matmul(yt, hT[:, e, k, P * t:P * t + P],
                                            expert(b, e)[:, HID + NBLK + P * k:HID + NBLK + P * k + P],
                                            start=False, stop=(e == 2 and k == NBLK - 1))
                ins.then_inc(S["y_ps"], 1)

            pe_program(pe, experts)


def lay_out(i):
    import numpy as np
    f = lambda n: np.asarray(i["L0_attn_" + n])
    g = lambda n: np.asarray(i["L0_ffn_" + n])
    l = lambda n: np.asarray(i["L1_" + n])
    con = np.ascontiguousarray

    def packed(w1, b, w2):
        return np.concatenate([w1, b.reshape(NBLK, P).T, w2.reshape(NBLK, P, D).transpose(1, 0, 2).reshape(P, HID)], 1)

    return {
        "x": con(f("x").reshape(NT, P, D).transpose(1, 0, 2)),
        "wqkv": con(np.stack([f("Wk"), f("Wv"), f("Wq")], 1)),
        "wb": f("Wb"),
        "cw": con(np.stack([f("conv_k"), f("conv_v"), f("conv_q")], 1)),
        "fsw": con(f("fir_short").reshape(P, FS_TAPS)),
        "frev": con(np.pad(f("fir_long").reshape(P, FL_TAPS), ((0, 0), (FL_TAPS, FL_TAPS)))),
        "w1x": con(f("W1")[0:D]),
        "w1s": con(np.tile(np.pad(f("W1")[D:], ((0, 16), (0, 0))), (H, 1))),
        "b1": con(f("b1")[:, None]),
        "w2": f("W2"),
        "bcst": con(np.tile(np.concatenate([f("base_bias").ravel(), f("b2"), f("log_temp"), f("conv_residual_logit"),
                                            np.zeros(12, np.float32)])[None], (P, 1))),
        "rmsw": con(np.tile(f("rms_w"), H)[:, None]),
        "wo": f("Wo"),
        "wm": con(packed(g("W1m"), g("b1m"), g("W2m"))),
        "experts": con(np.stack([packed(*w) for w in zip(g("W1e"), g("b1e"), g("W2e"))])),
        "wg": g("w_gate"),
        "bgate": con(np.tile(g("b_gate")[None], (NB, 1))),
        "b2e": g("b2e"),
        "b2m": con(g("b2m")[None]),
        "alpha": con(np.tile(g("alpha").reshape(1, 1), (P, 1))),
        "l1_wvT": con(l("attn_Wv").T),
        "l1_woT": con(l("attn_Wo").T),
        "l1_wtT": con(l("ffn_weight").T),
        "l1_bv": con(np.tile(l("attn_bv")[None], (P, 1))),
        "l1_bo": con(np.tile(l("attn_bo")[None], (P, 1))),
    }


def kernel(**inputs):
    import concourse.bacc as _bacc
    from concourse.bass_utils import run_bass_kernel_spmd as _run
    arrays = lay_out(inputs)
    nc = _bacc.Bacc("TRN2", target_bir_lowering=False, num_devices=1)
    inp = {name: nc.dram_tensor("in_" + name, a.shape, mybir.dt.from_np(a.dtype), kind="ExternalInput").ap()
           for name, a in arrays.items()}
    out = nc.dram_tensor("out_0_dram", (NB, L, D), F32, kind="ExternalOutput").ap()
    attention_mix_kernel(nc, inp, out)
    r = _run(nc, [{"in_" + name: a for name, a in arrays.items()}], core_ids=[0])
    return r.results[0]["out_0_dram"]
```

```python
import concourse.bass as bass
from concourse import mybir
from contextlib import ExitStack

import numpy as np

F32 = mybir.dt.float32
BF16 = mybir.dt.bfloat16
U32 = mybir.dt.uint32
ALU = mybir.AluOpType
ACT = mybir.ActivationFunctionType
AX = mybir.AxisListType

P = 128
NB, L, D = 8, 256, 128
T = NB * L
NT = T // P
H, DH = 4, 32
C = 32
NCH = L // C
Q4 = 4
BH = NB // Q4
NG = NCH * BH
TAPS, FS_TAPS, FL_TAPS = 4, 5, 64
W64 = 64
NW = T // W64
EPS = 1e-5
HID = 512
NBLK = HID // P
NE, TOPK = 8, 2
PACK = HID + NBLK + HID
HS, DS = 16, 8
NJ = 4
SLOT = 64
NGRP = 6
ROWS = NGRP * DS
MROWS = 3
ROUND = 1.5 * 2.0 ** 23


def attention_mix_kernel(nc, inp, out):
    ctx = ExitStack()
    with ctx:
        def sb(name, shape, dt=F32):
            return ctx.enter_context(nc.sbuf_tensor(name, shape, dt))

        def sem(name):
            return ctx.enter_context(nc.semaphore(name))

        ps = ctx.enter_context(nc.psum_tensor("ps", [P, 8, 512], F32))
        PA, PB = ps[:, 0:4, :], ps[:, 4:8, :]

        def flat(ap):
            return ap.rearrange("p a b -> p (a b)")

        def bc(ap, axis, n):
            u = ap.unsqueeze(axis)
            shape = list(u.shape)
            shape[axis] = n
            return u.broadcast_to(shape)

        ARENA = 35328
        arena = sb("arena", [P, ARENA])
        used = [0]

        def carve(shape, dt=F32, start=None, layer=1):
            if start is not None:
                used[0] = start
            words = int(np.prod(shape)) // (2 if dt == BF16 else 1)
            for lo, hi in ((20976, 25088), (27136, 30208)):
                if layer == 2 and used[0] < hi and used[0] + words > lo:
                    used[0] = hi
            flat_view = arena[:, used[0]:used[0] + words]
            used[0] += words
            assert used[0] <= ARENA
            if dt == BF16:
                flat_view = flat_view.bitcast(BF16)
            names = "abcdef"[:len(shape)]
            return flat_view.rearrange("p (%s) -> p %s" % (" ".join(names), " ".join(names)), **dict(zip(names, shape)))

        def words_of(*buffers):
            return sum(int(np.prod(b.shape[1:])) for b in buffers)

        ident = sb("ident", [P, P])
        ones = sb("ones", [P, P])
        tri = sb("tri", [P, C])
        X = sb("X", [P, NT, D])
        xn = X
        sq = carve([NT, D])
        xnT = sb("xnT", [P, NB, L])
        y0 = carve([NB, L])
        y1 = sb("y1", [P, NB, L])
        kqT = carve([2, NCH, NB, C])
        kT, qT = kqT[:, 0], kqT[:, 1]
        vT = carve([NCH, NB, C])
        vTp = carve([NB, W64 + L])
        wqkv = sb("wqkv", [P, 3, D])
        wb = sb("wb", [P, H])
        conv_w = sb("cw", [P, 3, TAPS])
        short_w = sb("fsw", [P, FS_TAPS])
        small = sb("small", [P, 8, NT * H])
        x_stats = small[:, 0:2, :].rearrange("p a x -> p (a x)")[:, 0:6 * NT].rearrange("p (t k) -> p t k", k=6)
        x_mv = small[:, 2, 0:2 * NT].rearrange("p (t k) -> p t k", k=2)
        DVE_TILES = range(3)
        betaT = y0[0:H].rearrange("p b (n c) -> p (b n c)", c=C).rearrange("p (n b c) -> p n b c", n=NCH, c=C)
        beta_sl = sb("beta_sl", [P, H, NG])
        beta_p = sb("beta_p", [P, W64])
        k_sl = sb("k_sl", [P, NG, D])
        v_sl = carve([NG, D])
        kb_sl = X
        vb_sl = y0[:].rearrange("p b l -> p (b l)").rearrange("p (g d) -> p g d", d=D)
        A64 = carve([2, H, NG, C])
        A_prob = carve([C, 2, C])
        Sbd = carve([2, NB, P])
        AT = carve([H, NG, C])
        G = carve([C, 2, C])
        knT = kT
        GT_blocks = carve([H * NG, P], start=used[0] - words_of(A64, A_prob, Sbd, G, AT))
        used[0] += words_of(G, AT)
        WT = A64[:, 1].rearrange("p h g c -> p (h g c)").rearrange("p (n b c) -> p n b c", n=NCH, c=C)
        v_windows = A64[:].rearrange("p a h g c -> p (a h g c)").rearrange("p (w x) -> p w x", w=NW)
        long_by_window = vT[:].rearrange("p n b c -> p (n b c)").rearrange("p (d o) -> p d o", o=W64)
        U = vT[:].rearrange("p n b c -> p (n b c)").rearrange("p (g d) -> p g d", d=D)
        delta_sl = U
        toeplitz = carve([2, H, 8, W64])
        long_tokens = toeplitz[0:W64].rearrange("p a h d o -> p (a h d o)").rearrange("p (w x) -> p w x", w=NW)
        short_sl = carve([NG, D])
        long_sl = carve([NG, D])
        toeplitz_slots = (toeplitz[:, 0], toeplitz[:, 1]) + tuple(flat(ap[:]).rearrange("p (h d o) -> p h d o", h=H, o=W64) for ap in (short_sl, long_sl))
        shortT = y1
        short_chunk_order = sq[:].rearrange("p g d -> p (g d)").rearrange("p (n b c) -> p n b c", n=NCH, c=C)
        stats = G[:].rearrange("p c q t -> p (c q t)").rearrange("p (x k) -> p x k", k=32)
        statsT = A_prob[:].rearrange("p s q c -> p (s q c)")
        h1 = toeplitz[:].rearrange("p a h d o -> p (a h d o)").rearrange("p (s x) -> p s x", x=1024)
        logT = kT[:].rearrange("p n b c -> p (n b c)")
        mix_sl = y0[:].rearrange("p b l -> p (b l)").rearrange("p (g d) -> p g d", d=D)
        mixT = X[:].rearrange("p g d -> p (g d)").rearrange("p (b l) -> p b l", b=NB)
        x1 = k_sl
        xres = y1[:].rearrange("p b l -> p (b l)").rearrange("p (g d) -> p g d", d=D)
        w1x = sb("w1x", [P, D])
        w1s = arena[:, 10240:10240 + H * D].rearrange("p (h d) -> p h d", h=H)
        b1 = sb("b1", [P, 1])
        w2 = sb("w2", [P, 4])
        bcst = sb("bcst", [P, 64])
        rmsw = sb("rmsw", [P, 1])
        wo = sb("wo", [P, D])
        gate_p = sb("lg", [P, NG * H, 4])
        gate_tmp = sb("gp", [P, 4, NG * H])
        main_expert = sb("wm", [P, PACK])
        experts_a = sb("we", [P, 2, PACK])
        NWE = 3 * TOPK
        experts_b = carve([TOPK, PACK], start=23032)
        experts_c = carve([TOPK, PACK], start=20976)
        hT = sb("hT", [P, 3, NBLK, L])
        hT_more = carve([3, NBLK, L], start=27136)

        def hidden_of(b):
            return (hT, hT_more)[b % 2]

        tmp = hT[:, 0].rearrange("p k l -> p (k l)")
        choice = sb("gw", [NB, 64])
        idx = sb("idx", [NB, 8], U32)
        gates_diag = sb("gwd", [NB, NB, TOPK])
        gates_all = sb("gall", [P, NB * TOPK])
        wg = sb("wg", [P, NE])
        bgate = sb("bgate", [NB, NE])
        iota8 = sb("iota8", [NB, NE])
        b2e = sb("b2e", [NE, D])
        b2m = sb("b2m", [1, D])
        biasb = sb("biasb", [NB, D])
        alph = sb("alph", [P, 4])

        proj_w_in = sem("proj_w_in")
        consts_done = sem("consts_done")
        ternary_w_in = sem("ternary_w_in")
        x_var_done = sem("x_var_done")
        x_rstd_done = sem("x_rstd_done")
        xn_done = sem("xn_done")
        xn_rest_done = sem("xn_rest_done")
        xT_in_ps = sem("xT_in_ps")
        xnT_done = sem("xnT_done")
        proj_in_ps = sem("proj_in_ps")
        products_done = sem("products_done")
        newest_tap_done = sem("newest_tap_done")
        conv_done = sem("conv_done")
        silu_done = sem("silu_done")
        chunks_in_ps = sem("chunks_in_ps")
        chunk_squares = sem("chunk_squares")
        chunk_sums = sem("chunk_sums")
        norms_done = sem("norms_done")
        chunks_done = sem("chunks_done")
        beta_done_fm = sem("beta_done_fm")
        beta_done = sem("beta_done")
        beta_p_in_ps = sem("beta_p_in_ps")
        v_chunks_done = sem("v_chunks_done")
        knT_in_ps = sem("knT_in_ps")
        knT_done = sem("knT_done")
        A_in_ps = sem("A_in_ps")
        A_done = sem("A_done")
        A_problems_in_ps = sem("A_problems_in_ps")
        A_problems_done = sem("A_problems_done")
        local_done = sem("local_done")
        local_masked = sem("local_masked")
        beta_rows_done = sem("beta_rows_done")
        G_is_identity = sem("G_is_identity")
        G_done = sem("G_done")
        GT_in_ps = sem("GT_in_ps")
        zeros_done = sem("zeros_done")
        GT_done = sem("GT_done")
        uw_in_ps = sem("uw_in_ps")
        U_done = sem("U_done")
        WT_done = sem("WT_done")
        wS_in_ps = sem("wS_in_ps")
        u_corrected = sem("u_corrected")
        dS_in_ps = sem("dS_in_ps")
        state_done = sem("state_done")
        chunk_out_in_ps = sem("chunk_out_in_ps")
        chunk_out_done = sem("chunk_out_done")
        short_tap_done = sem("short_tap_done")
        short_conv_done = sem("short_conv_done")
        short_ordered = sem("short_ordered")
        short_in_ps = sem("short_in_ps")
        short_done = sem("short_done")
        windows_in_ps = sem("windows_in_ps")
        windows_done = sem("windows_done")
        long_in_ps = sem("long_in_ps")
        long_windows_done = sem("long_windows_done")
        long_tokens_in_ps = sem("long_tokens_in_ps")
        long_tokens_done = sem("long_tokens_done")
        long_in = sem("long_in")
        squares_done = sem("squares_done")
        stats_done = sem("stats_done")
        stats_zeroed = sem("stats_zeroed")
        stats_in_ps = sem("stats_in_ps")
        statsT_done = sem("statsT_done")
        gate_stats_in_ps = sem("gate_stats_in_ps")
        gate_sum_done = sem("gate_sum_done")
        gate_hidden_done = sem("gate_hidden_done")
        gate_x_in_ps = sem("gate_x_in_ps")
        gate_x_done = sem("gate_x_done")
        w1s_in = sem("w1s_in")
        gate_logits_in_ps = sem("gate_logits_in_ps")
        gate_logits_done = sem("gate_logits_done")
        log_temp_ready = sem("log_temp_ready")
        gate_exp_done = sem("gate_exp_done")
        mix_done = sem("mix_done")
        rms_sums_done = sem("rms_sums_done")
        rms_done = sem("rms_done")
        mix_normed = sem("mix_normed")
        mixT_in_ps = sem("mixT_in_ps")
        mixT_done = sem("mixT_done")
        small_w_in = sem("small_w_in")
        token_sums_done = sem("token_sums_done")
        choice_in_ps = sem("choice_in_ps")
        choice_logits_done = sem("choice_logits_done")
        choice_exp_done = sem("choice_exp_done")
        choice_done = sem("choice_done")
        choice_gates_done = sem("choice_gates_done")
        choice_gates_in_ps = sem("choice_gates_in_ps")
        choice_gatesT_done = sem("choice_gatesT_done")
        expert_bias_in_ps = sem("expert_bias_in_ps")
        expert_bias_done = sem("expert_bias_done")
        gates_done = sem("gates_done")
        expert_scaled = sem("expert_scaled")
        up_in_ps = sem("up_in_ps")
        up_done = sem("up_done")
        y_in_ps = sem("y_in_ps")
        y_done = sem("y_done")
        attn_in_ps = sem("attn_in_ps")
        attn_done = sem("attn_done")
        p_done = sem("p_done")
        weighed = sem("weighed")
        x_again_in = sem("x_again_in")
        x_in = tuple(sem("x_in%d" % i) for i in range(2))
        toeplitz_in = tuple(sem("toeplitz_in%d" % j) for j in range(4))
        expert_in = tuple(sem("expert_in%d" % i) for i in range(NWE))
        dve_chain = sem("dve_chain")
        pool_chain = sem("pool_chain")

        ps_first = ps[:, 0:2, :]
        ps_scores = ps[:, 2:5, :]
        ps_out = ps[:, 5, 0:L]
        ps_small = ps[:, 6, 0:2 * D]
        ps_turn = ps[:, 7, :]
        ps_turn16 = ps_turn.bitcast(BF16)

        V1 = carve([5, 2, HS, 32], start=30208)
        used[0] = 0
        wv1 = sb("l1_wv", [P, D])
        bv1 = sb("l1_bv", [P, D])
        wo1 = sb("l1_wo", [P, D])
        bo1 = sb("l1_bo", [P, D])
        wt = sb("l1_wt", [P, D])
        w_scale = sb("l1_wsc", [P, 4])
        identb = carve([P], BF16, layer=2)
        sel = carve([NJ, DS + 1], layer=2)
        ln_stats = carve([2, 6], layer=2)
        mv = sb("l1_mv", [P, 2, 2])
        nhalf = carve([2], layer=2)
        xn1 = carve([2, 2, D], layer=2)
        xn1T = carve([NB, L], layer=2)
        res1 = carve([2, 2, HS, DS], layer=2)
        operands_from = used[0]
        KTM = carve([2, 2, HS, SLOT], BF16, layer=2)
        QTM = carve([2, 2, HS, SLOT], BF16, layer=2)
        KQ_words = arena[:, operands_from:used[0]]
        KT = carve([3, HS // 2, L], BF16, layer=2)
        QT = carve([3, HS // 2, L], BF16, layer=2)
        row_max = carve([2, 2, 2, HS // 2], layer=2)
        max_rest = carve([2, 2, 2, HS // 2], layer=2)
        max_parts = carve([2, 2, 2, MROWS, HS // 2], BF16, layer=2)
        max_partsT = carve([2, L], BF16, layer=2)[0:2 * MROWS * HS // 2]
        E1 = carve([8, 2, L], layer=2)
        outT = carve([4, L], layer=2)
        inv_sums = carve([2, HS // 2, NJ], layer=2)[0:64]
        out_regrouped = carve([NJ, HS, DS], layer=2)[0:64]
        out_features = carve([L], layer=2)

        l1_w_in = sem("l1_w_in")
        l1_abs_sums = sem("l1_abs_sums")
        l1_abs_total = sem("l1_abs_total")
        l1_scale_done = sem("l1_scale_done")
        l1_ternary_done = sem("l1_ternary_done")
        l1_buffers_ready = sem("l1_buffers_ready")
        l1_var_done = sem("l1_var_done")
        l1_rstd_done = sem("l1_rstd_done")
        l1_xn_done = sem("l1_xn_done")
        l1_residual_done = sem("l1_residual_done")
        l1_xT_in_ps = sem("l1_xT_in_ps")
        l1_xT_done = sem("l1_xT_done")
        l1_p_in_ps = sem("l1_p_in_ps")
        l1_p_done = sem("l1_p_done")
        l1_part1_done = sem("l1_part1_done")
        l1_rest1_done = sem("l1_rest1_done")
        l1_part2_done = sem("l1_part2_done")
        l1_rest2_done = sem("l1_rest2_done")
        l1_part3_done = sem("l1_part3_done")
        l1_operands_done = sem("l1_operands_done")
        l1_operands_in_ps = sem("l1_operands_in_ps")
        l1_operandsT_done = sem("l1_operandsT_done")
        l1_first_scores_in_ps = sem("l1_first_scores_in_ps")
        l1_max_done = sem("l1_max_done")
        l1_max_parts_done = sem("l1_max_parts_done")
        l1_maxT_in_ps = sem("l1_maxT_in_ps")
        l1_maxT_done = sem("l1_maxT_done")
        l1_scores_in_ps = sem("l1_scores_in_ps")
        l1_exp_done = sem("l1_exp_done")
        l1_out_in_ps = sem("l1_out_in_ps")
        l1_out_done = sem("l1_out_done")
        l1_regroup_in_ps = sem("l1_regroup_in_ps")
        l1_regroup_done = sem("l1_regroup_done")
        l1_outT_in_ps = sem("l1_outT_in_ps")
        l1_outT_done = sem("l1_outT_done")
        l1_y_in_ps = sem("l1_y_in_ps")
        l1_y_done = sem("l1_y_done")
        l1_written = sem("l1_written")
        l1_max_in = tuple(sem("l1_max_in%d" % i) for i in range(3))
        l1_dve_chain = sem("l1_dve_chain")

        AT_LN, AT_XT, AT_P, AT_SPLIT = -57, -52, -50, (-45, -43, -41)
        AT_TR = (-35, -33, -31, -25)
        AT_B = -24
        AT_M = -5
        AT_S1 = (19, 21)
        AT_S2 = 24
        AT_Y = 26
        LAG = 2
        FIRST, LAST = AT_LN, 16 * (NB - 1) + AT_Y + 4

        def due(s, at):
            b, r = divmod(s - at, 16)
            return b if r == 0 and 0 <= b < NB else None

        def heads_due(s, at):
            b, h = divmod(s - at, 16)
            return (b, h) if 0 <= b < NB else None

        order = {"M": [], "T": []}
        for s in range(FIRST, LAST):
            for name, at in (("xT", AT_XT), ("P", AT_P), ("S2", AT_S2), ("y", AT_Y)):
                b = due(s, at)
                if b is not None:
                    order["M"].append((name, b))
            for name, at in (("TR0", AT_TR[0]), ("TR1", AT_TR[1]), ("TR2", AT_TR[2]), ("TR3", AT_TR[3]), ("mT", AT_M), ("S10", AT_S1[0]), ("S11", AT_S1[1])):
                b = due(s, at)
                if b is not None:
                    order["T"].append((name, b))

        DONE = {"xT": (l1_xT_done, 1, 1), "P": (l1_p_done, 1, 1), "S2": (l1_outT_done, 1, 1), "y": (l1_y_done, 1, 1),
                "TR0": (l1_operandsT_done, 4, 1), "TR1": (l1_operandsT_done, 4, 2), "TR2": (l1_operandsT_done, 4, 3), "TR3": (l1_operandsT_done, 4, 4),
                "mT": (l1_maxT_done, 1, 1), "S10": (l1_regroup_done, 2, 1), "S11": (l1_regroup_done, 2, 2)}

        def before(bank, name, b):
            return order[bank].index((name, b))

        def head_rows(h, n):
            return slice(SLOT * (h % 2), SLOT * (h % 2) + n)

        def parts(tm, b):
            return tm[:, b % 2, :, :, 0:ROWS].rearrange("p t h (g d) -> p (t h) g d", d=DS)

        def P_rows(b):
            return V1[:, b % 5, :, :, 0:DS].rearrange("p t h d -> p (t h) d")

        def rest(i):
            return res1[:, i].rearrange("p t h d -> p (t h) d")

        PIECES = 7
        MIX_SPLIT = (4, 1)
        EARLY = 3
        HEAD_START = EARLY * PIECES - 2

        def period(ffn_piece, b):
            for piece in range(PIECES):
                ffn_piece(b, piece)

        def weave(ffn_piece, step):
            s = FIRST
            for i in range(EARLY * PIECES, PIECES * (NB + 1)):
                ffn_piece(*divmod(i, PIECES))
                while i >= HEAD_START and s < FIRST + (i + 1 - HEAD_START) * (-FIRST) // (PIECES * (NB + 1) - HEAD_START):
                    step(s)
                    s += 1
            for s in range(s, LAST):
                step(s)

        def second_layer_tensor(pe, ffn_piece):
            def free(bank, name, b):
                n = before(bank, name, b)
                if n:
                    name, b = order[bank][n - 1]
                    done, per, first = DONE[name]
                    pe.wait_ge(done, per * b + first)

            def step(s):
                b = due(s, AT_XT)
                if b is not None:
                    pe.wait_ge(l1_xn_done, b + 1)
                    free("M", "xT", b)
                    for t in range(2):
                        ins = pe.transpose(ps_small[:, P * t:P * t + P], xn1[:, b % 2, t, :], ident[:])
                    ins.then_inc(l1_xT_in_ps, 1)
                b = due(s, AT_P)
                if b is not None:
                    pe.wait_ge(l1_xT_done, b + 1)
                    free("M", "P", b)
                    for t in range(2):
                        ins = pe.matmul(ps_small[:, P * t:P * t + P], xn1T[:, b, P * t:P * t + P], wv1[:], start=True, stop=True)
                    ins.then_inc(l1_p_in_ps, 1)
                for r in range(4):
                    b = due(s, AT_TR[r])
                    if b is not None:
                        pe.wait_ge(l1_buffers_ready, 2)
                        pe.wait_ge(l1_operands_done, b + 1)
                        free("T", "TR%d" % r, b)
                        src = (KTM, QTM)[r % 2]
                        for pr in range(4):
                            pair = 4 * (r // 2) + pr
                            for t in range(2):
                                ins = pe.transpose(ps_turn16[:, L * pr + P * t:L * pr + P * t + P],
                                                   src[:, b % 2, t, 2 * pair:2 * pair + 2, :].rearrange("p h s -> p (h s)"), identb[:])
                        ins.then_inc(l1_operands_in_ps, 1)
                b = due(s, AT_M)
                if b is not None:
                    pe.wait_ge(l1_max_parts_done, b + 1)
                    free("T", "mT", b)
                    for t in range(2):
                        ins = pe.transpose(ps_turn16[0:48, P * t:P * t + P],
                                           max_parts[:, b % 2, t].rearrange("p a k h -> p (a k h)"), identb[:])
                    ins.then_inc(l1_maxT_in_ps, 1)
                for k in range(2):
                    b = due(s, AT_S1[k])
                    if b is not None:
                        pe.wait_ge(l1_out_done, NJ * b + NJ)
                        free("T", "S1%d" % k, b)
                        ot = outT[:].rearrange("p g q -> p (g q)")
                        for r in range(8):
                            ins = pe.matmul(ps_turn[0:64, 36 * r:36 * r + 36], ot[:, 8 * k + r::16], sel[:].rearrange("p j d -> p (j d)"), start=True, stop=True)
                        ins.then_inc(l1_regroup_in_ps, 1)
                b = due(s, AT_S2)
                if b is not None:
                    pe.wait_ge(l1_regroup_done, 2 * b + 2)
                    free("M", "S2", b)
                    for j in range(NJ):
                        ins = pe.transpose(ps_small[:, 64 * j:64 * j + 64], out_regrouped[:, j].rearrange("p r d -> p (r d)"), ident[0:64, 0:64])
                    ins.then_inc(l1_outT_in_ps, 1)
                b = due(s, AT_Y)
                if b is not None:
                    pe.wait_ge(l1_outT_done, b + 1)
                    free("M", "y", b)
                    if b == 0:
                        pe.wait_ge(l1_ternary_done, 1)
                    for t in range(2):
                        pe.matmul(ps_small[:, P * t:P * t + P], out_features[:, P * t:P * t + P], wo1[:], start=True, stop=False)
                        ins = pe.matmul(ps_small[:, P * t:P * t + P], xn1T[:, b, P * t:P * t + P], wt[:], start=False, stop=True)
                    ins.then_inc(l1_y_in_ps, 1)
                bh = heads_due(s, AT_B)
                if bh:
                    b, h = bh
                    u = HS * b + h
                    pe.wait_ge(l1_operandsT_done, 4 * b + 2 + 2 * (h // 8))
                    if u >= 2:
                        pe.wait_ge(l1_max_done, u - 1)
                    rows = head_rows(h, SLOT)
                    for t in range(2):
                        ins = pe.matmul(ps_first[:, u % 2, L * t:L * t + L], QT[rows, b % 3, h // 2, P * t:P * t + P],
                                        KT[rows, b % 3, h // 2, :], start=True, stop=True)
                    ins.then_inc(l1_first_scores_in_ps, 1)
                bh = heads_due(s, 0)
                if bh:
                    b, h = bh
                    u = HS * b + h
                    if h == 0:
                        pe.wait_ge(l1_max_in[b % 3], 32 * (b // 3 + 1))
                    if u == 0:
                        pe.wait_ge(y_done, NB)
                    if u >= 3:
                        pe.wait_ge(l1_exp_done, u - 2)
                    rows = head_rows(h, SLOT)
                    for t in range(2):
                        ins = pe.matmul(ps_scores[:, u % 3, L * t:L * t + L], KT[rows, b % 3, h // 2, P * t:P * t + P],
                                        QT[rows, b % 3, h // 2, :], start=True, stop=True)
                    ins.then_inc(l1_scores_in_ps, 1)
                for g in range(NJ):
                    b = due(s, 4 * g + 3 + LAG)
                    if b is not None:
                        group = NJ * b + g
                        pe.wait_ge(l1_exp_done, NJ * (group + 1))
                        if group:
                            pe.wait_ge(l1_out_done, group)
                        for t in range(2):
                            for jj in range(NJ):
                                ins = pe.matmul(ps_out[32 * jj:32 * jj + 32, :], V1[:, b % 5, t, 4 * g + jj, :],
                                                E1[:, (4 * g + jj) % 8, t, :], start=(t == 0), stop=(t == 1))
                        ins.then_inc(l1_out_in_ps, 1)
            weave(ffn_piece, step)

        def second_layer_scalar(act, ffn_piece):

            def step(s):
                b = due(s, AT_XT)
                if b is not None:
                    act.wait_ge(l1_xT_in_ps, b + 1)
                    act.copy(xn1T[:, b, :], ps_small).then_inc(l1_xT_done, 1)
                b = due(s, AT_SPLIT[0])
                if b is not None:
                    act.wait_ge(l1_p_done, b + 1)
                    act.wait_ge(l1_buffers_ready, 2)
                    if b >= 2:
                        act.wait_ge(l1_operands_in_ps, 4 * (b - 1))
                    act.copy(parts(KTM, b)[:, :, 0:3, :], P_rows(b).unsqueeze(2).broadcast_to([P, 2 * HS, 3, DS])).then_inc(l1_part1_done, 1)
                b = due(s, AT_SPLIT[1])
                if b is not None:
                    act.wait_ge(l1_rest1_done, b + 1)
                    act.copy(parts(KTM, b)[:, :, 3:5, :], rest(0).unsqueeze(2).broadcast_to([P, 2 * HS, 2, DS])).then_inc(l1_part2_done, 1)
                b = due(s, AT_SPLIT[2])
                if b is not None:
                    act.wait_ge(l1_rest2_done, b + 1)
                    act.copy(parts(KTM, b)[:, :, 5, :], rest(1)).then_inc(l1_part3_done, 1)
                for r in (1, 3):
                    b = due(s, AT_TR[r])
                    if b is not None:
                        act.wait_ge(l1_operands_in_ps, 4 * b + r + 1)
                        if b >= 3:
                            act.wait_ge(l1_scores_in_ps, HS * (b - 3) + 8 * (r // 2 + 1))
                        act.copy(QT[:, b % 3, 4 * (r // 2):4 * (r // 2) + 4, :].rearrange("p a q -> p (a q)"), ps_turn16).then_inc(l1_operandsT_done, 1)
                for g in range(NJ):
                    b = due(s, 4 * g + 3 + LAG + 1)
                    if b is not None:
                        act.wait_ge(l1_out_in_ps, NJ * b + g + 1)
                        if b:
                            act.wait_ge(l1_regroup_in_ps, 2 * b)
                        act.copy(outT[:, g, :], ps_out).then_inc(l1_out_done, 1)
                b = due(s, AT_S2)
                if b is not None:
                    act.wait_ge(l1_outT_in_ps, b + 1)
                    if b:
                        act.wait_ge(l1_y_in_ps, b)
                    act.copy(out_features[:].rearrange("p (g j i) -> p j g i", g=4, j=NJ), ps_small.rearrange("p (j g i) -> p j g i", g=4, j=NJ)).then_inc(l1_outT_done, 1)
                bh = heads_due(s, 0)
                if bh:
                    b, h = bh
                    u = HS * b + h
                    act.wait_ge(l1_scores_in_ps, u + 1)
                    if u >= 8:
                        act.wait_ge(l1_out_in_ps, u // 4 - 1)
                    act.activation(E1[:, u % 8].rearrange("p t q -> p (t q)"), ps_scores[:, u % 3, :], ACT.Exp, scale=DS ** -0.5).then_inc(l1_exp_done, 1)
            weave(ffn_piece, step)

        def second_layer_vector(dve, ffn_piece):
            chain1 = [0]

            def link_l1(ins):
                chain1[0] += 1
                ins.then_inc(l1_dve_chain, 1)
                dve.wait_ge(l1_dve_chain, chain1[0])

            def step(s):
                b = due(s, AT_LN)
                if b is not None:
                    dve.wait_ge(y_done, b + 1)
                    if b < EARLY - 1:
                        dve.wait_ge(attn_done, b + 1)
                    xb = x1[:, 2 * b:2 * b + 2, :]
                    for t in range(2):
                        link_l1(dve.bn_stats(ln_stats[:, t, :], xb[:, t, :]))
                    for t in range(2):
                        link_l1(dve.bn_aggr(mv[:, t, :], ln_stats[:, t, :]))
                    dve.tensor_scalar(mv[:, :, 1], mv[:, :, 1], EPS, None, ALU.add).then_inc(l1_var_done, 1)
                b = due(s, AT_LN + 2)
                if b is not None:
                    xb = x1[:, 2 * b:2 * b + 2, :]
                    dve.wait_ge(l1_rstd_done, b + 1)
                    if b >= 2:
                        dve.wait_ge(l1_xT_in_ps, b - 1)
                    for t in range(2):
                        ins = dve.tensor_scalar(xn1[:, b % 2, t, :], xb[:, t, :], mv[:, t, 0:1], mv[:, t, 1:2], ALU.subtract, ALU.mult)
                    ins.then_inc(l1_xn_done, 1)
                b = due(s, AT_P)
                if b is not None:
                    dve.wait_ge(l1_p_in_ps, b + 1)
                    if b >= 5:
                        dve.wait_ge(l1_out_in_ps, NJ * (b - 4))
                    v = V1[:, b % 5, :, :, 0:DS]
                    for t in range(2):
                        ins = dve.tensor_tensor(v[:, t], ps_small[:, P * t:P * t + P].rearrange("p (h d) -> p h d", d=DS),
                                            bv1[:].rearrange("p (h d) -> p h d", d=DS), ALU.add)
                    ins.then_inc(l1_p_done, 1)
                for r in (0, 2):
                    b = due(s, AT_TR[r])
                    if b is not None:
                        dve.wait_ge(l1_operands_in_ps, 4 * b + r + 1)
                        if b >= 3:
                            dve.wait_ge(l1_scores_in_ps, HS * (b - 3) + 8 * (r // 2 + 1))
                        dve.tensor_copy(KT[:, b % 3, 4 * (r // 2):4 * (r // 2) + 4, :].rearrange("p a q -> p (a q)"), ps_turn16).then_inc(l1_operandsT_done, 1)
                b = due(s, AT_M)
                if b is not None:
                    dve.wait_ge(l1_maxT_in_ps, b + 1)
                    if b >= 2:
                        dve.wait_ge(l1_max_in[(b - 2) % 3], 32 * ((b - 2) // 3 + 1))
                    dve.tensor_copy(max_partsT[:, b % 2, :], ps_turn16[0:48, 0:L]).then_inc(l1_maxT_done, 1)
                for k in range(2):
                    b = due(s, AT_S1[k])
                    if b is not None:
                        dve.wait_ge(l1_regroup_in_ps, 2 * b + k + 1)
                        if b:
                            dve.wait_ge(l1_outT_in_ps, b)
                        p = ps_turn[0:64, 0:36 * 8].rearrange("p (r j d) -> p r j d", r=8, j=NJ)
                        link_l1(dve.reciprocal(inv_sums[:, k], p[:, :, :, DS]))
                        dve.tensor_tensor(out_regrouped[:, :, 8 * k:8 * k + 8, :].rearrange("p j r d -> p r j d"), p[:, :, :, 0:DS],
                                          inv_sums[:, k].unsqueeze(3).broadcast_to([64, 8, NJ, DS]), ALU.mult).then_inc(l1_regroup_done, 1)
                b = due(s, AT_Y)
                if b is not None:
                    dve.wait_ge(l1_y_in_ps, b + 1)
                    dve.wait_ge(l1_residual_done, b + 1)
                    xb = x1[:, 2 * b:2 * b + 2, :].rearrange("p t d -> p (t d)")
                    dve.tensor_tensor(xb, ps_small, xb, ALU.add).then_inc(l1_y_done, 1)
                bh = heads_due(s, AT_B)
                if bh:
                    b, h = bh
                    u = HS * b + h
                    dve.wait_ge(l1_first_scores_in_ps, u + 1)
                    if b >= 2 and h == 0:
                        dve.wait_ge(l1_max_parts_done, b - 1)
                    dve.reduce_max(row_max[:, b % 2, :, h % 2, h // 2], ps_first[:, u % 2, :].rearrange("p (t k) -> p t k", t=2), axis=AX.X).then_inc(l1_max_done, 1)
                b = due(s, AT_B + 16)
                if b is not None:
                    dve.wait_ge(l1_max_done, HS * b + 16)
                    if b >= 2:
                        dve.wait_ge(l1_maxT_in_ps, b - 1)
                    m = row_max[:, b % 2].rearrange("p t r a -> p (t r) a")
                    left = max_rest[:, b % 2].rearrange("p t r a -> p (t r) a")
                    o = max_parts[:, b % 2].rearrange("p t r k a -> p (t r) k a")
                    link_l1(dve.tensor_scalar(o[:, :, 0], m, -1.0, None, ALU.mult))
                    link_l1(dve.scalar_tensor_tensor(out=left, in0=m, scalar=-1.0, in1=o[:, :, 0], op0=ALU.mult, op1=ALU.subtract))
                    link_l1(dve.tensor_copy(o[:, :, 1], left))
                    link_l1(dve.tensor_tensor(left, left, o[:, :, 1], ALU.subtract))
                    ins = dve.tensor_copy(o[:, :, 2], left)
                    ins.then_inc(l1_max_parts_done, 1)
            weave(ffn_piece, step)

        def second_layer_gpsimd(pool, ffn_piece):
            def step(s):
                b = due(s, AT_LN)
                if b is not None:
                    pool.wait_ge(l1_var_done, b + 1)
                    pool.tensor_tensor(mv[:, :, 1], mv[:, :, 1], nhalf[:], ALU.pow).then_inc(l1_rstd_done, 1)
                b = due(s, AT_SPLIT[0])
                if b is not None:
                    k, q = parts(KTM, b), parts(QTM, b)
                    pool.wait_ge(l1_part1_done, b + 1)
                    pool.tensor_tensor(rest(0), P_rows(b), k[:, :, 0, :], ALU.subtract).then_inc(l1_rest1_done, 1)
                    pool.tensor_copy(q[:, :, 0:6:3, :], k[:, :, 0:2, :])
                    pool.wait_ge(l1_part2_done, b + 1)
                    pool.tensor_tensor(rest(1), rest(0), k[:, :, 3, :], ALU.subtract).then_inc(l1_rest2_done, 1)
                    pool.tensor_copy(q[:, :, 5, :], k[:, :, 0, :])
                    pool.tensor_copy(q[:, :, 1:5:3, :], k[:, :, 3:5, :])
                    pool.wait_ge(l1_part3_done, b + 1)
                    pool.tensor_copy(q[:, :, 2, :], k[:, :, 5, :]).then_inc(l1_operands_done, 1)
                    pool.wait_ge(l1_xn_done, b + 1)
                    xb = x1[:, 2 * b:2 * b + 2, :]
                    pool.tensor_tensor(xb, xb, bo1[:].unsqueeze(1).broadcast_to([P, 2, D]), ALU.add).then_inc(l1_residual_done, 1)
            weave(ffn_piece, step)

        def second_layer_sync(sp):
            for s in range(FIRST, LAST):
                b = due(s, AT_M)
                if b is not None:
                    sp.wait_ge(l1_maxT_done, b + 1)
                    sp.wait_ge(l1_operandsT_done, 4 * b + 4)
                    for par in range(2):
                        r0 = SLOT * par + ROWS
                        sp.dma_start(QT[r0:r0 + MROWS, b % 3], max_partsT[24 * par:24 * par + 24, b % 2, :]).then_inc(l1_max_in[b % 3], 16)
                b = due(s, AT_Y)
                if b is not None:
                    sp.wait_ge(l1_y_done, b + 1)
                    sp.dma_start(out[b].rearrange("(t p) d -> p t d", p=P), x1[:, 2 * b:2 * b + 2, :]).then_inc(l1_written, 16)
            sp.wait_ge(l1_written, 16 * NB)


        block = ctx.enter_context(nc.Block())

        xw = y0[:].rearrange("p b l -> p (b l)")
        ps_logits = ps[:, 7, 0:NG * H * 4].rearrange("p (g h k) -> p g h k", h=H, k=4)
        ffn_h, ffn_y = ps[:, 2:4, :], ps[:, 4:6, :]
        SIDE = (ps[:, 0:2, :], ps[:, 6:8, :])

        def side_tile(g):
            half, r = divmod(g, NG // 2)
            return SIDE[half][:, r // 4, P * (r % 4):P * (r % 4) + P]


        def expert(b, e):
            if e == 0:
                return main_expert[:]
            return (experts_a, experts_b, experts_c)[b % 3][:, e - 1, :]

        def chunk_tile(ap, n, bh):
            return ap[:, n, Q4 * bh:Q4 * bh + Q4, :].rearrange("p q c -> p (q c)")

        psW = ps[:, 4, 0:BH * D].rearrange("p (b x) -> p b x", b=BH)
        psO = ps[:, 6:8, 0:D]
        psS = ps[:, 0:4, 0:BH * DH].rearrange("p q (b x) -> p q b x", b=BH)

        def chunked(ap):
            return ap.rearrange("p b (n c) -> p b n c", c=C)

        def by_batch(ap):
            return ap.rearrange("p n b c -> p b n c")

        v_prod = [words.rearrange("p (b l) -> p b l", b=NB) for words in
                  (X[:].rearrange("p g d -> p (g d)"), v_sl[:].rearrange("p g d -> p (g d)"), y1[:].rearrange("p b l -> p (b l)"))]
        short_prod = [words.rearrange("p (b l) -> p b l", b=NB) for words in
                      (kT[:].rearrange("p n b c -> p (n b c)"), hT[:, 1:3].rearrange("p s k l -> p (s k l)"),
                       vT[:].rearrange("p n b c -> p (n b c)"), experts_a[:].rearrange("p e x -> p (e x)")[:, 0:T])]
        v_conv = sq[:].rearrange("p g d -> p (g d)").rearrange("p (b l) -> p b l", b=NB)

        def pair_of(bank):
            return flat(bank).rearrange("p (h g k c) -> p h g k c", h=H, k=2, c=C)

        def A_src(bank, a, pair):
            return pair_of(bank)[W64 * a:W64 * a + W64, 2 * pair:2 * pair + 2, :, 0, :]

        def A_dst(half, a, pair):
            return A64[0:W64, a, 2 * pair:2 * pair + 2, NG // 2 * half:NG // 2 * (half + 1), :]

        def local_src(bank, pair):
            return pair_of(bank)[:, 2 * pair:2 * pair + 2, :, 1, :]

        def local_dst(half, pair):
            return AT[:, 2 * pair:2 * pair + 2, NG // 2 * half:NG // 2 * (half + 1), :]

        def copy_gt(copy, bank, r, qs):
            for q in qs:
                a, low = divmod(q, 2)
                src = flat(bank)[C * low:C * low + C].rearrange("p (c a x) -> p c a x", a=2, x=H * NG)[:, :, a, :]
                ins = copy(GT_blocks[C * q:C * q + C, :, C * q + 16 * r:C * q + 16 * r + 16].rearrange("p x c -> p c x"), src)
            return ins

        WT_words = WT.rearrange("p n b c -> p (n b c)")

        def w_half(ap, half):
            return ap.rearrange("p (b x) -> p b x", b=4)[:, 2 * half:2 * half + 2, :]

        def fl64_view(r):
            return long_tokens.rearrange("p w (h d) -> p w h d", h=H)[:, :, :, 16 * r:16 * r + 16]

        def fl_psv(bank):
            return flat(bank)[0:W64].rearrange("p (d h w) -> p w h d", h=H, w=NW)

        SRC = (short_sl[:], long_sl[:], delta_sl, v_sl[:])

        STREAM_ORDER = (3, 1, 0, 2)
        delta_sq = kT[:].rearrange("p n b c -> p (n b c)").rearrange("p (g d) -> p g d", d=D)
        square_of = (short_sl[:], vb_sl, sq[:], delta_sq)

        def heads(ap):
            return ap.rearrange("p g (h d) -> p (g h) d", d=DH)

        weighed_sl = (X[:], logT.rearrange("p (g d) -> p g d", d=D))
        LB = bcst[:, 0:16].rearrange("p (h k) -> p h k", h=H)

        def scalar_gates_and_experts(act):
            act.wait_ge(short_done, 1)
            act.activation(square_of[2], SRC[STREAM_ORDER[2]], ACT.Square).then_inc(squares_done, 1)
            act.wait_ge(log_temp_ready, 1)
            act.activation(bcst[:, 44:48], bcst[:, 40:44], ACT.Exp, scale=-1.0).then_inc(gate_exp_done, 1)
            act.wait_ge(gate_exp_done, 1)
            act.activation(bcst[:, 44:48], bcst[:, 44:48], ACT.Ln, bias=1.0).then_inc(gate_exp_done, 1)
            act.activation(bcst[:, 48:52], bcst[:, 24:28], ACT.Sigmoid).then_inc(gate_exp_done, 1)
            for n in range(NCH):
                if n == 1:
                    act.wait_ge(choice_logits_done, 1)
                    act.activation(choice[:, 0:8], choice[:, 0:8], ACT.Exp).then_inc(choice_exp_done, 1)
                gs = slice(BH * n, BH * n + BH)
                act.wait_ge(chunk_out_done, n + 1)
                act.activation(delta_sq[:, gs, :], delta_sl[:, gs, :], ACT.Square).then_inc(squares_done, 1)
            act.wait_ge(stats_done, 5)
            l2 = stats[:, :, 3:16:4]
            act.activation(l2, l2, ACT.Sqrt).then_inc(squares_done, 1)
            act.wait_ge(gate_x_in_ps, 1)
            act.copy(xw, flat(PB)).then_inc(gate_x_done, 1)
            act.wait_ge(stats_in_ps, 1)
            act.copy(statsT, flat(PA)).then_inc(statsT_done, 1)
            for u in range(2 * H):
                act.wait_ge(gate_sum_done, u + 1)
                act.activation(h1[:, u % 2, :], h1[:, u % 2, :], ACT.Gelu, bias=b1[:]).then_inc(gate_hidden_done, 1)
            act.wait_ge(gate_logits_done, 2)
            act.activation(gate_p[:], gate_p[:], ACT.Exp).then_inc(gate_exp_done, 1)
            def hidden(b, piece):
                if piece < 6 and b < NB:
                    e, m = divmod(piece, 2)
                    u = 6 * b + piece
                    act.wait_ge(up_in_ps, u + 1)
                    if b >= 2 and piece == 0:
                        act.wait_ge(y_in_ps, b - 1)
                    for k in (2 * m, 2 * m + 1):
                        ins = act.activation(hidden_of(b)[:, e, k, :], ffn_h[:, u % 2, L * (k % 2):L * (k % 2) + L],
                                             ACT.Gelu_apprx_tanh, bias=expert(b, e)[:, HID + k:HID + k + 1])
                    ins.then_inc(up_done, 1)

            period(hidden, 0)
            for piece in range(MIX_SPLIT[0]):
                hidden(1, piece)
            act.wait_ge(mix_done, 1)
            act.activation(sq[:], mix_sl, ACT.Square).then_inc(mix_done, 1)
            for b, piece in [(1, p) for p in range(MIX_SPLIT[0], PIECES)] + [(2, p) for p in range(MIX_SPLIT[1])]:
                hidden(b, piece)
            act.wait_ge(rms_sums_done, 1)
            act.activation(gate_tmp[:, 0, :], gate_tmp[:, 0, :], ACT.Sqrt, scale=1.0 / DH, bias=small[:, 7, 0:1]).then_inc(rms_done, 1)
            for piece in range(MIX_SPLIT[1], PIECES):
                hidden(2, piece)
            act.wait_ge(mixT_in_ps, 1)
            for half, bank in enumerate(SIDE):
                ns = slice(NCH // 2 * half, NCH // 2 * (half + 1))
                ins = act.activation(mixT.rearrange("p b (n c) -> p n b c", c=C)[:, ns], flat(bank).rearrange("p (n b c) -> p n b c", b=NB, c=C),
                                     ACT.Copy, scale=rmsw[:])
            ins.then_inc(mixT_done, 1)
            second_layer_scalar(act, hidden)

        @block.sync
        def _(sp):
            for i in range(2):
                half = slice(NT // 2 * i, NT // 2 * (i + 1))
                sp.dma_start(X[:, half, :], inp["x"][:, half, :]).then_inc(x_in[i], 16)
            for dst, name in ((w1x[:], "w1x"), (b1[:], "b1"), (bcst[:, 0:40], "bcst"), (rmsw[:], "rmsw"),
                              (wo[:], "wo"), (main_expert[:], "wm"), (wg[:], "wg"), (bgate[:], "bgate"), (b2e[:], "b2e"),
                              (b2m[:], "b2m"), (alph[:, 0:1], "alpha")):
                sp.dma_start(dst, inp[name]).then_inc(small_w_in, 16)
            for dst, n in ((wv1, "wvT"), (bv1, "bv"), (wo1, "woT"), (bo1, "bo")):
                sp.dma_start(dst[:], inp["l1_" + n]).then_inc(l1_w_in, 16)
            sp.dma_start(w2[:], inp["w2"]).then_inc(small_w_in, 16)
            for j in range(4):
                for h in range(H):
                    src = bass.AP(inp["frev"].tensor, (DH * h + 8 * j) * 192, [[1, P], [192, 8], [1, W64]])
                    sp.dma_start(toeplitz_slots[j][:, h], src).then_inc(toeplitz_in[j], 16)
            sp.wait_ge(long_tokens_done, 2)
            for q in range(Q4):
                for par in range(2):
                    for bh in range(BH):
                        src = long_tokens[C * par:C * par + C, 4 * (Q4 * bh + q):4 * (Q4 * bh + q) + 4, :]
                        dst = long_sl[C * q:C * q + C].rearrange("p (nh par bh) x -> p nh par bh x", par=2, bh=BH)[:, :, par, bh, :]
                        sp.dma_start(dst, src).then_inc(long_in, 16)
            sp.wait_ge(short_ordered, 1)
            sp.dma_start(w1s, inp["w1s"]).then_inc(w1s_in, 16)
            sp.dma_start(xres, inp["x"]).then_inc(x_again_in, 16)
            sp.wait_ge(choice_done, 1)
            for i in range(NB * TOPK):
                if i == 2:
                    sp.wait_ge(chunk_out_done, NCH)
                if i == 4:
                    sp.wait_ge(gate_logits_done, 1)
                if i >= NWE:
                    sp.wait_ge(y_in_ps, i // TOPK - 2)
                e = sp.value_load(idx[i // TOPK:i // TOPK + 1, i % TOPK:i % TOPK + 1], min_val=0, max_val=NE - 1)
                sp.dma_start(expert(i // TOPK, 1 + i % TOPK), inp["experts"][bass.ds(e, 1), :, :].rearrange("e p x -> p (e x)")).then_inc(expert_in[i % NWE], 16)
            second_layer_sync(sp)

        @block.gpsimd
        def _(pool):
            chain = [0]

            def link(ins):
                chain[0] += 1
                ins.then_inc(pool_chain, 1)
                pool.wait_ge(pool_chain, chain[0])

            pool.memset(ones[:], 1.0).then_inc(consts_done, 1)
            link(pool.memset(ident[:], 0.0))
            pool.affine_select(out=ident[:], in_=ident[:], compare_op=ALU.not_equal, fill=1.0, base=0,
                               pattern=[[-1, P]], channel_multiplier=1).then_inc(consts_done, 1)
            for i in range(4):
                pool.wait_ge(x_var_done, i + 1)
                pool.tensor_tensor(x_mv[:, 4 * i:4 * i + 4, 1], x_mv[:, 4 * i:4 * i + 4, 1], small[:, 7, 2:6], ALU.pow).then_inc(x_rstd_done, 1)
                if len(DVE_TILES) < 4:
                    pool.wait_ge(x_rstd_done, i + 1)
                    for t in range(len(DVE_TILES), 4):
                        ins = pool.tensor_scalar(xn[:, 4 * i + t, :], X[:, 4 * i + t, :], x_mv[:, 4 * i + t, 0:1], x_mv[:, 4 * i + t, 1:2],
                                                 ALU.subtract, ALU.mult)
                    ins.then_inc(xn_rest_done, 1)
            link(pool.memset(tri[:], 1.0))
            for q in range(Q4):
                link(pool.affine_select(out=tri[C * q:C * q + C, :], in_=tri[C * q:C * q + C, :],
                                        compare_op=ALU.is_ge, fill=0.0, base=0,
                                        pattern=[[1, C]], channel_multiplier=-1))
            pool.iota(iota8[:], [[1, NE]], base=0, channel_multiplier=0, allow_small_or_imprecise_dtypes=True).then_inc(stats_zeroed, 1)
            link(pool.memset(G[:], 0.0))
            pool.affine_select(out=G[:], in_=G[:], compare_op=ALU.not_equal, fill=1.0, base=0,
                               pattern=[[1, C], [0, 2], [-1, C]], channel_multiplier=0).then_inc(G_is_identity, 1)
            pool.wait_ge(l1_scale_done, 1)
            link(pool.tensor_scalar(wt[:], wt[:], w_scale[:, 2:3], None, ALU.mult))
            link(pool.tensor_scalar(wt[:], wt[:], 1.0, -1.0, ALU.min, ALU.max))
            link(pool.tensor_scalar(wt[:], wt[:], ROUND, None, ALU.add))
            link(pool.tensor_scalar(wt[:], wt[:], ROUND, None, ALU.subtract))
            pool.tensor_scalar(wt[:], wt[:], w_scale[:, 1:2], None, ALU.mult).then_inc(l1_ternary_done, 1)
            pool.wait_ge(newest_tap_done, 4)
            for i in range(1, TAPS):
                pool.wait_ge(products_done, i)
                ins = pool.tensor_tensor(v_conv[:, :, i:], v_conv[:, :, i:], v_prod[i - 1][:, :, 0:L - i], ALU.add)
                if i < TAPS - 1:
                    link(ins)
            ins.then_inc(conv_done, 1)
            pool.wait_ge(beta_done, 1)
            pool.wait_ge(silu_done, 3)
            for src, dst, ready in ((v_sl, vb_sl, v_chunks_done), (k_sl, kb_sl, chunks_done)):
                pool.wait_ge(ready, 1)
                pool.tensor_tensor(dst[:].rearrange("p g (h d) -> p g h d", h=H),
                                   src[:].rearrange("p g (h d) -> p g h d", h=H),
                                   bc(beta_sl[:].rearrange("p h g -> p g h"), 3, DH), ALU.mult).then_inc(beta_rows_done, 1)
            pool.wait_ge(local_done, 4)
            at3 = AT[:].rearrange("p h g c -> p (h g) c")
            pool.tensor_tensor(at3, at3, bc(tri[:], 1, H * NG), ALU.mult).then_inc(local_masked, 1)
            pool.wait_ge(long_in_ps, 4)
            gt_words = GT_blocks[:].rearrange("p x c -> p (x c)")
            pool.memset(gt_words[:, 0:words_of(A64)], 0.0)
            pool.memset(Sbd[:], 0.0).then_inc(zeros_done, 1)
            def short_tap(i):
                pool.wait_ge(products_done, TAPS - 1 + i)
                return pool.tensor_tensor(shortT[:, :, i:], shortT[:, :, i:], short_prod[i - 1][:, :, 0:L - i], ALU.add)

            link(short_tap(1))
            link(short_tap(2))
            pool.wait_ge(G_done, 1)
            pool.memset(A_prob[:], 0.0).then_inc(zeros_done, 1)
            link(short_tap(3))
            pool.wait_ge(GT_in_ps, 2)
            pool.memset(stats, 0.0).then_inc(stats_zeroed, 1)
            short_tap(4).then_inc(short_conv_done, 1)
            pool.wait_ge(uw_in_ps, 2)
            pool.memset(Sbd[:], 0.0).then_inc(zeros_done, 1)
            pool.wait_ge(gates_done, 1)
            def scale_expert(i):
                if i < NB * TOPK:
                    pool.wait_ge(expert_in[i % NWE], 16 * (i // NWE + 1))
                    w2 = expert(i // TOPK, 1 + i % TOPK)[:, HID + NBLK:]
                    pool.tensor_scalar(w2, w2, gates_all[:, i:i + 1], None, ALU.mult).then_inc(expert_scaled, 1)

            def scale_next(b, piece):
                if piece in (3, 5):
                    scale_expert(TOPK * (b + 1) + piece // 2 - 1)

            scale_expert(0)
            scale_expert(1)
            pool.wait_ge(p_done, 2)
            for i, k in enumerate((2, 3)):
                pool.tensor_tensor(heads(weighed_sl[i]), heads(SRC[k]), bc(gate_p[:, :, k], 2, DH), ALU.mult).then_inc(weighed, 1)
            for b in range(EARLY):
                period(scale_next, b)
            pool.wait_ge(mixT_done, 1)
            pool.memset(nhalf, -0.5)
            link(pool.memset(KQ_words, 0.0))
            pool.memset(KTM[:, :, :, :, ROWS:ROWS + MROWS], 1.0)
            pool.tensor_copy(identb, ident[:])
            pool.tensor_copy(sel, ident[:].rearrange("p (j d) -> p j d", j=NJ)[:, :, 0:DS + 1]).then_inc(l1_buffers_ready, 1)
            pool.wait_ge(l1_buffers_ready, 2)
            second_layer_gpsimd(pool, scale_next)

        @block.scalar
        def _(act):
            act.dma_start(wt[:], inp["l1_wtT"]).then_inc(ternary_w_in, 16)
            act.dma_start(wqkv[:], inp["wqkv"]).then_inc(proj_w_in, 16)
            act.dma_start(wb[:], inp["wb"]).then_inc(proj_w_in, 16)
            act.dma_start(conv_w[:], inp["cw"]).then_inc(proj_w_in, 16)
            act.dma_start(short_w[:], inp["fsw"]).then_inc(proj_w_in, 16)
            for i in range(4):
                act.wait_ge(xT_in_ps, i + 1)
                act.copy(xnT[:, 2 * i:2 * i + 2, :], PA[:, i, :]).then_inc(xnT_done, 1)
            act.wait_ge(proj_w_in, 64)

            def newest_tap(projection, i, y, bank):
                act.wait_ge(proj_in_ps, projection + 1)
                act.activation(y[:].rearrange("p b l -> p (b l)"), flat(bank), ACT.Copy,
                               scale=conv_w[:, i, TAPS - 1:TAPS]).then_inc(newest_tap_done, 1)

            newest_tap(0, 0, y0, PB)
            newest_tap(1, 2, y1, PA)
            act.wait_ge(conv_done, 1)
            act.activation(by_batch(kT[:]), chunked(y0[:]), ACT.Silu).then_inc(silu_done, 1)
            act.wait_ge(chunks_in_ps, 1)
            act.activation(sq[:].rearrange("p a b -> p (a b)"), flat(PB), ACT.Square).then_inc(chunk_squares, 1)
            act.wait_ge(conv_done, 2)
            act.activation(by_batch(qT[:]), chunked(y1[:]), ACT.Silu).then_inc(silu_done, 1)
            act.wait_ge(chunk_sums, 1)
            act.activation(small[:, 2, :], small[:, 2, :], ACT.Sqrt, bias=small[:, 7, 1:2]).then_inc(norms_done, 1)
            act.wait_ge(proj_in_ps, 3)
            act.wait_ge(silu_done, 1)
            act.activation(by_batch(betaT), flat(PA)[0:H].rearrange("p (b n c) -> p b n c", n=NCH, c=C),
                           ACT.Sigmoid).then_inc(beta_done_fm, 1)
            act.wait_ge(knT_in_ps, 2)
            act.copy(knT[:, NCH // 2:].rearrange("p n b c -> p (n b c)"), flat(PB[:, 2:4, :])).then_inc(knT_done, 1)
            act.wait_ge(chunks_in_ps, 2)
            act.wait_ge(proj_in_ps, 4)
            act.copy(y0[:].rearrange("p b l -> p (b l)"), flat(PB)).then_inc(newest_tap_done, 1)
            act.wait_ge(newest_tap_done, 3)
            act.activation(v_conv, y0[:], ACT.Copy, scale=conv_w[:, 1, TAPS - 1:TAPS]).then_inc(newest_tap_done, 1)
            for i in range(1, TAPS):
                act.activation(v_prod[i - 1], y0[:], ACT.Copy, scale=conv_w[:, 1, TAPS - 1 - i:TAPS - i]).then_inc(products_done, 1)
            for half, bank in enumerate((PA, PB)):
                act.wait_ge(A_in_ps, half + 1)
                for a in range(2):
                    ins = act.copy(A_dst(half, a, 1), A_src(bank, a, 1))
                ins.then_inc(A_done, 1)
                act.copy(local_dst(half, 1), local_src(bank, 1)).then_inc(local_done, 1)
            act.wait_ge(conv_done, 3)
            act.activation(by_batch(vT[:]), chunked(v_conv), ACT.Silu)
            act.activation(vTp[:, :, W64:], v_conv, ACT.Silu).then_inc(silu_done, 1)
            act.wait_ge(silu_done, 3)
            act.activation(shortT[:], vTp[:, :, W64:], ACT.Copy, scale=short_w[:, FS_TAPS - 1:FS_TAPS]).then_inc(short_tap_done, 1)
            act.wait_ge(chunks_in_ps, 3)
            act.activation(sq[:].rearrange("p a b -> p (a b)"), flat(PB), ACT.Square).then_inc(chunk_squares, 1)
            act.wait_ge(chunks_in_ps, 4)
            act.copy(v_sl[:].rearrange("p a b -> p (a b)"), flat(PA)).then_inc(v_chunks_done, 1)
            for i in (1, 2):
                act.activation(short_prod[i - 1], vTp[:, :, W64:], ACT.Copy, scale=short_w[:, FS_TAPS - 1 - i:FS_TAPS - i]).then_inc(products_done, 1)
            for half, bank in enumerate((PA, PB)):
                act.wait_ge(windows_in_ps, half + 1)
                act.copy(v_windows[:, NW // 2 * half:NW // 2 * (half + 1), :].rearrange("p w x -> p (w x)"), flat(bank)).then_inc(windows_done, 1)
            for j in range(4):
                act.wait_ge(long_in_ps, j + 1)
                act.copy(long_by_window[:, 8 * j:8 * j + 8, :],
                         PA[:, j, :].rearrange("p (d o) -> p d o", o=W64)[:, :, ::-1]).then_inc(long_windows_done, 1)
            for r, bank in enumerate((PA, PB)):
                act.wait_ge(long_tokens_in_ps, r + 1)
                act.copy(fl64_view(r), fl_psv(bank)).then_inc(long_tokens_done, 1)
            for i in (3, 4):
                act.activation(short_prod[i - 1], vTp[:, :, W64:], ACT.Copy, scale=short_w[:, FS_TAPS - 1 - i:FS_TAPS - i]).then_inc(products_done, 1)
            act.activation(square_of[0], SRC[STREAM_ORDER[0]], ACT.Square).then_inc(squares_done, 1)
            act.wait_ge(GT_in_ps, 2)
            act.wait_ge(zeros_done, 2)
            copy_gt(act.copy, PB, 1, range(Q4)).then_inc(GT_done, 1)
            act.wait_ge(chunk_sums, 2)
            act.activation(small[:, 3, :], small[:, 3, :], ACT.Sqrt, bias=small[:, 7, 1:2]).then_inc(norms_done, 1)
            act.wait_ge(short_conv_done, 1)
            act.copy(short_chunk_order.rearrange("p n b c -> p b n c"), chunked(shortT[:])).then_inc(short_ordered, 1)
            act.wait_ge(uw_in_ps, 1)
            act.copy(U.rearrange("p g d -> p (g d)"), flat(PA)).then_inc(U_done, 1)
            act.wait_ge(uw_in_ps, 2)
            act.copy(w_half(WT_words, 1), PB[:, 2:4, :]).then_inc(WT_done, 1)
            act.wait_ge(long_in, 16 * 16)
            act.activation(square_of[1], SRC[STREAM_ORDER[1]], ACT.Square).then_inc(squares_done, 1)
            act.wait_ge(short_in_ps, 1)
            act.wait_ge(stats_done, 1)
            act.copy(short_sl[:].rearrange("p g d -> p (g d)"), flat(PA)).then_inc(short_done, 1)
            scalar_gates_and_experts(act)

        @block.vector
        def _(dve):
            chain = [0]

            def link(ins):
                chain[0] += 1
                ins.then_inc(dve_chain, 1)
                dve.wait_ge(dve_chain, chain[0])

            dve.memset(small[:, 7, 0:1], EPS)
            dve.memset(small[:, 7, 1:2], 1e-6)
            dve.memset(vTp[:, :, 0:W64], 0.0)
            dve.memset(small[:, 7, 2:6], -0.5)
            dve.wait_ge(ternary_w_in, 16)
            dve.tensor_reduce(w_scale[:, 0:1], wt[:], axis=AX.X, op=ALU.add, apply_absolute_value=True).then_inc(l1_abs_sums, 1)
            dve.wait_ge(l1_abs_total, 1)
            link(dve.tensor_scalar(w_scale[:, 1:2], PB[:, 0, 0:1], 1.0 / (D * D), 1e-5, ALU.mult, ALU.max))
            dve.reciprocal(w_scale[:, 2:3], w_scale[:, 1:2]).then_inc(l1_scale_done, 1)

            def token_stats(i):
                dve.wait_ge(x_in[i // 2], 16)
                for t in range(4 * i, 4 * i + 4):
                    ins = dve.bn_stats(x_stats[:, t, :], X[:, t, :])
                link(ins)
                for t in range(4 * i, 4 * i + 4):
                    ins = dve.bn_aggr(x_mv[:, t, :], x_stats[:, t, :])
                link(ins)
                dve.tensor_scalar(x_mv[:, 4 * i:4 * i + 4, 1], x_mv[:, 4 * i:4 * i + 4, 1], EPS, None, ALU.add).then_inc(x_var_done, 1)

            def normalise(eng, i, tiles, done):
                for t in tiles:
                    ins = eng.tensor_scalar(xn[:, 4 * i + t, :], X[:, 4 * i + t, :], x_mv[:, 4 * i + t, 0:1], x_mv[:, 4 * i + t, 1:2],
                                            ALU.subtract, ALU.mult)
                ins.then_inc(done, 1)

            for i in range(5):
                if i < 4:
                    token_stats(i)
                if i:
                    dve.wait_ge(x_rstd_done, i)
                    normalise(dve, i - 1, DVE_TILES, xn_done)
            def convolve(n, i, y, bank):
                dve.wait_ge(newest_tap_done, n + 1)
                p3 = flat(bank).rearrange("p (b l) -> p b l", b=NB)
                for s in range(1, TAPS):
                    ins = dve.scalar_tensor_tensor(out=y[:, :, s:], in0=p3[:, :, 0:L - s],
                                                   scalar=conv_w[:, i, TAPS - 1 - s:TAPS - s], in1=y[:, :, s:],
                                                   op0=ALU.mult, op1=ALU.add)
                    if s < TAPS - 1:
                        link(ins)
                ins.then_inc(conv_done, 1)

            convolve(0, 0, y0, PB)
            convolve(1, 2, y1, PA)
            dve.wait_ge(chunk_squares, 1)
            dve.reduce_sum(small[:, 2, :], sq[:].rearrange("p g (h d) -> p (g h) d", d=DH), axis=AX.X).then_inc(chunk_sums, 1)
            dve.wait_ge(norms_done, 1)
            link(dve.reciprocal(small[:, 2, :], small[:, 2, :]))
            dve.tensor_tensor(k_sl[:].rearrange("p g (h d) -> p (g h) d", d=DH),
                              flat(PB).rearrange("p (g d) -> p g d", d=DH),
                              bc(small[:, 2, :], 2, DH), ALU.mult).then_inc(chunks_done, 1)
            dve.wait_ge(knT_in_ps, 1)
            dve.tensor_copy(knT[:, 0:NCH // 2].rearrange("p n b c -> p (n b c)"), flat(PB[:, 0:2, :])).then_inc(knT_done, 1)
            dve.wait_ge(chunks_in_ps, 2)
            dve.tensor_copy(beta_sl[:].rearrange("p h g -> p g h"),
                            PA[:, 0, 0:NG * H].rearrange("p (g h) -> p g h", h=H)).then_inc(beta_done, 1)
            dve.wait_ge(beta_p_in_ps, 1)
            for qhi in range(2):
                ins = dve.tensor_copy(beta_p[W64 * qhi:W64 * qhi + W64, :], PA[0:W64, 1 + qhi, 0:W64])
            ins.then_inc(chunks_done, 1)
            for half, bank in enumerate((PA, PB)):
                dve.wait_ge(A_in_ps, half + 1)
                for a in range(2):
                    ins = dve.tensor_copy(A_dst(half, a, 0), A_src(bank, a, 0))
                ins.then_inc(A_done, 1)
                dve.tensor_copy(local_dst(half, 0), local_src(bank, 0)).then_inc(local_done, 1)
            dve.wait_ge(A_problems_in_ps, 1)
            dve.tensor_tensor(A_prob[:].rearrange("p s q c -> p s (q c)"), flat(PA).rearrange("p (s x) -> p s x", s=C),
                              bc(beta_p[:], 1, C), ALU.mult).then_inc(A_problems_done, 1)
            dve.wait_ge(A_problems_done, 1)
            dve.wait_ge(G_is_identity, 1)
            for s in range(C - 1):
                m, w = C - 1 - s, s + 1
                t = tmp[:, 0:m * 2 * w].rearrange("p (c q t) -> p c q t", q=2, t=w)
                link(dve.tensor_tensor(t, bc(A_prob[:, s, :, w:].rearrange("p q c -> p c q"), 3, w),
                                       bc(G[:, s, :, 0:w], 1, m), ALU.mult))
                ins = dve.tensor_tensor(G[:, w:, :, 0:w], G[:, w:, :, 0:w], t, ALU.subtract)
                if s < C - 2:
                    link(ins)
            ins.then_inc(G_done, 1)
            dve.wait_ge(GT_in_ps, 1)
            dve.wait_ge(zeros_done, 2)
            copy_gt(dve.tensor_copy, PA, 0, range(Q4)).then_inc(GT_done, 1)
            dve.wait_ge(chunk_squares, 2)
            dve.reduce_sum(small[:, 3, :], sq[:].rearrange("p g (h d) -> p (g h) d", d=DH), axis=AX.X).then_inc(chunk_sums, 1)
            def stat(i, kind):
                k = STREAM_ORDER[i]
                if kind == 0:
                    if k == 1:
                        dve.wait_ge(long_in, 16 * 16)
                    dve.reduce_sum(stats[:, :, 4 * k], heads(SRC[k]), axis=AX.X)
                elif kind == 1:
                    dve.tensor_reduce(stats[:, :, 4 * k + 2], heads(SRC[k]), axis=AX.X, op=ALU.add, apply_absolute_value=True)
                else:
                    dve.wait_ge(squares_done, i + 1)
                    dve.reduce_sum(stats[:, :, 4 * k + 3], heads(square_of[i]), axis=AX.X).then_inc(stats_done, 1)

            def delta_stats(n):
                dve.wait_ge(chunk_out_done, n + 1)
                rows = slice(BH * H * n, BH * H * (n + 1))
                dve.reduce_sum(stats[:, rows, 8], heads(delta_sl[:, BH * n:BH * n + BH, :]), axis=AX.X)
                dve.tensor_reduce(stats[:, rows, 10], heads(delta_sl[:, BH * n:BH * n + BH, :]), axis=AX.X, op=ALU.add, apply_absolute_value=True)
                dve.wait_ge(squares_done, 4 + n)
                ins = dve.reduce_sum(stats[:, rows, 11], heads(delta_sq[:, BH * n:BH * n + BH, :]), axis=AX.X)
                if n == NCH - 1:
                    ins.then_inc(stats_done, 1)

            def token_mean():
                dve.wait_ge(xnT_done, 4)
                dve.reduce_sum(small[:, 4, 0:NB], xnT[:], axis=AX.X).then_inc(token_sums_done, 1)

            def gate_logit():
                dve.wait_ge(choice_in_ps, 1)
                link(dve.scalar_tensor_tensor(out=choice[:, 0:8], in0=ps[0:NB, 5, 0:NE], scalar=1.0 / L, in1=bgate[:],
                                              op0=ALU.mult, op1=ALU.add))
                link(dve.reduce_max(choice[:, 8:9], choice[:, 0:8], axis=AX.X))
                dve.tensor_scalar(choice[:, 0:8], choice[:, 0:8], choice[:, 8:9], None, ALU.subtract).then_inc(choice_logits_done, 1)

            def top_two():
                dve.wait_ge(choice_exp_done, 1)
                link(dve.reduce_sum(choice[:, 8:9], choice[:, 0:8], axis=AX.X))
                link(dve.reciprocal(choice[:, 8:9], choice[:, 8:9]))
                link(dve.tensor_scalar(choice[:, 0:8], choice[:, 0:8], choice[:, 8:9], None, ALU.mult))
                link(dve.max(choice[:, 16:24], choice[:, 0:8]))
                dve.max_index(idx[:], choice[:, 16:24], choice[:, 0:8]).then_inc(choice_done, 1)

            def gate_weights():
                dve.wait_ge(choice_done, 1)
                link(dve.reduce_sum(choice[:, 8:9], choice[:, 16:18], axis=AX.X))
                link(dve.reciprocal(choice[:, 8:9], choice[:, 8:9]))
                link(dve.tensor_scalar(alph[:, 1:2], alph[:, 0:1], 0.1, 1.0, ALU.max, ALU.min))
                link(dve.tensor_scalar(alph[:, 2:3], alph[:, 1:2], -1.0, 1.0, ALU.mult, ALU.add))
                link(dve.tensor_scalar(choice[:, 24:26], choice[:, 16:18], choice[:, 8:9], alph[0:NB, 2:3], ALU.mult, ALU.mult))
                link(dve.tensor_copy(choice[:, 26:28], idx[:, 0:2]))
                link(dve.tensor_scalar(choice[:, 32:40], iota8[:], choice[:, 26:27], choice[:, 24:25], ALU.is_equal, ALU.mult))
                link(dve.tensor_scalar(choice[:, 40:48], iota8[:], choice[:, 27:28], choice[:, 25:26], ALU.is_equal, ALU.mult))
                link(dve.tensor_tensor(choice[:, 32:40], choice[:, 32:40], choice[:, 40:48], ALU.add))
                link(dve.tensor_copy(choice[0:1, 48:56], alph[0:1, 1:2].broadcast_to([1, NB])))
                w2 = main_expert[:, HID + NBLK:]
                link(dve.tensor_scalar(w2, w2, alph[:, 1:2], None, ALU.mult))
                dve.tensor_tensor(gates_diag[:], bc(ident[0:NB, 0:NB], 2, TOPK), bc(choice[:, 24:26], 1, NB), ALU.mult).then_inc(choice_gates_done, 1)

            def gates_everywhere():
                dve.wait_ge(choice_gates_in_ps, 1)
                dve.tensor_copy(gates_all[:], ps[:, 5, 64:64 + NB * TOPK]).then_inc(gates_done, 1)
                dve.tensor_copy(choice[:, 56:64], ps[0:NE, 5, 128:128 + NB]).then_inc(choice_gatesT_done, 1)

            def bias_sum():
                dve.wait_ge(expert_bias_in_ps, 1)
                dve.tensor_copy(biasb[:], ps[0:NB, 5, 256:256 + D]).then_inc(expert_bias_done, 1)

            def temperature_in():
                dve.wait_ge(small_w_in, 16 * 12)
                link(dve.tensor_tensor(LB, LB, bc(bcst[:, 16:20], 1, H), ALU.add))
                dve.scalar_tensor_tensor(out=bcst[:, 40:44], in0=bcst[:, 20:24], scalar=-1.0, in1=bcst[:, 20:24],
                                              op0=ALU.mult, op1=ALU.max).then_inc(log_temp_ready, 1)

            def temperature():
                dve.wait_ge(gate_exp_done, 3)
                link(dve.scalar_tensor_tensor(out=bcst[:, 44:48], in0=bcst[:, 20:24], scalar=0.0, in1=bcst[:, 44:48],
                                              op0=ALU.max, op1=ALU.add))
                link(dve.tensor_scalar(bcst[:, 44:48], bcst[:, 44:48], 1e-4, None, ALU.add))
                link(dve.reciprocal(bcst[:, 44:48], bcst[:, 44:48]))

            dve.wait_ge(stats_zeroed, 2)
            stat(0, 0)
            stat(0, 1)
            stat(0, 2)
            token_mean()
            temperature_in()
            dve.wait_ge(uw_in_ps, 2)
            dve.tensor_copy(w_half(WT_words, 0), PB[:, 0:2, :]).then_inc(WT_done, 1)
            dve.wait_ge(zeros_done, 3)
            dve.wait_ge(norms_done, 2)
            link(dve.reciprocal(small[:, 3, :], small[:, 3, :]))
            between = {(0, 0): (lambda: stat(1, 0),), (1, 0): (gate_logit, lambda: stat(1, 1)), (2, 0): (lambda: stat(1, 2),),
                       (3, 0): (top_two,), (4, 0): (lambda: stat(2, 0),), (5, 0): (gate_weights,),
                       (6, 0): (gates_everywhere, lambda: stat(2, 1)), (7, 0): (bias_sum, temperature, lambda: stat(2, 2))}
            dve.wait_ge(short_done, 1)
            for n in range(NCH):
                gs = slice(BH * n, BH * n + BH)
                if n:
                    dve.wait_ge(wS_in_ps, n)
                    dve.tensor_tensor(U[:, gs, :], U[:, gs, :], psW, ALU.subtract).then_inc(u_corrected, 1)
                for extra in between.get((n, 0), ()):
                    extra()
                if n:
                    delta_stats(n - 1)
                if n < NCH - 1:
                    dve.wait_ge(dS_in_ps, n + 1)
                    for h in range(H):
                        hs = slice(DH * h, DH * h + DH)
                        old, new = (Sbd[hs, i % 2].rearrange("p (bh q) x -> p q bh x", q=Q4)[:, :, :, hs]
                                    for i in (n, n + 1))
                        if n:
                            ins = dve.tensor_tensor(new, old, psS[hs], ALU.add)
                        else:
                            ins = dve.tensor_copy(new, psS[hs])
                    ins.then_inc(state_done, 1)
                dve.wait_ge(chunk_out_in_ps, n + 1)
                dve.tensor_tensor(delta_sl[:, gs, :].rearrange("p g (h d) -> p g h d", d=DH),
                                  psO.rearrange("p g (h d) -> p g h d", d=DH),
                                  bc(small[:, 3, BH * H * n:BH * H * (n + 1)].rearrange("p (g h) -> p g h", h=H), 3, DH),
                                  ALU.mult).then_inc(chunk_out_done, 1)
                for extra in between.get((n, 1), ()):
                    extra()

            delta_stats(NCH - 1)
            dve.wait_ge(stats_done, 4)
            link(dve.tensor_scalar(stats[:, :, 0:16:2], stats[:, :, 0:16:2], 1.0 / DH, None, ALU.mult))
            mean, var, l2 = (stats[:, :, k:16:4] for k in (0, 1, 3))
            link(dve.tensor_tensor(var, mean, mean, ALU.mult))
            dve.scalar_tensor_tensor(out=var, in0=l2, scalar=1.0 / DH, in1=var, op0=ALU.mult,
                                     op1=ALU.subtract).then_inc(stats_done, 1)
            for u in range(2 * H):
                dve.wait_ge(gate_stats_in_ps, u + 1)
                if u == 0:
                    dve.wait_ge(gate_x_done, 1)
                if u >= 2:
                    dve.wait_ge(gate_logits_in_ps, u - 1)
                dve.tensor_tensor(h1[:, u % 2, :], flat(PA[:, 2 * (u % 2):2 * (u % 2) + 2, :]),
                                  xw[:, 1024 * (u % 2):1024 * (u % 2) + 1024], ALU.add).then_inc(gate_sum_done, 1)
            dve.wait_ge(gate_logits_in_ps, 2 * H)
            lg4 = gate_p[:].rearrange("p (g h) k -> p g h k", h=H)
            dve.tensor_tensor(lg4, ps_logits, bc(LB, 1, NG), ALU.add).then_inc(gate_logits_done, 1)
            dve.wait_ge(gate_logits_done, 1)
            link(dve.tensor_tensor(lg4, lg4, bc(bc(bcst[:, 44:48], 1, NG), 3, 4), ALU.mult))
            link(dve.reduce_max(gate_tmp[:, 0, :], gate_p[:], axis=AX.X))
            dve.tensor_tensor(gate_p[:], gate_p[:], bc(gate_tmp[:, 0, :], 2, 4), ALU.subtract).then_inc(gate_logits_done, 1)
            dve.wait_ge(gate_exp_done, 4)
            for last in range(2):
                link(dve.reduce_sum(gate_tmp[:, 1, :], gate_p[:], axis=AX.X))
                link(dve.reciprocal(gate_tmp[:, 1, :], gate_tmp[:, 1, :]))
                dve.tensor_tensor(gate_p[:], gate_p[:], bc(gate_tmp[:, 1, :], 2, 4), ALU.mult).then_inc(p_done, 1)
                dve.wait_ge(p_done, last + 1)
                if not last:
                    link(dve.tensor_scalar(gate_p[:, :, 0:2], gate_p[:, :, 0:2], 0.05, None, ALU.max))
            def residual(b, piece):
                b = b - 1
                if piece == 6 and b >= 0:
                    dve.wait_ge(y_in_ps, b + 1)
                    if b == 0:
                        dve.wait_ge(x_again_in, 16)
                    dve.tensor_tensor(x1[:, 2 * b:2 * b + 2, :], ffn_y[:, b % 2, 0:2 * D].rearrange("p (t d) -> p t d", d=D),
                                      xres[:, 2 * b:2 * b + 2, :], ALU.add).then_inc(y_done, 1)

            p0 = lg4[:, :, :, 0]
            link(dve.scalar_tensor_tensor(out=p0, in0=bc(bcst[:, 48:52], 1, NG), scalar=0.5, in1=p0, op0=ALU.mult, op1=ALU.add))
            link(dve.tensor_tensor(heads(mix_sl), heads(SRC[0]), bc(gate_p[:, :, 0], 2, DH), ALU.mult))
            link(dve.tensor_tensor(heads(sq[:]), heads(SRC[1]), bc(gate_p[:, :, 1], 2, DH), ALU.mult))
            link(dve.tensor_tensor(mix_sl, mix_sl, sq[:], ALU.add))
            dve.wait_ge(weighed, 1)
            link(dve.tensor_tensor(mix_sl, mix_sl, weighed_sl[0], ALU.add))
            dve.wait_ge(weighed, 2)
            dve.tensor_tensor(mix_sl, mix_sl, weighed_sl[1], ALU.add).then_inc(mix_done, 1)
            residual(1, 6)
            dve.wait_ge(mix_done, 2)
            dve.reduce_sum(gate_tmp[:, 0, :], heads(sq[:]), axis=AX.X).then_inc(rms_sums_done, 1)
            dve.wait_ge(rms_done, 1)
            link(dve.reciprocal(gate_tmp[:, 0, :], gate_tmp[:, 0, :]))
            dve.tensor_tensor(heads(mix_sl), heads(mix_sl), bc(gate_tmp[:, 0, :], 2, DH), ALU.mult).then_inc(mix_normed, 1)
            residual(2, 6)
            for b in range(EARLY - 1):
                dve.wait_ge(attn_in_ps, b + 1)
                xb = x1[:, 2 * b:2 * b + 2, :]
                dve.wait_ge(y_done, b + 1)
                dve.tensor_tensor(xb, ps[:, 6 + b % 2, 0:2 * D].rearrange("p (t d) -> p t d", d=D), xb, ALU.add).then_inc(attn_done, 1)
            dve.wait_ge(mixT_done, 1)
            link(dve.memset(V1, 0.0))
            dve.memset(V1[:, :, :, :, DS:DS + 1], 1.0).then_inc(l1_buffers_ready, 1)
            second_layer_vector(dve, residual)

        @block.tensor
        def _(pe):
            pe.wait_ge(consts_done, 2)
            pe.wait_ge(l1_abs_sums, 1)
            pe.matmul(PB[:, 0, 0:1], ones[:], w_scale[:, 0:1], start=True, stop=True).then_inc(l1_abs_total, 1)
            for i in range(5):
                if i < 4:
                    pe.wait_ge(xn_done, i + 1)
                    if len(DVE_TILES) < 4:
                        pe.wait_ge(xn_rest_done, i + 1)
                    for t in range(4):
                        ins = pe.transpose(PA[:, i, P * t:P * t + P], xn[:, 4 * i + t, :], ident[:])
                    ins.then_inc(xT_in_ps, 1)
                if i == 1:
                    pe.wait_ge(proj_w_in, 64)
                    pe.wait_ge(l1_scale_done, 1)
                if i:
                    pe.wait_ge(xnT_done, i)
                    ins = pe.matmul(PB[:, i - 1, :], wqkv[:, 0, :], xnT[:, 2 * (i - 1):2 * i, :], start=True, stop=True)
            ins.then_inc(proj_in_ps, 1)

            def project(w, bank, m=P):
                for j in range(4):
                    ins = pe.matmul(bank[0:m, j, :], w, xnT[:, 2 * j:2 * j + 2, :], start=True, stop=True)
                ins.then_inc(proj_in_ps, 1)

            def to_chunks(src, bank):
                for n in range(NCH):
                    for bh in range(BH):
                        g = BH * n + bh
                        ins = pe.transpose(bank[:, g // 4, P * (g % 4):P * (g % 4) + P], chunk_tile(src, n, bh), ident[:])
                return ins

            project(wqkv[:, 2, :], PA)
            pe.wait_ge(conv_done, 1)
            pe.wait_ge(silu_done, 1)
            to_chunks(kT, PB).then_inc(chunks_in_ps, 1)
            pe.wait_ge(conv_done, 2)
            project(wb[:], PA, H)
            pe.wait_ge(chunks_done, 1)
            for g in range(NG):
                ins = pe.transpose(PB[:, g // 4, P * (g % 4):P * (g % 4) + P], k_sl[:, g, :], ident[:])
                if g % (NG // 2) == NG // 2 - 1:
                    ins.then_inc(knT_in_ps, 1)
            pe.wait_ge(beta_done_fm, 1)
            for n in range(NCH):
                for bh in range(BH):
                    g = BH * n + bh
                    ins = pe.transpose(PA[:, 0, H * g:H * g + H], chunk_tile(betaT, n, bh), ident[0:H, 0:H])
            ins.then_inc(chunks_in_ps, 1)
            pe.wait_ge(beta_done, 1)
            for qhi in range(2):
                part = slice(W64 * qhi, W64 * qhi + W64)
                ins = pe.transpose(PA[0:W64, 1 + qhi, 0:W64], beta_sl[part].rearrange("p h g -> p (h g)"), ident[part, part])
            ins.then_inc(beta_p_in_ps, 1)
            pe.wait_ge(knT_done, 2)
            project(wqkv[:, 1, :], PB)
            pe.wait_ge(chunks_done, 2)
            pe.wait_ge(silu_done, 2)
            for half, bank in enumerate((PA, PB)):
                if half:
                    pe.wait_ge(newest_tap_done, 3)
                for gg in range(NG // 2):
                    g = NG // 2 * half + gg
                    for q in range(Q4):
                        for h in range(H):
                            hs = slice(DH * h, DH * h + DH)
                            b = Q4 * (g % BH) + q
                            ins = pe.matmul(bank[C * q:C * q + C, h, 2 * C * gg:2 * C * gg + 2 * C], knT[hs, g // BH, b, :],
                                            kqT[hs, :, g // BH, b, :], start=True, stop=True)
                ins.then_inc(A_in_ps, 1)
            pe.wait_ge(A_done, 4)
            a3 = A64[0:W64].rearrange("p a h g s -> p (a h g) s")
            for s in range(C):
                ins = pe.transpose(PA[:, s // 8, W64 * (s % 8):W64 * (s % 8) + W64], a3[:, :, s], ident[0:W64, 0:W64])
            ins.then_inc(A_problems_in_ps, 1)
            pe.wait_ge(local_done, 4)
            to_chunks(qT, PB).then_inc(chunks_in_ps, 1)
            pe.wait_ge(A_problems_done, 1)
            pe.wait_ge(silu_done, 3)
            to_chunks(vT, PA).then_inc(chunks_in_ps, 1)
            pe.wait_ge(chunk_squares, 2)
            pe.wait_ge(v_chunks_done, 1)
            for w in range(NW):
                bank = (PA, PB)[w // 16]
                ins = pe.transpose(bank[:, w % 16 // 4, P * (w % 4):P * (w % 4) + P],
                                   vTp[:, w // 4, W64 * (w % 4):W64 * (w % 4) + P], ident[:])
                if w % 16 == 15:
                    ins.then_inc(windows_in_ps, 1)
            pe.wait_ge(windows_done, 2)
            for j in range(4):
                pe.wait_ge(toeplitz_in[j], 16 * H)
                for d in range(8):
                    for h in range(H):
                        ins = pe.matmul(PA[C * h:C * h + C, j, W64 * d:W64 * d + W64], v_windows[:, :, DH * h + 8 * j + d],
                                        toeplitz_slots[j][:, h, d, :], start=True, stop=True)
                ins.then_inc(long_in_ps, 1)
            pe.wait_ge(long_windows_done, 4)
            for d in range(DH):
                bank = (PA, PB)[d // 16]
                ins = pe.transpose(bank[0:W64, d % 16 // 4, P * (d % 4):P * (d % 4) + P], long_by_window[:, d, :], ident[:])
                if d % 16 == 15:
                    ins.then_inc(long_tokens_in_ps, 1)
            pe.wait_ge(G_done, 1)
            pe.wait_ge(long_tokens_done, 2)
            for c in range(C):
                bank = (PA, PB)[c // 16]
                ins = pe.transpose(bank[0:W64, c % 16 // 4, P * (c % 4):P * (c % 4) + P],
                                   G[:, c].rearrange("p q t -> p (q t)"), ident[:])
                if c % 16 == 15:
                    ins.then_inc(GT_in_ps, 1)
            pe.wait_ge(GT_done, 2)
            pe.wait_ge(beta_rows_done, 2)
            for g in range(NG):
                for h in range(H):
                    hs = slice(DH * h, DH * h + DH)
                    for q in range(Q4):
                        ins = pe.matmul(PA[C * q:C * q + C, g // 4, P * (g % 4) + DH * h:P * (g % 4) + DH * h + DH],
                                        GT_blocks[:, NG * h + g, C * q:C * q + C], vb_sl[:, g, hs], start=True, stop=True)
            ins.then_inc(uw_in_ps, 1)
            for g in range(NG):
                for h in range(H):
                    hs = slice(DH * h, DH * h + DH)
                    ins = pe.matmul(PB[hs, g // 4, P * (g % 4):P * (g % 4) + P], kb_sl[:, g, hs],
                                GT_blocks[:, NG * h + g, :], start=True, stop=True)
            ins.then_inc(uw_in_ps, 1)
            pe.wait_ge(short_ordered, 1)
            pe.wait_ge(U_done, 1)
            to_chunks(short_chunk_order, PA).then_inc(short_in_ps, 1)
            pe.wait_ge(short_done, 1)
            pe.wait_ge(WT_done, 2)
            pe.wait_ge(local_masked, 1)
            for n in range(NCH):
                if n:
                    pe.wait_ge(state_done, n)
                    for b in range(NB):
                        q, bh = b % Q4, b // Q4
                        ins = pe.matmul(psW[C * q:C * q + C, bh, :], WT[:, n, b, :], Sbd[:, n % 2, b, :], start=True, stop=True)
                    ins.then_inc(wS_in_ps, 1)
                    pe.wait_ge(chunk_out_done, n)
                    for b in range(NB):
                        q, bh = b % Q4, b // Q4
                        pe.matmul(psO[C * q:C * q + C, bh, :], qT[:, n, b, :], Sbd[:, n % 2, b, :], start=True, stop=False)
                    pe.wait_ge(u_corrected, n)
                if n < NCH - 1:
                    for bh in range(BH):
                        for h in range(H):
                            for q in range(Q4):
                                qs = slice(C * q, C * q + C)
                                ins = pe.matmul(psS[DH * h:DH * h + DH, q, bh, :], k_sl[qs, BH * n + bh, DH * h:DH * h + DH],
                                                U[qs, BH * n + bh, DH * h:DH * h + DH], start=True, stop=True)
                    ins.then_inc(dS_in_ps, 1)
                for b in range(NB):
                    q, bh = b % Q4, b // Q4
                    qs = slice(C * q, C * q + C)
                    for h in range(H):
                        hs = slice(DH * h, DH * h + DH)
                        ins = pe.matmul(psO[qs, bh, hs], AT[qs, h, BH * n + bh, :], U[qs, BH * n + bh, hs],
                                        start=(n == 0), stop=(n == 0 or h == H - 1))
                ins.then_inc(chunk_out_in_ps, 1)
                if n == 0:
                    pe.wait_ge(token_sums_done, 1)
                    pe.wait_ge(small_w_in, 16 * 12)
                    pe.matmul(ps[0:NB, 5, 0:NE], small[:, 4, 0:NB], wg[:], start=True, stop=True).then_inc(choice_in_ps, 1)
                if n == 5:
                    pe.wait_ge(choice_gates_done, 1)
                    pe.matmul(ps[:, 5, 64:64 + NB * TOPK], ones[0:NB, :], gates_diag[:], start=True, stop=True)
                    pe.transpose(ps[0:NE, 5, 128:128 + NB], choice[:, 32:40], ident[0:NB, 0:NB]).then_inc(choice_gates_in_ps, 1)
                if n == 6:
                    pe.wait_ge(choice_gatesT_done, 1)
                    pe.matmul(ps[0:NB, 5, 256:256 + D], choice[:, 56:64], b2e[:], start=True, stop=False)
                    pe.matmul(ps[0:NB, 5, 256:256 + D], choice[0:1, 48:56], b2m[:], start=False, stop=True).then_inc(expert_bias_in_ps, 1)
            xc = xnT[:].rearrange("p b (n c) -> p n b c", c=C)
            pe.wait_ge(chunk_out_done, NCH)
            pe.wait_ge(expert_bias_done, 1)
            for j in range(4):
                ins = pe.matmul(PB[:, j, :], w1x[:], xc[:, 2 * j:2 * j + 2], start=True, stop=True)
            ins.then_inc(gate_x_in_ps, 1)
            pe.wait_ge(squares_done, 4 + NCH)
            for g in range(NG):
                ins = pe.transpose(PA[:, g // 4, P * (g % 4):P * (g % 4) + P],
                                   stats[:, H * g:H * g + H, :].rearrange("p h k -> p (h k)"), ident[:])
            ins.then_inc(stats_in_ps, 1)
            pe.wait_ge(statsT_done, 1)
            pe.wait_ge(gate_x_done, 1)
            pe.wait_ge(w1s_in, 16)
            pe.wait_ge(chunk_out_done, NCH)

            def gate_logits(u):
                h, half = u // 2, u % 2
                pe.wait_ge(gate_hidden_done, u + 1)
                for i in range(NG // 2):
                    ins = pe.matmul(ps_logits[:, NG // 2 * half + i, h, :], h1[:, u % 2, P * i:P * i + P], w2[:],
                                    start=True, stop=True)
                ins.then_inc(gate_logits_in_ps, 1)

            for u in range(2 * H):
                h, half = u // 2, u % 2
                if u >= 2:
                    gate_logits(u - 2)
                for k in range(2):
                    j = 2 * half + k
                    ins = pe.matmul(PA[:, 2 * (u % 2) + k, :], w1s[:, h, :], statsT[:, 512 * j:512 * j + 512],
                                    start=True, stop=True)
                ins.then_inc(gate_stats_in_ps, 1)
            gate_logits(2 * H - 2)
            gate_logits(2 * H - 1)
            pe.wait_ge(gate_logits_done, 1)
            def up(b, half):
                e, m = divmod(half, 2)
                u = 6 * b + half
                if e and m == 0:
                    pe.wait_ge(expert_scaled, 2 * b + e)
                if u >= 2:
                    pe.wait_ge(up_done, u - 1)
                for k in (2 * m, 2 * m + 1):
                    ins = pe.matmul(ffn_h[:, u % 2, L * (k % 2):L * (k % 2) + L], expert(b, e)[:, P * k:P * k + P],
                                    xnT[:, b, :], start=True, stop=True)
                ins.then_inc(up_in_ps, 1)

            def down(b, third):
                t, e = divmod(third, 3)
                yt = ffn_y[:, b % 2, D * t:D * t + D]
                if third == 0:
                    if b >= 2:
                        pe.wait_ge(y_done, b - 1)
                    pe.wait_ge(up_done, 6 * b + 6)
                if e == 0:
                    pe.matmul(yt, ident[0:NB, b:b + 1].broadcast_to([NB, P]), biasb[:], start=True, stop=False)
                    if b >= EARLY - 1:
                        pe.matmul(yt, mixT[:, b, P * t:P * t + P], wo[:], start=False, stop=False)
                for k in range(NBLK):
                    ins = pe.matmul(yt, hidden_of(b)[:, e, k, P * t:P * t + P],
                                    expert(b, e)[:, HID + NBLK + P * k:HID + NBLK + P * k + P],
                                    start=False, stop=(e == 2 and k == NBLK - 1))
                if third == 5:
                    ins.then_inc(y_in_ps, 1)

            def experts(b, piece):
                if piece < 6:
                    if b < NB:
                        up(b, piece)
                    if b:
                        down(b - 1, piece)

            for b in range(EARLY):
                period(experts, b)
            pe.wait_ge(mix_normed, 1)
            for g in range(NG):
                ins = pe.transpose(side_tile(g), mix_sl[:, g, :], ident[:])
            ins.then_inc(mixT_in_ps, 1)
            pe.wait_ge(mixT_done, 1)
            for b in range(EARLY - 1):
                if b >= 2:
                    pe.wait_ge(attn_done, b - 1)
                for t in range(2):
                    ins = pe.matmul(ps[:, 6 + b % 2, D * t:D * t + D], mixT[:, b, P * t:P * t + P], wo[:], start=True, stop=True)
                ins.then_inc(attn_in_ps, 1)
            pe.wait_ge(attn_done, EARLY - 1)

            second_layer_tensor(pe, experts)


def lay_out(i):
    import numpy as np
    f = lambda n: np.asarray(i["L0_attn_" + n])
    g = lambda n: np.asarray(i["L0_ffn_" + n])
    l = lambda n: np.asarray(i["L1_" + n])
    con = np.ascontiguousarray

    def packed(w1, b, w2):
        return np.concatenate([w1, b.reshape(NBLK, P).T, w2.reshape(NBLK, P, D).transpose(1, 0, 2).reshape(P, HID)], 1)

    w1s = np.zeros((P, H, D), np.float32)
    for h in range(H):
        w1s[DH * h:DH * h + 16, h] = f("W1")[D:]
    return {
        "x": con(f("x").reshape(NT, P, D).transpose(1, 0, 2)),
        "wqkv": con(np.stack([f("Wk"), f("Wv"), f("Wq")], 1)),
        "wb": f("Wb"),
        "cw": con(np.stack([f("conv_k"), f("conv_v"), f("conv_q")], 1)),
        "fsw": con(f("fir_short").reshape(P, FS_TAPS)),
        "frev": con(np.pad(f("fir_long").reshape(P, FL_TAPS), ((0, 0), (FL_TAPS, FL_TAPS)))),
        "w1x": con(f("W1")[0:D]),
        "w1s": w1s,
        "b1": con(f("b1")[:, None]),
        "w2": f("W2"),
        "bcst": con(np.tile(np.concatenate([f("base_bias").ravel(), f("b2"), f("log_temp"), f("conv_residual_logit"),
                                            np.zeros(12, np.float32)])[None], (P, 1))),
        "rmsw": con(np.tile(f("rms_w"), H)[:, None]),
        "wo": f("Wo"),
        "wm": con(packed(g("W1m"), g("b1m"), g("W2m"))),
        "experts": con(np.stack([packed(*w) for w in zip(g("W1e"), g("b1e"), g("W2e"))])),
        "wg": g("w_gate"),
        "bgate": con(np.tile(g("b_gate")[None], (NB, 1))),
        "b2e": g("b2e"),
        "b2m": con(g("b2m")[None]),
        "alpha": con(np.tile(g("alpha").reshape(1, 1), (P, 1))),
        "l1_wvT": con(l("attn_Wv").T),
        "l1_woT": con(l("attn_Wo").T),
        "l1_wtT": con(l("ffn_weight").T),
        "l1_bv": con(np.tile(l("attn_bv")[None], (P, 1))),
        "l1_bo": con(np.tile(l("attn_bo")[None], (P, 1))),
    }


def kernel(**inputs):
    import concourse.bacc as _bacc
    from concourse.bass_utils import run_bass_kernel_spmd as _run
    arrays = lay_out(inputs)
    nc = _bacc.Bacc("TRN2", target_bir_lowering=False, num_devices=1)
    inp = {name: nc.dram_tensor("in_" + name, a.shape, mybir.dt.from_np(a.dtype), kind="ExternalInput").ap()
           for name, a in arrays.items()}
    out = nc.dram_tensor("out_0_dram", (NB, L, D), F32, kind="ExternalOutput").ap()
    attention_mix_kernel(nc, inp, out)
    r = _run(nc, [{"in_" + name: a for name, a in arrays.items()}], core_ids=[0])
    return r.results[0]["out_0_dram"]
```
